# Optimizing a Trainium2 kernel written in Bass

```python
import numpy as np
import jax
import jax.numpy as jnp

def _softmax(x, axis=-1):
    return jax.nn.softmax(x, axis=axis)

def _gelu(x):
    return jax.nn.gelu(x, approximate=True)

def _silu(x):
    return jax.nn.silu(x)

def _sigmoid(x):
    return jax.nn.sigmoid(x)

def _layernorm(x, axis=-1, eps=1e-05):
    m = jnp.mean(x, axis=axis, keepdims=True)
    v = jnp.var(x, axis=axis, keepdims=True)
    return (x - m) / jnp.sqrt(v + eps)

def _scatter_add(tgt, idx, src, axis=0):
    return tgt.at[idx].add(src)

def _segment_sum(src, seg, n):
    return jax.ops.segment_sum(src, seg, n)
kernel_name = 'mk_gnn_resnorm_d4_gnn_r64_2c5da3'

def setup_inputs(seed: int=0):
    np.random.seed(seed)
    _w = jnp.asarray

    def _rec_inputs():
        import jax
        import jax.numpy as jnp
        _gk = jax.random.key(seed)
        x = -0.0005121 + 1.001 * jax.random.normal(jax.random.fold_in(_gk, 1), (50000, 160), jnp.float32)
        src = jax.random.randint(jax.random.fold_in(_gk, 2), (25000,), 0, 50000, jnp.int32)
        dst = jax.random.randint(jax.random.fold_in(_gk, 3), (25000,), 0, 50000, jnp.int32)
        _o = jnp.argsort(dst, stable=True)
        src = src[_o]
        dst = dst[_o]
        edge_attr_16 = -0.000191324 + 0.999809 * jax.random.normal(jax.random.fold_in(_gk, 12), (25000, 16), jnp.float32)
        edge_attr_4 = 0.000126197 + 0.999763 * jax.random.normal(jax.random.fold_in(_gk, 13), (25000, 4), jnp.float32)
        edge_attr_8 = jax.random.uniform(jax.random.fold_in(_gk, 14), (25000, 8), jnp.float32, 0.0, 1)
        node_vec1 = jax.random.uniform(jax.random.fold_in(_gk, 16), (50000, 1), jnp.float32, 0.0, 1)
        return (x, src, dst, edge_attr_16, edge_attr_4, edge_attr_8, node_vec1)
    x, src, dst, edge_attr_16, edge_attr_4, edge_attr_8, node_vec1 = _rec_inputs()

    def _L0_gnn_setup():
        import jax, jax.numpy as jnp
        import numpy as np
        N = 20000
        E = 5000
        MUL0 = 64
        MUL1 = 32
        FC_IN = 16
        FC_H = 64
        WNUM = 192
        key = jax.random.key(seed)
        ks = jax.random.split(key, 16)
        return {'x': jax.random.normal(ks[0], (N, MUL0 + 3 * MUL1), jnp.float32), 'node_attr': jnp.ones((N, 1), jnp.float32), 'edge_scalars': jax.random.normal(ks[1], (E, FC_IN), jnp.float32), 'edge_attr_sh': jax.random.normal(ks[2], (E, 4), jnp.float32), 'edge_src': jax.random.randint(ks[3], (E,), 0, N), 'edge_dst': jax.random.randint(ks[4], (E,), 0, N), 'Wfc1': jax.random.normal(ks[5], (FC_IN, FC_H), jnp.float32), 'Wfc2': jax.random.normal(ks[6], (FC_H, WNUM), jnp.float32), 'Wsc0': jax.random.normal(ks[7], (MUL0, MUL0), jnp.float32), 'Wsc1': jax.random.normal(ks[8], (MUL1, MUL1), jnp.float32), 'Wl1_0': jax.random.normal(ks[9], (MUL0, MUL0), jnp.float32), 'Wl1_1': jax.random.normal(ks[10], (MUL1, MUL1), jnp.float32), 'Wl2_s': jax.random.normal(ks[11], (MUL0 + MUL1, MUL0), jnp.float32), 'Wl2_v': jax.random.normal(ks[12], (MUL0 + MUL1, MUL1), jnp.float32), 'Wa': 0.1 * jax.random.normal(ks[13], (MUL0 + MUL1, 1), jnp.float32)}
    _L0_gnn_all = _L0_gnn_setup()
    _L0_gnn_in = {k: v for k, v in _L0_gnn_all.items() if k in ('Wfc1', 'Wfc2', 'Wsc0', 'Wsc1', 'Wl1_0', 'Wl1_1', 'Wl2_s', 'Wl2_v', 'Wa')}
    del _L0_gnn_all

    def _L1_gnn_setup():
        import jax, jax.numpy as jnp
        import numpy as np
        N, E = (20000, 5000)
        CS, CV = (64, 32)
        AS_, AV, H = (16, 8, 4)
        NB = 16
        SQRT3 = 1.7320508075688772
        SQRT2 = 1.4142135623730951
        EPS = 1e-05

        def _cg_tp(s, v, y0, y1, w_ss, w_sv, w_vs, w_vv0, w_vv1):
            out_s = jnp.concatenate([w_ss * s * y0[:, None], w_vv0 * (jnp.einsum('eci,ei->ec', v, y1) / SQRT3)], axis=-1)
            out_v = jnp.concatenate([(w_sv * s)[:, :, None] * y1[:, None, :], (w_vs * jnp.ones_like(v[..., 0]))[..., None] * v * y0[:, None, None], (w_vv1 * jnp.ones_like(v[..., 0]))[..., None] * (jnp.cross(v, y1[:, None, :]) / SQRT2)], axis=1)
            return (out_s, out_v)

        def _equiv_layernorm(s, v, gamma_s, beta_s, gamma_v):
            mu = jnp.mean(s, axis=-1, keepdims=True)
            var = jnp.var(s, axis=-1, keepdims=True)
            s_n = (s - mu) * jax.lax.rsqrt(var + EPS) * gamma_s + beta_s
            rms = jnp.sqrt(jnp.mean(jnp.sum(v * v, axis=-1), axis=-1, keepdims=True) + EPS)
            v_n = v / rms[..., None] * gamma_v[None, :, None]
            return (s_n, v_n)
        key = jax.random.key(seed)
        ks = jax.random.split(key, 26)

        def rn(k, shape, fan):
            return jax.random.normal(k, shape, jnp.float32) / np.sqrt(fan)
        D1S, D1V = (CS + CV, CS + 2 * CV)
        WN = 2 * CS + 3 * CV
        inp = {'node': jax.random.normal(ks[0], (N, CS + 3 * CV), jnp.float32), 'edge_index': jax.random.randint(ks[1], (2, E), 0, N, jnp.int64 if jax.config.jax_enable_x64 else jnp.int32), 'rbf': jax.random.uniform(ks[2], (E, NB), jnp.float32), 'rsh': jax.random.normal(ks[3], (E, 4), jnp.float32), 'gamma_s': jnp.ones((CS,), jnp.float32), 'beta_s': jnp.zeros((CS,), jnp.float32), 'gamma_v': jnp.ones((CV,), jnp.float32), 'Ws_src': rn(ks[4], (CS, CS), CS), 'Wv_src': rn(ks[5], (CV, CV), CV), 'Ws_dst': rn(ks[6], (CS, CS), CS), 'Wv_dst': rn(ks[7], (CV, CV), CV), 'W_rbf': rn(ks[8], (NB, WN), NB), 'W_alpha': rn(ks[9], (D1S, H * AS_), D1S), 'alpha_dot': rn(ks[10], (1, H, AS_), AS_), 'Ws_val': rn(ks[11], (D1S, CS), D1S), 'Wv_val': rn(ks[12], (D1V, CV), D1V), 'Wg': rn(ks[13], (CS, CV), CS), 'w2_ss': rn(ks[14], (CS,), 1), 'w2_sv': rn(ks[15], (CS,), 1), 'w2_vs': rn(ks[16], (CV,), 1), 'w2_vv0': rn(ks[17], (CV,), 1), 'w2_vv1': rn(ks[18], (CV,), 1), 'Ws_vlin': rn(ks[19], (D1S, H * AS_), D1S), 'Wv_vlin': rn(ks[20], (D1V, H * AV), D1V), 'Wps': rn(ks[21], (H * AS_, CS), H * AS_), 'Wpv': rn(ks[22], (H * AV, CV), H * AV)}
        return inp
    _L1_gnn_all = _L1_gnn_setup()
    _L1_gnn_in = {k: v for k, v in _L1_gnn_all.items() if k in ('gamma_s', 'beta_s', 'gamma_v', 'Ws_src', 'Wv_src', 'Ws_dst', 'Wv_dst', 'W_rbf', 'W_alpha', 'alpha_dot', 'Ws_val', 'Wv_val', 'Wg', 'w2_ss', 'w2_sv', 'w2_vs', 'w2_vv0', 'w2_vv1', 'Ws_vlin', 'Wv_vlin', 'Wps', 'Wpv')}
    del _L1_gnn_all

    def _L2_gnn_setup():
        import jax, jax.numpy as jnp
        import numpy as np
        N = 50000
        E = 12500
        MUL0 = 64
        MUL1 = 32
        NB = 8
        HID = 64
        WNUM = MUL0 + MUL0 + MUL1 + MUL1
        D_IN = MUL0 + 3 * MUL1
        AVG_DEG = E / N
        key = jax.random.key(seed)
        ks = jax.random.split(key, 16)
        p = lambda i, s: jax.random.normal(ks[i], s, jnp.float32)
        return {'node_features': p(0, (N, D_IN)), 'edge_sh': p(1, (E, 4)), 'edge_embed': jax.random.uniform(ks[2], (E, NB), jnp.float32), 'W1_s': p(3, (MUL0, MUL0)), 'W1_v': p(4, (MUL1, MUL1)), 'fc_w1': p(5, (NB, HID)), 'fc_b1': jnp.zeros((HID,), jnp.float32), 'fc_w2': p(6, (HID, WNUM)) * 0.1, 'fc_b2': jnp.zeros((WNUM,), jnp.float32), 'W2_s': p(7, (96, 96)), 'W2_v': p(8, (96, MUL1)), 'Wsc_s': p(9, (MUL0, 96)), 'Wsc_v': p(10, (MUL1, MUL1)), 'edge_index': jax.random.randint(ks[11], (2, E), 0, N)}
    _L2_gnn_all = _L2_gnn_setup()
    _L2_gnn_in = {k: v for k, v in _L2_gnn_all.items() if k in ('W1_s', 'W1_v', 'fc_w1', 'fc_b1', 'fc_w2', 'fc_b2', 'W2_s', 'W2_v', 'Wsc_s', 'Wsc_v')}
    del _L2_gnn_all

    def _L3_gnn_setup():
        import jax, jax.numpy as jnp
        import numpy as np
        INV3 = 1.0 / np.sqrt(3.0)

        def _fctp(x_s, x_v, attr, w0, w1):
            s = x_s @ w0 * (1.0 / np.sqrt(x_s.shape[-1])) * attr
            v = jnp.einsum('nud,uw->nwd', x_v, w1) * (1.0 / np.sqrt(x_v.shape[-2])) * attr[..., None]
            return (s, v)
        key = jax.random.key(seed)
        ks = jax.random.split(key, 16)
        N, E = (50000, 12500)
        inp = {'node_input': jax.random.normal(ks[0], (N, 160), jnp.float32), 'node_attr': jnp.ones((N, 1), jnp.float32), 'edge_attr': jax.random.normal(ks[1], (E, 4), jnp.float32), 'edge_scalars': jax.random.normal(ks[2], (E, 8), jnp.float32), 'sc_w0': jax.random.normal(ks[3], (64, 64), jnp.float32), 'sc_w1': jax.random.normal(ks[4], (32, 32), jnp.float32), 'lin1_w0': jax.random.normal(ks[5], (64, 64), jnp.float32), 'lin1_w1': jax.random.normal(ks[6], (32, 32), jnp.float32), 'fc_w1': jax.random.normal(ks[7], (8, 64), jnp.float32), 'fc_w2': jax.random.normal(ks[8], (64, 192), jnp.float32), 'lin2_w0': jax.random.normal(ks[9], (96, 64), jnp.float32), 'lin2_w1': jax.random.normal(ks[10], (96, 32), jnp.float32), 'lin3_w': jax.random.normal(ks[11], (96, 1), jnp.float32), 'edge_src': jax.random.randint(ks[12], (E,), 0, N), 'edge_dst': jax.random.randint(ks[13], (E,), 0, N), 'num_neighbors': 16}
        return inp
    _L3_gnn_all = _L3_gnn_setup()
    _L3_gnn_in = {k: v for k, v in _L3_gnn_all.items() if k in ('sc_w0', 'sc_w1', 'lin1_w0', 'lin1_w1', 'fc_w1', 'fc_w2', 'lin2_w0', 'lin2_w1', 'lin3_w')}
    del _L3_gnn_all
    return {'x': x, 'src': src, 'dst': dst, 'edge_attr_16': edge_attr_16, 'edge_attr_4': edge_attr_4, 'edge_attr_8': edge_attr_8, 'node_vec1': node_vec1, 'L0_gnn_Wfc1': _L0_gnn_in['Wfc1'], 'L0_gnn_Wfc2': _L0_gnn_in['Wfc2'], 'L0_gnn_Wsc0': _L0_gnn_in['Wsc0'], 'L0_gnn_Wsc1': _L0_gnn_in['Wsc1'], 'L0_gnn_Wl1_0': _L0_gnn_in['Wl1_0'], 'L0_gnn_Wl1_1': _L0_gnn_in['Wl1_1'], 'L0_gnn_Wl2_s': _L0_gnn_in['Wl2_s'], 'L0_gnn_Wl2_v': _L0_gnn_in['Wl2_v'], 'L0_gnn_Wa': _L0_gnn_in['Wa'], 'L1_gnn_gamma_s': _L1_gnn_in['gamma_s'], 'L1_gnn_beta_s': _L1_gnn_in['beta_s'], 'L1_gnn_gamma_v': _L1_gnn_in['gamma_v'], 'L1_gnn_Ws_src': _L1_gnn_in['Ws_src'], 'L1_gnn_Wv_src': _L1_gnn_in['Wv_src'], 'L1_gnn_Ws_dst': _L1_gnn_in['Ws_dst'], 'L1_gnn_Wv_dst': _L1_gnn_in['Wv_dst'], 'L1_gnn_W_rbf': _L1_gnn_in['W_rbf'], 'L1_gnn_W_alpha': _L1_gnn_in['W_alpha'], 'L1_gnn_alpha_dot': _L1_gnn_in['alpha_dot'], 'L1_gnn_Ws_val': _L1_gnn_in['Ws_val'], 'L1_gnn_Wv_val': _L1_gnn_in['Wv_val'], 'L1_gnn_Wg': _L1_gnn_in['Wg'], 'L1_gnn_w2_ss': _L1_gnn_in['w2_ss'], 'L1_gnn_w2_sv': _L1_gnn_in['w2_sv'], 'L1_gnn_w2_vs': _L1_gnn_in['w2_vs'], 'L1_gnn_w2_vv0': _L1_gnn_in['w2_vv0'], 'L1_gnn_w2_vv1': _L1_gnn_in['w2_vv1'], 'L1_gnn_Ws_vlin': _L1_gnn_in['Ws_vlin'], 'L1_gnn_Wv_vlin': _L1_gnn_in['Wv_vlin'], 'L1_gnn_Wps': _L1_gnn_in['Wps'], 'L1_gnn_Wpv': _L1_gnn_in['Wpv'], 'L2_gnn_W1_s': _L2_gnn_in['W1_s'], 'L2_gnn_W1_v': _L2_gnn_in['W1_v'], 'L2_gnn_fc_w1': _L2_gnn_in['fc_w1'], 'L2_gnn_fc_b1': _L2_gnn_in['fc_b1'], 'L2_gnn_fc_w2': _L2_gnn_in['fc_w2'], 'L2_gnn_fc_b2': _L2_gnn_in['fc_b2'], 'L2_gnn_W2_s': _L2_gnn_in['W2_s'], 'L2_gnn_W2_v': _L2_gnn_in['W2_v'], 'L2_gnn_Wsc_s': _L2_gnn_in['Wsc_s'], 'L2_gnn_Wsc_v': _L2_gnn_in['Wsc_v'], 'L3_gnn_sc_w0': _L3_gnn_in['sc_w0'], 'L3_gnn_sc_w1': _L3_gnn_in['sc_w1'], 'L3_gnn_lin1_w0': _L3_gnn_in['lin1_w0'], 'L3_gnn_lin1_w1': _L3_gnn_in['lin1_w1'], 'L3_gnn_fc_w1': _L3_gnn_in['fc_w1'], 'L3_gnn_fc_w2': _L3_gnn_in['fc_w2'], 'L3_gnn_lin2_w0': _L3_gnn_in['lin2_w0'], 'L3_gnn_lin2_w1': _L3_gnn_in['lin2_w1'], 'L3_gnn_lin3_w': _L3_gnn_in['lin3_w']}

def reference(x, src, dst, edge_attr_16, edge_attr_4, edge_attr_8, node_vec1, L0_gnn_Wfc1, L0_gnn_Wfc2, L0_gnn_Wsc0, L0_gnn_Wsc1, L0_gnn_Wl1_0, L0_gnn_Wl1_1, L0_gnn_Wl2_s, L0_gnn_Wl2_v, L0_gnn_Wa, L1_gnn_gamma_s, L1_gnn_beta_s, L1_gnn_gamma_v, L1_gnn_Ws_src, L1_gnn_Wv_src, L1_gnn_Ws_dst, L1_gnn_Wv_dst, L1_gnn_W_rbf, L1_gnn_W_alpha, L1_gnn_alpha_dot, L1_gnn_Ws_val, L1_gnn_Wv_val, L1_gnn_Wg, L1_gnn_w2_ss, L1_gnn_w2_sv, L1_gnn_w2_vs, L1_gnn_w2_vv0, L1_gnn_w2_vv1, L1_gnn_Ws_vlin, L1_gnn_Wv_vlin, L1_gnn_Wps, L1_gnn_Wpv, L2_gnn_W1_s, L2_gnn_W1_v, L2_gnn_fc_w1, L2_gnn_fc_b1, L2_gnn_fc_w2, L2_gnn_fc_b2, L2_gnn_W2_s, L2_gnn_W2_v, L2_gnn_Wsc_s, L2_gnn_Wsc_v, L3_gnn_sc_w0, L3_gnn_sc_w1, L3_gnn_lin1_w0, L3_gnn_lin1_w1, L3_gnn_fc_w1, L3_gnn_fc_w2, L3_gnn_lin2_w0, L3_gnn_lin2_w1, L3_gnn_lin3_w):
    import jax
    import jax.numpy as jnp

    def _L0_gnn_ref(x, node_attr, edge_scalars, edge_attr_sh, edge_src, edge_dst, Wfc1, Wfc2, Wsc0, Wsc1, Wl1_0, Wl1_1, Wl2_s, Wl2_v, Wa):
        import jax, jax.numpy as jnp
        import numpy as np
        N = 20000
        E = 5000
        MUL0 = 64
        MUL1 = 32
        FC_IN = 16
        FC_H = 64
        WNUM = 192
        n = x.shape[0]
        x0 = x[:, :MUL0]
        x1 = x[:, MUL0:].reshape(n, MUL1, 3)
        a = node_attr
        h = jax.nn.silu(edge_scalars @ (Wfc1 / jnp.sqrt(jnp.float32(FC_IN))))
        w = h @ (Wfc2 / jnp.sqrt(jnp.float32(FC_H)))
        w0 = w[:, :64]
        w1 = w[:, 64:128]
        w2 = w[:, 128:160]
        w3 = w[:, 160:192]
        inv8 = 1.0 / jnp.sqrt(jnp.float32(MUL0))
        inv32 = 1.0 / jnp.sqrt(jnp.float32(MUL1))
        sc = jnp.concatenate([x0 @ Wsc0 * a * inv8, (jnp.einsum('num,uv->nvm', x1, Wsc1) * a[..., None] * inv32).reshape(n, 3 * MUL1)], axis=1)
        f0 = x0 @ Wl1_0 * a * inv8
        f1 = jnp.einsum('num,uv->nvm', x1, Wl1_1) * a[..., None] * inv32
        e0 = f0[edge_src]
        e1 = f1[edge_src]
        sh0 = edge_attr_sh[:, :1]
        sh1 = edge_attr_sh[:, 1:4]
        mid0 = w0 * e0 * sh0
        mid1 = w3 * jnp.einsum('eum,em->eu', e1, sh1) / jnp.sqrt(3.0)
        mid2 = w1[:, :, None] * e0[:, :, None] * sh1[:, None, :]
        mid3 = w2[:, :, None] * e1 * sh0[:, :, None]
        cnt = jnp.clip(jax.ops.segment_sum(jnp.ones(edge_dst.shape, x.dtype), edge_dst, num_segments=n), 1.0)

        def smean(v):
            s = jax.ops.segment_sum(v, edge_dst, num_segments=n)
            return s / cnt.reshape((n,) + (1,) * (v.ndim - 1))
        n0, n1 = (smean(mid0), smean(mid1))
        n2, n3 = (smean(mid2), smean(mid3))
        scal = jnp.concatenate([n0, n1], axis=1)
        vec = jnp.concatenate([n2, n3], axis=1)
        inv96 = 1.0 / jnp.sqrt(jnp.float32(MUL0 + MUL1))
        alpha = scal @ Wa * a * inv96
        out_s = scal @ Wl2_s * a * inv96
        out_v = jnp.einsum('num,uv->nvm', vec, Wl2_v) * a[..., None] * inv96
        conv = jnp.concatenate([out_s, out_v.reshape(n, 3 * MUL1)], axis=1)
        return sc + alpha * conv

    def _L1_gnn_ref(node, rbf, rsh, gamma_s, beta_s, gamma_v, Ws_src, Wv_src, Ws_dst, Wv_dst, W_rbf, W_alpha, alpha_dot, Ws_val, Wv_val, Wg, w2_ss, w2_sv, w2_vs, w2_vv0, w2_vv1, Ws_vlin, Wv_vlin, Wps, Wpv, edge_index):
        import jax, jax.numpy as jnp
        import numpy as np
        N, E = (20000, 5000)
        CS, CV = (64, 32)
        AS_, AV, H = (16, 8, 4)
        NB = 16
        SQRT3 = 1.7320508075688772
        SQRT2 = 1.4142135623730951
        EPS = 1e-05

        def _cg_tp(s, v, y0, y1, w_ss, w_sv, w_vs, w_vv0, w_vv1):
            out_s = jnp.concatenate([w_ss * s * y0[:, None], w_vv0 * (jnp.einsum('eci,ei->ec', v, y1) / SQRT3)], axis=-1)
            out_v = jnp.concatenate([(w_sv * s)[:, :, None] * y1[:, None, :], (w_vs * jnp.ones_like(v[..., 0]))[..., None] * v * y0[:, None, None], (w_vv1 * jnp.ones_like(v[..., 0]))[..., None] * (jnp.cross(v, y1[:, None, :]) / SQRT2)], axis=1)
            return (out_s, out_v)

        def _equiv_layernorm(s, v, gamma_s, beta_s, gamma_v):
            mu = jnp.mean(s, axis=-1, keepdims=True)
            var = jnp.var(s, axis=-1, keepdims=True)
            s_n = (s - mu) * jax.lax.rsqrt(var + EPS) * gamma_s + beta_s
            rms = jnp.sqrt(jnp.mean(jnp.sum(v * v, axis=-1), axis=-1, keepdims=True) + EPS)
            v_n = v / rms[..., None] * gamma_v[None, :, None]
            return (s_n, v_n)
        n = node.shape[0]
        e = rsh.shape[0]
        s = node[:, :CS]
        v = node[:, CS:].reshape(n, CV, 3)
        s_n, v_n = _equiv_layernorm(s, v, gamma_s, beta_s, gamma_v)
        src, dst = (edge_index[0], edge_index[1])
        msg_s = (s_n @ Ws_src)[src] + (s_n @ Ws_dst)[dst]
        msg_v = jnp.einsum('ncx,cd->ndx', v_n, Wv_src)[src] + jnp.einsum('ncx,cd->ndx', v_n, Wv_dst)[dst]
        y0, y1 = (rsh[:, 0], rsh[:, 1:4])
        w1 = rbf @ W_rbf
        m1_s, m1_v = _cg_tp(msg_s, msg_v, y0, y1, w1[:, :CS], w1[:, CS:2 * CS], w1[:, 2 * CS:2 * CS + CV], w1[:, 2 * CS + CV:2 * CS + 2 * CV], w1[:, 2 * CS + 2 * CV:])
        a = (m1_s @ W_alpha).reshape(e, H, AS_)
        a = jnp.where(a > 0, a, 0.2 * a)
        a = jnp.sum(a * alpha_dot, axis=-1, keepdims=True)
        amax = jax.ops.segment_max(a, dst, num_segments=n)
        amax = jnp.where(jnp.isfinite(amax), amax, 0.0)
        ex = jnp.exp(a - amax[dst])
        den = jax.ops.segment_sum(ex, dst, num_segments=n)
        alpha = ex / (den[dst] + 1e-16)
        val_s = m1_s @ Ws_val
        val_v = jnp.einsum('ecx,cd->edx', m1_v, Wv_val)
        val_v = val_v * jax.nn.sigmoid(val_s @ Wg)[..., None]
        val_s = jax.nn.sigmoid(val_s)
        m2_s, m2_v = _cg_tp(val_s, val_v, y0, y1, w2_ss, w2_sv, w2_vs, w2_vv0, w2_vv1)
        hs = (m2_s @ Ws_vlin).reshape(e, H, AS_)
        hv = jnp.einsum('ecx,cd->edx', m2_v, Wv_vlin).reshape(e, H, AV, 3)
        h = jnp.concatenate([hs, hv.reshape(e, H, AV * 3)], axis=-1)
        agg = jax.ops.segment_sum(alpha * h, dst, num_segments=n)
        agg_s = agg[:, :, :AS_].reshape(n, H * AS_)
        agg_v = agg[:, :, AS_:].reshape(n, H * AV, 3)
        out = node + jnp.concatenate([agg_s @ Wps, jnp.einsum('ncx,cd->ndx', agg_v, Wpv).reshape(n, CV * 3)], axis=-1)
        return out

    def _L2_gnn_ref(node_features, edge_sh, edge_embed, W1_s, W1_v, fc_w1, fc_b1, fc_w2, fc_b2, W2_s, W2_v, Wsc_s, Wsc_v, edge_index):
        import jax, jax.numpy as jnp
        import numpy as np
        N = 50000
        E = 12500
        MUL0 = 64
        MUL1 = 32
        NB = 8
        HID = 64
        WNUM = MUL0 + MUL0 + MUL1 + MUL1
        D_IN = MUL0 + 3 * MUL1
        AVG_DEG = E / N
        n = node_features.shape[0]
        s = node_features[:, :MUL0]
        v = node_features[:, MUL0:].reshape(n, MUL1, 3)
        xs = s @ W1_s / np.sqrt(MUL0)
        xv = jnp.einsum('nmc,mk->nkc', v, W1_v) / np.sqrt(MUL1)
        src, dst = (edge_index[0], edge_index[1])
        sh0 = edge_sh[:, 0]
        sh1 = edge_sh[:, 1:4]
        w = jax.nn.silu(edge_embed @ fc_w1 + fc_b1) @ fc_w2 + fc_b2
        w_ss = w[:, :MUL0]
        w_sv = w[:, MUL0:2 * MUL0]
        w_vs = w[:, 2 * MUL0:2 * MUL0 + MUL1]
        w_vv = w[:, 2 * MUL0 + MUL1:]
        xs_e = xs[src]
        xv_e = xv[src]
        m0_a = w_ss * xs_e * sh0[:, None]
        m1_a = (w_sv * xs_e)[:, :, None] * sh1[:, None, :]
        m1_b = w_vs[:, :, None] * xv_e * sh0[:, None, None]
        m0_b = w_vv * jnp.einsum('emc,ec->em', xv_e, sh1) / np.sqrt(3.0)
        msg = jnp.concatenate([m0_a, m0_b, m1_a.reshape(-1, MUL0 * 3), m1_b.reshape(-1, MUL1 * 3)], axis=1)
        agg = jax.ops.segment_sum(msg, dst, num_segments=n) / np.sqrt(AVG_DEG)
        agg_s = agg[:, :96]
        agg_v = agg[:, 96:].reshape(n, 96, 3)
        out_s = agg_s @ W2_s / np.sqrt(96.0)
        out_v = jnp.einsum('nmc,mk->nkc', agg_v, W2_v) / np.sqrt(96.0)
        out_s = out_s + s @ Wsc_s / np.sqrt(MUL0)
        out_v = out_v + jnp.einsum('nmc,mk->nkc', v, Wsc_v) / np.sqrt(MUL1)
        scalars = jax.nn.silu(out_s[:, :MUL0])
        gates = jax.nn.silu(out_s[:, MUL0:MUL0 + MUL1])
        gated = out_v * gates[:, :, None]
        feats = jnp.concatenate([scalars, gated.reshape(n, MUL1 * 3)], axis=1)
        return node_features + feats

    def _L3_gnn_ref(node_input, node_attr, edge_attr, edge_scalars, sc_w0, sc_w1, lin1_w0, lin1_w1, fc_w1, fc_w2, lin2_w0, lin2_w1, lin3_w, edge_src, edge_dst, num_neighbors):
        import jax, jax.numpy as jnp
        import numpy as np
        INV3 = 1.0 / np.sqrt(3.0)

        def _fctp(x_s, x_v, attr, w0, w1):
            s = x_s @ w0 * (1.0 / np.sqrt(x_s.shape[-1])) * attr
            v = jnp.einsum('nud,uw->nwd', x_v, w1) * (1.0 / np.sqrt(x_v.shape[-2])) * attr[..., None]
            return (s, v)
        N = node_input.shape[0]
        h = jax.nn.silu(edge_scalars @ fc_w1 * (1.0 / np.sqrt(8.0)))
        weight = h @ fc_w2 * (1.0 / np.sqrt(64.0))
        xs, xv = (node_input[:, :64], node_input[:, 64:].reshape(N, 32, 3))
        sc_s, sc_v = _fctp(xs, xv, node_attr, sc_w0, sc_w1)
        f_s, f_v = _fctp(xs, xv, node_attr, lin1_w0, lin1_w1)
        gs = f_s[edge_src]
        gv = f_v[edge_src]
        ys, yv = (edge_attr[:, :1], edge_attr[:, 1:])
        w1_, w2_ = (weight[:, :64], weight[:, 64:128])
        w3_, w4_ = (weight[:, 128:160], weight[:, 160:192])
        m0a = gs * ys * w1_
        m0b = jnp.sum(gv * yv[:, None, :], -1) * INV3 * w4_
        m1a = gs[..., None] * yv[:, None, :] * w2_[..., None]
        m1b = gv * ys[..., None] * w3_[..., None]
        E = m0a.shape[0]
        edge_feat = jnp.concatenate([m0a, m0b, m1a.reshape(E, 192), m1b.reshape(E, 96)], -1)
        mid = jax.ops.segment_sum(edge_feat, edge_dst, num_segments=N)
        mid = mid / np.sqrt(float(num_neighbors))
        mid_s, mid_v = (mid[:, :96], mid[:, 96:].reshape(N, 96, 3))
        c_s, c_v = _fctp(mid_s, mid_v, node_attr, lin2_w0, lin2_w1)
        conv = jnp.concatenate([c_s, c_v.reshape(N, -1)], -1)
        scfeat = jnp.concatenate([sc_s, sc_v.reshape(N, -1)], -1)
        angle = 0.1 * (mid_s @ lin3_w) * (1.0 / np.sqrt(96.0)) * node_attr
        return jnp.cos(angle) * scfeat + jnp.sin(angle) * conv
    edge_index = jnp.stack([src, dst])
    x = _layernorm(x + _L0_gnn_ref(x, node_vec1, edge_attr_16, edge_attr_4, src, dst, L0_gnn_Wfc1, L0_gnn_Wfc2, L0_gnn_Wsc0, L0_gnn_Wsc1, L0_gnn_Wl1_0, L0_gnn_Wl1_1, L0_gnn_Wl2_s, L0_gnn_Wl2_v, L0_gnn_Wa), axis=-1)
    x = _layernorm(x + _L1_gnn_ref(x, edge_attr_16, edge_attr_4, L1_gnn_gamma_s, L1_gnn_beta_s, L1_gnn_gamma_v, L1_gnn_Ws_src, L1_gnn_Wv_src, L1_gnn_Ws_dst, L1_gnn_Wv_dst, L1_gnn_W_rbf, L1_gnn_W_alpha, L1_gnn_alpha_dot, L1_gnn_Ws_val, L1_gnn_Wv_val, L1_gnn_Wg, L1_gnn_w2_ss, L1_gnn_w2_sv, L1_gnn_w2_vs, L1_gnn_w2_vv0, L1_gnn_w2_vv1, L1_gnn_Ws_vlin, L1_gnn_Wv_vlin, L1_gnn_Wps, L1_gnn_Wpv, edge_index), axis=-1)
    x = _layernorm(x + _L2_gnn_ref(x, edge_attr_4, edge_attr_8, L2_gnn_W1_s, L2_gnn_W1_v, L2_gnn_fc_w1, L2_gnn_fc_b1, L2_gnn_fc_w2, L2_gnn_fc_b2, L2_gnn_W2_s, L2_gnn_W2_v, L2_gnn_Wsc_s, L2_gnn_Wsc_v, edge_index), axis=-1)
    x = _layernorm(x + _L3_gnn_ref(x, node_vec1, edge_attr_4, edge_attr_8, L3_gnn_sc_w0, L3_gnn_sc_w1, L3_gnn_lin1_w0, L3_gnn_lin1_w1, L3_gnn_fc_w1, L3_gnn_fc_w2, L3_gnn_lin2_w0, L3_gnn_lin2_w1, L3_gnn_lin3_w, src, dst, 16), axis=-1)
    return x

_drawn_inputs = setup_inputs


def setup_inputs(seed=0):
    import zlib

    import numpy as np

    out = dict(_drawn_inputs(seed))
    spreads = {'L1_gnn_gamma_s': (1.0, 0.58),
     'L1_gnn_beta_s': (0.0, 0.489),
     'L1_gnn_gamma_v': (1.0, 0.6),
     'L2_gnn_fc_b1': (0.0, 0.1),
     'L2_gnn_fc_b2': (0.0, 0.1)}
    factors = {'L0_gnn_Wfc1': 8.0,
     'L0_gnn_Wfc2': 8.0,
     'L0_gnn_Wl1_0': 8.0,
     'L0_gnn_Wl1_1': 8.0,
     'L0_gnn_Wl2_s': 8.0,
     'L0_gnn_Wl2_v': 8.0,
     'L0_gnn_Wa': 8.0,
     'L3_gnn_lin1_w0': 8.0,
     'L3_gnn_lin1_w1': 8.0,
     'L3_gnn_fc_w1': 8.0,
     'L3_gnn_fc_w2': 8.0,
     'L3_gnn_lin2_w0': 8.0,
     'L3_gnn_lin2_w1': 8.0,
     'L3_gnn_lin3_w': 8.0}
    for name, (base, spread) in spreads.items():
        noise = np.random.default_rng([zlib.crc32(name.encode()), seed]).standard_normal(out[name].shape)
        drawn = base * np.exp(spread * noise) if base else spread * noise
        out[name] = jnp.asarray(drawn.astype(out[name].dtype))
    for name, factor in factors.items():
        out[name] = (out[name] * factor).astype(out[name].dtype)
    return out
```

```python
import concourse.bass as bass
from concourse import mybir
from contextlib import ExitStack
import math

N = 50000
E = 25000
D = 160
CS, CV = 64, 32
TILE = 128
T = 4
GE = TILE * T
NG = -(-E // GE)
NG += NG % 2
EP = NG * GE
NC = -(-N // GE)
AW = 192
EPS = 1e-5
BIG = float(1 << 22)

fp32 = mybir.dt.float32
i32 = mybir.dt.int32
u8 = mybir.dt.uint8
ALU = mybir.AluOpType
ACT = mybir.ActivationFunctionType
AX = mybir.AxisListType

R3, R8, R32, R96 = 3 ** -0.5, 1 / 8, 32 ** -0.5, 96 ** -0.5

CONV = {
    0: dict(S=66, K=16, silu=1 / 4, scale=dict(E1=R8, E2=R32, F1=1.0, W1=R8, W2=R8, A1=R96, A2=R96 * R3,
                                            B1=R96, B2=R96, CN=1.0, SS=R8, SV=R32)),
    2: dict(S=96, K=8, silu=1.0, scale=dict(E1=R8, E2=R32, F1=1.0, W1=1.0, W2=1.0, A1=2 * R96,
                                          A2=2 * R96 * R3, B1=2 * R96, B2=2 * R96, SS=R8, SV=R32)),
    3: dict(S=65, K=8, silu=8 ** -0.5, scale=dict(E1=R8, E2=R32, F1=1.0, W1=R8, W2=R8, A1=R96 / 4,
                                                 A2=R96 * R3 / 4, B1=R96 / 4, B2=R96 / 4, SS=R8, SV=R32)),
}
MAGIC = 1.5 * 2 ** 23
SM = dict(b1=0, b2=1, gamma_s=3, gamma_v=4, beta=5, ss=6, sv=7, vs=8, vv0=9, vv1=10)
NSMALL = 11
R2 = 2 ** -0.5
ATT = dict(MS=(1.0, "gamma_s"), M1=(1.0, "gamma_v"), M2=(1.0, "gamma_v"),
           B1=(1.0, None), B2=(1.0, None), C=(1.0, None), D=(1.0, None), F=(1.0, None), G=(1.0, None),
           A1=(1.0, None), A2=(R3, None), G1=(1.0, None), G2=(1.0, None), VT1=(1.0, None), VT2=(1.0, None),
           WG=(1.0, None), V0=(1.0, None), V1=(1.0, None), VC=(1.0, None), VF=(R2, None), VG=(-R2, None),
           AD=(1.0, None), US=(0.5, "ss"), UV=(0.5, "sv"), HD=(0.5 * R3, "vv0"), H0=(0.5, "vs"),
           HF=(0.5 * R2, "vv1"), HG=(-0.5 * R2, "vv1"), PS=(1.0, None), PV=(1.0, None), S64=(1.0, None), S96=(1.0, None))
ATT_BLOCKS = list(ATT)
NW1 = len(ATT_BLOCKS)
ORDER = [("NT0", 2, "nt_copied", 3, 1), ("NT1", 2, "nt_copied", 3, 2), ("NT2", 2, "nt_copied", 3, 3),
         ("XS", 4, "hx_s", 1, 1), ("XV", 4, "hx_v", 1, 1), ("GS", 4, "scan_s", 1, 1), ("GV", 4, "scan_v", 1, 1),
         ("MS", 2, "m_copied", 2, 1), ("MV", 2, "m_copied", 2, 2),
         ("AV", 3, "leaky", 1, 1), ("GT", 3, "gate_t", 1, 1), ("VV", 3, "gated", 1, 1),
         ("B1", 2, "prods", 6, 1), ("B2", 2, "prods", 6, 2), ("C", 2, "prods", 6, 3),
         ("D", 2, "prods", 6, 4), ("F", 2, "prods", 6, 5), ("G", 2, "prods", 6, 6),
         ("RS", 4, "norm", 2, 1), ("RV", 4, "norm", 2, 2),
         ("AT", 3, "a_less_max", 1, 1), ("US", 3, "us_y", 1, 1), ("UV", 3, "uv_y", 1, 1),
         ("HS", 3, "hs", 1, 1), ("HV", 3, "hv", 1, 1),
         ("PS", 4, "p_copied", 2, 1), ("PV", 4, "p_copied", 2, 2), ("R0", 4, "agg", 1, 1), ("R1", 4, "agg", 1, 1)]
NAMES = [o[0] for o in ORDER]
BLOCKS = [(layer, name) for layer in CONV for name in CONV[layer]["scale"]]


def live(s, lag, count):
    return 0 <= s - lag < count if isinstance(s, int) else True


def steps(eng, count, body, lead=6, lag=3):
    for s in range(lead):
        body(s, s % 2)
    with eng.Fori(lead, count - 1, 2) as s:
        body(s, 0)
        body(s + 1, 1)
    for s in range(count, count + lag):
        body(s, s % 2)


def gnn_kernel(nc, t, out, layers=4):
    ctx = ExitStack()
    with ctx:
        def sb(name, shape, dt=fp32, scope=ctx):
            return scope.enter_context(nc.sbuf_tensor(name, shape, dt))

        def sems(prefix, names):
            return {n: ctx.enter_context(nc.semaphore(f"{prefix}_{n}")) for n in names.split()}

        x_table = [t["x"]] + [nc.dram_tensor(f"x_layer{l}", (N, D), fp32).ap() for l in (1, 2, 3)] + [out]
        if layers < 4:
            x_table[layers] = out
        agg_table = nc.dram_tensor("aggregates", (N, AW), fp32).ap()

        weights = sb("weights", [128, len(BLOCKS), 128])
        wl1 = sb("weights_layer1", [128, NW1, 128])
        small = sb("small_columns", [128, NSMALL])
        ident = sb("identity", [128, 128])
        bias = sb("layer1_biases", [128, 3])
        minus_half = sb("minus_half", [128, 4 * T])
        ones_col = sb("ones_column", [128, 1])
        ones_row = sb("ones_row", [1, GE])
        src_i = sb("src_index", [128, EP // TILE], i32)
        dst_i = sb("dst_index", [128, EP // TILE], i32)
        last_i = sb("last_index", [128, EP // TILE], i32)
        y_col = sb("sh_columns", [128, EP // TILE, 4])
        ya_col = sb("sh_times_attr", [128, EP // TILE, 4])
        a_src = sb("attr_of_src", [128, EP // TILE])
        goes_on = sb("segment_goes_on", [128, EP], u8)

        def V(name):
            return wl1[:, ATT_BLOCKS.index(name), :]

        def W(layer, name):
            return weights[:, BLOCKS.index((layer, name)), :]

        gathered = sb("gathered", [128, 2, T, D + 1])
        idx_src = sb("gather_index", [128, 2, T], i32)
        idx_last = sb("scatter_index", [128, 2, T], i32)
        xt1 = sb("scaled_x_T1", [128, GE])
        xt2 = sb("scaled_x_T2", [128, GE])
        vec_y = sb("vector_times_y", [96, GE])
        vec_m = sb("vector_message", [96, GE])
        fact = sb("mean_and_alpha", [128, 2, 3, T])
        sum_s = sb("running_scalars", [96, 2, GE])
        sum_v = sb("running_vectors", [96, 2, GE])
        agg_out = sb("agg_out", [128, 2, T, AW])
        with ExitStack() as part:
            gathered_d = sb("gathered_dst", [128, 2, T, D], scope=part)
            idx_dst = sb("gather_index_dst", [128, 2, T], i32, scope=part)
            ln_st = sb("edge_ln_stats", [128, 2, T, 2, 6], scope=part)
            ln_mv = sb("edge_ln_mean_var", [128, 2, 2, T, 2, 2], scope=part)
            ln_sq = sb("edge_ln_square", [128, 2, T], scope=part)
            ln_var = sb("edge_ln_var", [128, 2, 2, T, 2], scope=part)
            ln_r = sb("edge_ln_rstd", [128, 2, 2, T, 2], scope=part)
            normed = sb("normed", [128, 2, T, 320], scope=part)
            y_big = sb("sh_rows_4", [96, 2, 4, GE], scope=part)
            z_in = sb("rbf_and_sh_rows", [64, 2, 2, GE], scope=part)
            z_rows = sb("rbf_times_sh", [64, GE], scope=part)
            nt = sb("normed_T", [128, 3, GE], scope=part)
            m_s = sb("message_scalars", [128, GE], scope=part)
            m_v = sb("message_vectors", [96, GE], scope=part)
            pr = sb("message_products", [128, 6, GE], scope=part)
            th = sb("leaky_and_tanh", [128, GE], scope=part)
            lk = th[0:64, :]
            gt = sb("tanh_gates", [96, GE], scope=part)
            vg = sb("gated_vectors", [96, GE], scope=part)
            vy = sb("gated_times_y", [96, 4, GE], scope=part)
            us = sb("projected_scalars", [64, GE], scope=part)
            uv = sb("projected_vectors", [96, GE], scope=part)
            xs_y = sb("value_scalars_y0", [64, GE], scope=part)
            xv_y = sb("value_vectors_ym", [96, GE], scope=part)
            h_s = sb("head_scalars", [64, GE], scope=part)
            h_v = sb("head_vectors", [96, GE], scope=part)
            neg = sb("segment_start_minus", [4, GE], scope=part)
            a_max = sb("running_max", [4, 2, GE + 1], scope=part)
            carried = sb("max_carried", [4, GE], scope=part)
            am = sb("a_minus_max", [4, GE], scope=part)
            dec = sb("decay", [4, GE], scope=part)
            ex = sb("exp_a", [4, GE], scope=part)
            den = sb("denominator", [4, 2, GE], scope=part)
            rden = sb("reciprocal_denominator", [4, GE], scope=part)
        with ExitStack() as part:
            row_i = sb("dst_rows", [128, 2, GE + 1], i32, scope=part)
            attr_t = sb("edge_attr_rows", [16, 2, GE], scope=part)
            y_rows = sb("sh_rows", [96, 2, GE], scope=part)
            scaled = sb("scaled_x", [128, 2, T, 256], scope=part)
            xq_prod = sb("x1_times_y", [128, T, 96], scope=part)
            hid = sb("hidden", [64, GE], scope=part)
            w_sb = sb("edge_weights", [128, 2, GE], scope=part)
            prod = sb("products", [128, 2, GE], scope=part)
        with ExitStack() as part:
            x_in = sb("x_chunk", [128, 2, T, D + 1], scope=part)
            agg_in = sb("agg_chunk", [128, 2, T, AW], scope=part)
            attr_in = sb("attr_chunk", [128, 2, T], scope=part)
            nt_s = sb("x_scalars_T", [64, 2, GE], scope=part)
            nt_v = sb("x_vectors_T", [96, 2, GE], scope=part)
            mid = sb("node_mid", [128, 2, T, AW], scope=part)
            feat = sb("node_features", [128, 2, T, D], scope=part)
            gate = sb("node_gates", [128, 2, T, CV], scope=part)
            res = sb("residual", [128, 2, T, D], scope=part)
            stats = sb("ln_stats", [128, 2, T, 6], scope=part)
            mv = sb("ln_mean_var", [128, 2, T, 2], scope=part)
            var_eps = sb("ln_var_eps", [128, 2, T], scope=part)
            rstd = sb("ln_rstd", [128, 2, T], scope=part)
            turn = sb("angle_turns", [128, 2, 2, T], scope=part)
            turn_k = sb("angle_whole_turns", [128, 2, 2, T], scope=part)
            trig = sb("cos_sin", [128, 2, 2, T], scope=part)
            y_out = sb("y_chunk", [128, 2, T, D], scope=part)

        psum = ctx.enter_context(nc.psum_tensor("psum", [128, 8, GE], fp32))

        def bank(b, rows=128):
            return psum[0:rows, b, :]

        P = sems("setup", "beta bias clamp cols_in consts eq ident ident0 idx_in last rows_done rows_in0 "
                          "rows_in1 scaled scaled1 small_in table_zeroed weights_in zeroed")
        conv_sems = sems("edge", "agg aprod aprod_v attr0 attr1 back e_mm fact gather0 gather1 hidden hidden_mm "
                                 "index index_used products proj scan_s scan_v scatter0 scatter1 transposed vec_m "
                                 "vec_y w_copied w_mm xa xq xs_act xt_copied ya")
        EDGE = {0: conv_sems, 2: conv_sems, 3: conv_sems}
        EDGE[1] = sems("edge1", "a_less_max agg aggr applied at_mm av_mm av_read back carried carry decay den "
                                "den_e eps ex gate_t gated gather0 gather1 gs_mm gt_mm gv_mm hs hs_mm hv hv_mm "
                                "hx_s hx_v index index_used leaky m_copied maxed ms ms_mm mv_mm neg norm nt "
                                "nt_copied p_copied p_mm prods rden rows0 rows1 rs_mm rstd rv_mm scan_s scan_v "
                                "scatter0 scatter1 square stats step us_mm us_y uv_mm uv_y vv_mm vy w_mm xs_mm "
                                "xv_mm z")
        node_sems = sems("node", "act aggr applied eps feat half load0 load1 mid res rstd stats store0 store1 "
                                 "transposed trig turn u_mm xt_copied")
        NODE = {l: node_sems for l in range(4)}

        def edge_counts(l):
            if l == 1:
                return {}
            n = {name: NG for name in conv_sems}
            n.update(gather0=32 * NG, gather1=32 * NG, scatter0=32 * NG, scatter1=32 * NG, attr0=16 * NG, attr1=16 * NG)
            if l:
                n.update(ya=0, aprod=0, fact=0)
            return n

        def node_counts(l):
            n = {name: NC for name in node_sems}
            n.update(load0=8 * loads[l] * NC, load1=8 * loads[l] * NC, store0=8 * NC, store1=8 * NC)
            if l == 1:
                n.update(mid=0, transposed=0, xt_copied=0, u_mm=0)
            n.update(act=NC, feat=NC) if l == 2 else n.update(act=0, feat=0)
            n.update(turn=5 * NC, trig=NC, half=NC) if l == 3 else n.update(turn=0, trig=0, half=0)
            return n

        loads = {0: 3, 1: 2, 2: 2, 3: 3}
        base = {}

        def begin(l):
            base.clear()
            for group, counts in ((conv_sems, edge_counts), (node_sems, node_counts)):
                for name, sem in group.items():
                    base[sem.name] = sum(counts(k).get(name, 0) for k in range(l))

        def wait(eng, sem, value):
            if not isinstance(value, int) or value > 0:
                eng.wait_ge(sem, value + base.get(sem.name, 0))

        def held(eng, value, sem=None):
            eng.lower_val(value + (base.get(sem.name, 0) if sem is not None else 0))
            return value

        block = ctx.enter_context(nc.Block())

        def apart(eng):
            eng.wait_ge(P["consts"], 3)

        def apart_from(eng, value):
            held(eng, value)
            apart(eng)

        def setup_sync(eng):
            eng.dma_start(weights[:, :, :].rearrange("p b c -> p (b c)"), t["weights"]).then_inc(P["weights_in"], 16)
            eng.dma_start(wl1[:, :, :].rearrange("p b c -> p (b c)"), t["weights1"]).then_inc(P["weights_in"], 16)
            eng.dma_start(small[:, :], t["small"]).then_inc(P["small_in"], 16)
            eng.dma_start(src_i[:, :], t["src"]).then_inc(P["idx_in"], 16)
            eng.dma_start(dst_i[:, :], t["dst"]).then_inc(P["idx_in"], 16)
            eng.dma_start(last_i[:, :], t["dst_next"]).then_inc(P["idx_in"], 16)
            eng.dma_start(y_col[:, :, :].rearrange("p t c -> p (t c)"), t["sh_cols"]).then_inc(P["cols_in"], 16)

            def row(s, par):
                if live(s, 0, NG):
                    if not isinstance(s, int) or s >= 2:
                        held(eng, s - 1)
                        apart(eng)
                        wait(eng, P["rows_done"], s - 1)
                    eng.dma_start(row_i[:, par, :],
                                  t["dst_row"][0:1, bass.ds(s * GE, GE + 1)].to_broadcast([128, GE + 1]))\
                       .then_inc(P["rows_in1"] if par else P["rows_in0"], 16)
            steps(eng, NG, row, lag=0)

        def setup_tensor(eng):
            eng.wait_ge(P["weights_in"], 32)
            eng.wait_ge(P["small_in"], 16)
            eng.matmul(bank(0)[:, 0:1], V("MS"), small[:, SM["beta"]:SM["beta"] + 1], start=True, stop=True)\
               .then_inc(P["beta"], 1)
            eng.matmul(bank(1, 64)[:, 0:96], V("VT1")[0:64, 0:64], V("WG")[0:64, 0:96], start=True, stop=True)
            eng.matmul(bank(2, 96)[:, 0:96], V("VT2")[0:64, 0:96], V("WG")[0:64, 0:96], start=True, stop=True)\
               .then_inc(P["beta"], 1)
            eng.wait_ge(P["scaled1"], n_scaled1)
            eng.wait_ge(P["consts"], 3)
            eng.matmul(bank(3)[:, 0:1], V("US"), ones_col[:, :], start=True, stop=True)
            eng.matmul(bank(4)[:, 0:1], V("UV"), ones_col[:, :], start=True, stop=True).then_inc(P["beta"], 1)

        def setup_gpsimd(eng):
            eng.memset(ones_col[:, :], 1.0).then_inc(P["consts"], 1)
            eng.memset(ident[:, :], 0.0).then_inc(P["ident0"], 1)
            eng.memset(ones_row[:, :], 1.0).then_inc(P["consts"], 1)
            eng.memset(minus_half[:, :], -0.5).then_inc(P["consts"], 1)
            eng.memset(agg_out[:, :, :, :], 0.0).then_inc(P["zeroed"], 1)
            eng.wait_ge(P["ident0"], 1)
            eng.affine_select(out=ident[:, :], in_=ident[:, :], compare_op=ALU.not_equal, fill=1.0,
                              base=0, pattern=[[-1, 128]], channel_multiplier=1).then_inc(P["ident"], 1)

        def setup_scalar(eng):
            eng.wait_ge(P["zeroed"], 1)
            zeros = agg_out[:, :, :, :].rearrange("p a t c -> p (a t c)")
            rows = 8 * TILE
            for c in range(N // rows):
                eng.dma_start(agg_table[c * rows:(c + 1) * rows, :].rearrange("(p j) c -> p (j c)", p=128),
                              zeros).then_inc(P["table_zeroed"], 16)
            left = N - N // rows * rows
            eng.dma_start(agg_table[N - left:N, :].rearrange("(p j) c -> p (j c)", j=8), zeros[0:left // 8, :])\
               .then_inc(P["table_zeroed"], 16)
        table_zeroed = 16 * (N // (8 * TILE) + 1)

        def setup_vector(eng):
            eng.wait_ge(P["weights_in"], 32)
            n = 0
            for layer, name in BLOCKS:
                scale = CONV[layer]["scale"][name]
                if scale != 1.0:
                    eng.tensor_scalar(W(layer, name), W(layer, name), scale, None, ALU.mult).then_inc(P["scaled"], 1)
                    n += 1
            eng.wait_ge(P["small_in"], 16)
            eng.wait_ge(P["beta"], 2)
            for name, (scale, col) in ATT.items():
                if col:
                    eng.tensor_scalar(V(name), V(name), scale, small[:, SM[col]:SM[col] + 1], ALU.mult, ALU.mult)\
                       .then_inc(P["scaled1"], 1)
                elif scale != 1.0:
                    eng.tensor_scalar(V(name), V(name), scale, None, ALU.mult).then_inc(P["scaled1"], 1)
            eng.tensor_copy(bias[:, 0:1], bank(0)[:, 0:1])
            eng.tensor_copy(V("G1")[0:64, 0:96], bank(1, 64)[:, 0:96])
            eng.tensor_scalar(V("G2")[0:96, 0:96], bank(2, 96)[:, 0:96], R3, None, ALU.mult)
            eng.wait_ge(P["beta"], 3)
            eng.tensor_copy(bias[:, 1:2], bank(3)[:, 0:1])
            eng.tensor_copy(bias[:, 2:3], bank(4)[:, 0:1]).then_inc(P["bias"], 1)
            eng.wait_ge(P["idx_in"], 48)
            same = xq_prod[:, :, :].rearrange("p t c -> p (t c)")[:, 0:EP // TILE]
            eng.tensor_tensor(same, last_i[:, :], dst_i[:, :], ALU.is_equal).then_inc(P["eq"], 1)
            eng.wait_ge(P["eq"], 1)
            eng.scalar_tensor_tensor(out=last_i[:, :], in0=same, scalar=BIG, in1=dst_i[:, :],
                                     op0=ALU.mult, op1=ALU.add).then_inc(P["last"], 1)
            eng.wait_ge(P["last"], 1)
            eng.tensor_scalar(dst_i[:, :], dst_i[:, :], float(N - 1), None, ALU.min).then_inc(P["clamp"], 1)

            def row(s, par):
                if live(s, 0, NG):
                    sem = P["rows_in1"] if par else P["rows_in0"]
                    wait(eng, sem, (s - par) * 8 + 16)
                    eng.tensor_tensor(goes_on[:, bass.ds(s * GE, GE)], row_i[:, par, 1:GE + 1], row_i[:, par, 0:GE],
                                      ALU.is_equal).then_inc(P["rows_done"], 1)
            steps(eng, NG, row, lag=0)
        n_scaled1 = sum(v != (1.0, None) for v in ATT.values())
        n_scaled = sum(CONV[l]["scale"][b] != 1.0 for l, b in BLOCKS)

        TA, TB, H, OS, OV2, OV3, E1, E2 = range(8)
        W1, W2, R0 = TA, TB, OS

        def edge_sync(eng, l):
            S = EDGE[l]
            K = CONV[l]["K"]
            if l:
                stored(eng, l - 1)

            def step(s, par):
                if live(s, 0, NG):
                    held(eng, s - 1, S["hidden_mm"])
                    held(eng, s - 1, S["vec_y"])
                    apart(eng)
                    wait(eng, S["hidden_mm"], s - 1)
                    wait(eng, S["vec_y"], s - 1)
                    sem = S["attr1"] if par else S["attr0"]
                    eng.dma_start(attr_t[0:K, par, :], t[f"attr{K}"][:, bass.ds(s * GE, GE)]).then_inc(sem, 16)
                    eng.dma_start(y_rows[:, par, :], t["sh_big"][96:192, bass.ds(s * GE, GE)]).then_inc(sem, 16)
            steps(eng, NG, step, lag=0)

        def edge_gpsimd(eng, l):
            S = EDGE[l]
            width = D + 1 if l == 0 else D
            if l == 0:
                eng.wait_ge(P["idx_in"], 48)
            else:
                stored(eng, l - 1)
            if l == 0:
                eng.wait_ge(P["last"], 1)

            def step(s, par):
                held(eng, N - 1)
                if live(s, 0, NG):
                    g = s
                    read = held(eng, (g - par) * 32, S["gather0"])
                    now, before = held(eng, g + 1, S["index"]), held(eng, g - 1, S["xs_act"])
                    apart(eng)
                    wait(eng, S["gather1"] if par else S["gather0"], read)
                    eng.tensor_copy(idx_src[:, par, :], src_i[:, bass.ds(g * T, T)]).then_inc(S["index"], 1)
                    apart(eng)
                    wait(eng, S["xs_act"], before)
                    wait(eng, S["xq"], before)
                    wait(eng, S["xa"], before)
                    wait(eng, S["index"], now)
                    for b in range(T):
                        eng.indirect_dma_start(gathered[:, par, b, 0:width], None, x_table[l][:, :],
                                               bass.IndirectOffsetOnAxis(idx_src[:, par, b:b + 1], 0))\
                           .then_inc(S["gather1"] if par else S["gather0"], 16)
                if live(s, 3, NG):
                    g = s - 3
                    q = 1 - par
                    sem = S["scatter1"] if q else S["scatter0"]
                    if isinstance(g, int) and g == 0 and l == 0:
                        eng.wait_ge(P["table_zeroed"], table_zeroed)
                    read, now = held(eng, (g - q) * 32, sem), held(eng, g + 1, S["agg"])
                    apart(eng)
                    wait(eng, sem, read)
                    eng.tensor_copy(idx_last[:, q, :], last_i[:, bass.ds(g * T, T)]).then_inc(S["index_used"], 1)
                    apart(eng)
                    wait(eng, S["index_used"], now)
                    wait(eng, S["agg"], now)
                    for b in range(T):
                        eng.indirect_dma_start(agg_table[:, :], bass.IndirectOffsetOnAxis(idx_last[:, q, b:b + 1], 0),
                                               agg_out[:, q, b, :], None, bounds_check=N - 1, oob_is_err=False)\
                           .then_inc(sem, 16)
            steps(eng, NG, step)

        def edge_scalar(eng, l):
            S = EDGE[l]
            C = CONV[l]
            rows_s = C["S"]
            ns = {0: 64, 2: 96, 3: 64}[l]
            y = y_col if l == 2 else ya_col
            if l == 2:
                eng.wait_ge(P["small_in"], 16)

            def step(s, par):
                if live(s, 0, NG):
                    g = s
                    wait(eng, S["gather1"] if par else S["gather0"], (g - par) * 32 + 64)
                    wait(eng, S["transposed"], g - 1)
                    if l == 0:
                        wait(eng, S["ya"], g + 1)
                    for b in range(T):
                        op = eng.activation(scaled[:, par, b, 64:224], gathered[:, par, b, 0:D], ACT.Copy,
                                            scale=y[:, bass.ds(g * T + b, 1), 0:1].rearrange("p t c -> p (t c)"))
                    op.then_inc(S["xs_act"], 1)
                if live(s, 1, NG):
                    g = s - 1
                    wait(eng, S["transposed"], g + 1)
                    wait(eng, S["e_mm"], g)
                    eng.activation(xt1[:, :], bank(TA), ACT.Copy)
                    eng.activation(xt2[:, :], bank(TB), ACT.Copy).then_inc(S["xt_copied"], 1)
                    wait(eng, S["hidden_mm"], g + 1)
                    wait(eng, S["w_mm"], g)
                    bias = small[0:64, SM["b1"]:SM["b1"] + 1] if l == 2 else 0.0
                    eng.activation(hid[:, :], bank(H, 64), ACT.Silu, bias=bias, scale=C["silu"]).then_inc(S["hidden"], 1)
                    wait(eng, S["w_mm"], g + 1)
                    wait(eng, S["products"], g)
                    for k, b in enumerate((W1, W2)):
                        if l == 2:
                            op = eng.activation(w_sb[:, k, :], bank(b), ACT.Identity,
                                                bias=small[:, SM["b2"] + k:SM["b2"] + k + 1])
                        else:
                            op = eng.activation(w_sb[:, k, :], bank(b), ACT.Copy)
                    op.then_inc(S["w_copied"], 1)
                if live(s, 2, NG) and l:
                    g = s - 2
                    wait(eng, S["back"], g + 1)
                    sem = S["scatter1"] if par else S["scatter0"]
                    wait(eng, sem, (g - par) * 32)
                    r = psum[:, R0:R0 + 2, :].rearrange("p a (b c) -> p (a b) c", c=256)
                    rows = agg_out[:, par]
                    eng.activation(rows[:, :, 0:ns], r[:, :, 0:ns], ACT.Copy)
                    if l == 3:
                        eng.activation(rows[:, :, D:D + 1], r[:, :, 64:65], ACT.Copy)
                    op = eng.activation(rows[:, :, ns:ns + 96].rearrange("p t (v m) -> p t v m", m=3),
                                        r[:, :, 128:224].rearrange("p t (m v) -> p t v m", m=3), ACT.Copy)
                    op.then_inc(S["agg"], 1)
            steps(eng, NG, step)

        def edge_tensor(eng, l):
            S = EDGE[l]
            C = CONV[l]
            rows_s = C["S"]
            if l == 0:
                eng.wait_ge(P["scaled"], n_scaled)
                eng.wait_ge(P["ident"], 1)
                eng.wait_ge(P["consts"], 3)

            def step(s, par):
                if live(s, 1, NG):
                    g, q = s - 1, 1 - par
                    wait(eng, S["xs_act"], g + 1)
                    wait(eng, S["xq"], g + 1)
                    wait(eng, S["xa"], g + 1)
                    wait(eng, S["w_copied"], g)
                    for b in range(T):
                        eng.transpose(psum[:, TA, b * 128:b * 128 + 128], scaled[:, q, b, 0:128], ident[:, :])
                        op = eng.transpose(psum[:, TB, b * 128:b * 128 + 128], scaled[:, q, b, 128:256], ident[:, :])
                    op.then_inc(S["transposed"], 1)
                    wait(eng, S["attr1"] if q else S["attr0"], (g - q) * 16 + 32)
                    wait(eng, S["hidden"], g)
                    eng.matmul(bank(H, 64), W(l, "F1")[0:C["K"], 0:64], attr_t[0:C["K"], q, :], start=True, stop=True)\
                       .then_inc(S["hidden_mm"], 1)
                if live(s, 2, NG):
                    g = s - 2
                    wait(eng, S["products"], g + 1)
                    wait(eng, S["agg"], g)
                    wait(eng, S["vec_m"], g)
                    eng.matmul(bank(OS, rows_s), W(l, "A1")[:, 0:rows_s], prod[:, 0, :], start=True, stop=False)
                    if l == 0:
                        eng.matmul(bank(OS, rows_s), W(l, "CN")[0:1, 0:rows_s], ones_row[:, :], start=False, stop=False)
                    eng.matmul(bank(OS, rows_s), W(l, "A2")[:, 0:rows_s], prod[:, 1, :], start=False, stop=True)
                    eng.matmul(bank(OV2, 96), W(l, "B1")[:, 0:96], prod[:, 0, :], start=True, stop=True)
                    eng.matmul(bank(OV3, 96), W(l, "B2")[:, 0:96], prod[:, 1, :], start=True, stop=True)\
                       .then_inc(S["proj"], 1)
                if live(s, 1, NG):
                    g = s - 1
                    wait(eng, S["xt_copied"], g + 1)
                    wait(eng, S["products"], g)
                    eng.matmul(bank(E1), W(l, "E1"), xt1[:, :], start=True, stop=True)
                    eng.matmul(bank(E2), W(l, "E2"), xt2[:, :], start=True, stop=True).then_inc(S["e_mm"], 1)
                    wait(eng, S["hidden"], g + 1)
                    eng.matmul(bank(W1), W(l, "W1")[0:64, :], hid[:, :], start=True, stop=True)
                    eng.matmul(bank(W2), W(l, "W2")[0:64, :], hid[:, :], start=True, stop=True).then_inc(S["w_mm"], 1)
                if live(s, 2, NG):
                    g = s - 2
                    wait(eng, S["scan_s"], g + 1)
                    wait(eng, S["scan_v"], g + 1)
                    for b in range(T):
                        o = psum[:, R0 + b // 2, (b % 2) * 256:(b % 2) * 256 + 256]
                        eng.transpose(o[:, 0:rows_s], sum_s[0:rows_s, par, b * 128:b * 128 + 128],
                                      ident[0:rows_s, 0:rows_s])
                        op = eng.transpose(o[:, 128:224], sum_v[:, par, b * 128:b * 128 + 128], ident[0:96, 0:96])
                    op.then_inc(S["back"], 1)
            steps(eng, NG, step)

        def edge_vector(eng, l):
            S = EDGE[l]
            rows_s = CONV[l]["S"]
            if l == 0:
                eng.wait_ge(P["cols_in"], 16)
                eng.wait_ge(P["rows_done"], NG)
                eng.wait_ge(P["consts"], 3)
            y = y_col if l == 2 else ya_col

            def step(s, par):
                if live(s, 0, NG):
                    g = s
                    tiles = bass.ds(g * T, T)
                    wait(eng, S["gather1"] if par else S["gather0"], (g - par) * 32 + 64)
                    if l == 0:
                        a = gathered[:, par, :, D:D + 1]
                        eng.tensor_copy(a_src[:, tiles].unsqueeze(2), a).then_inc(S["aprod"], 1)
                        eng.tensor_tensor(ya_col[:, tiles, :], y_col[:, tiles, :], a.to_broadcast([128, T, 4]), ALU.mult)\
                           .then_inc(S["ya"], 1)
                        wait(eng, S["aprod"], g + 1)
                        wait(eng, S["ya"], g + 1)
                    wait(eng, S["transposed"], g - 1)
                    if l == 2:
                        eng.tensor_copy(scaled[:, par, :, 0:64], gathered[:, par, :, 0:64]).then_inc(S["xa"], 1)
                    else:
                        eng.tensor_tensor(scaled[:, par, :, 0:64], gathered[:, par, :, 0:64],
                                          a_src[:, tiles].unsqueeze(2).to_broadcast([128, T, 64]), ALU.mult)\
                           .then_inc(S["xa"], 1)
                    prod4 = xq_prod[:, :, :].rearrange("p t (u m) -> p t u m", m=3)
                    wait(eng, S["xq"], g)
                    eng.tensor_tensor(prod4, gathered[:, par, :, 64:D].rearrange("p t (u m) -> p t u m", m=3),
                                      y[:, tiles, 1:4].unsqueeze(2).to_broadcast([128, T, CV, 3]), ALU.mult)\
                       .then_inc(S["aprod_v"], 1)
                    wait(eng, S["aprod_v"], g + 1)
                    eng.tensor_reduce(scaled[:, par, :, 224:256], prod4, AX.X, ALU.add).then_inc(S["xq"], 1)
                if live(s, 2, NG):
                    g = s - 2
                    cols = bass.ds(g * GE, GE)
                    wait(eng, S["proj"], g + 1)
                    wait(eng, S["attr1"] if par else S["attr0"], (g - par) * 16 + 32)
                    eng.tensor_tensor(vec_y[:, :], bank(OV2, 96), y_rows[:, par, :], ALU.mult).then_inc(S["vec_y"], 1)
                    wait(eng, S["back"], g - 1)
                    first = isinstance(g, int) and g == 0
                    wait(eng, S["scan_s"], g)
                    eng.tensor_tensor_scan(sum_s[0:rows_s, par, :], goes_on[0:rows_s, cols], bank(OS, rows_s),
                                           0.0 if first else sum_s[0:rows_s, 1 - par, GE - 1:GE],
                                           ALU.mult, ALU.add).then_inc(S["scan_s"], 1)
                    wait(eng, S["vec_y"], g + 1)
                    wait(eng, S["scan_v"], g)
                    eng.tensor_tensor(vec_m[:, :], vec_y[:, :], bank(OV3, 96), ALU.add).then_inc(S["vec_m"], 1)
                    wait(eng, S["vec_m"], g + 1)
                    eng.tensor_tensor_scan(sum_v[:, par, :], goes_on[0:96, cols], vec_m[:, :],
                                           0.0 if first else sum_v[:, 1 - par, GE - 1:GE],
                                           ALU.mult, ALU.add).then_inc(S["scan_v"], 1)
                if live(s, 1, NG):
                    g = s - 1
                    wait(eng, S["w_copied"], g + 1)
                    wait(eng, S["e_mm"], g + 1)
                    wait(eng, S["proj"], g)
                    eng.tensor_tensor(prod[:, 0, :], w_sb[:, 0, :], bank(E1), ALU.mult)
                    eng.tensor_tensor(prod[:, 1, :], w_sb[:, 1, :], bank(E2), ALU.mult).then_inc(S["products"], 1)
                if live(s, 2, NG) and l == 0:
                    g = s - 2
                    wait(eng, S["back"], g + 1)
                    sem = S["scatter1"] if par else S["scatter0"]
                    wait(eng, sem, (g - par) * 32)
                    if isinstance(g, int) and g == 0:
                        eng.wait_ge(P["table_zeroed"], table_zeroed)
                    r = psum[:, R0:R0 + 2, :].rearrange("p a (b c) -> p (a b) c", c=256)
                    f = fact[:, par]
                    eng.reciprocal(f[:, 0, :].unsqueeze(2), r[:, :, 65:66]).then_inc(S["fact"], 1)
                    wait(eng, S["fact"], 3 * g + 1)
                    eng.tensor_tensor(f[:, 1, :].unsqueeze(2), r[:, :, 64:65], f[:, 0, :].unsqueeze(2), ALU.mult)\
                       .then_inc(S["fact"], 1)
                    wait(eng, S["fact"], 3 * g + 2)
                    eng.tensor_tensor(f[:, 2, :], f[:, 1, :], f[:, 0, :], ALU.mult).then_inc(S["fact"], 1)
                    wait(eng, S["fact"], 3 * g + 3)
                    rows = agg_out[:, par]
                    eng.tensor_tensor(rows[:, :, 0:64], r[:, :, 0:64],
                                      f[:, 2, :].unsqueeze(2).to_broadcast([128, T, 64]), ALU.mult)
                    eng.tensor_tensor(rows[:, :, 64:D].rearrange("p t (v m) -> p t v m", m=3),
                                      r[:, :, 128:224].rearrange("p t (m v) -> p t v m", m=3),
                                      f[:, 2, :].unsqueeze(2).unsqueeze(3).to_broadcast([128, T, CV, 3]), ALU.mult)\
                       .then_inc(S["agg"], 1)
            steps(eng, NG, step)

        def bank_free(eng, s, name):
            n = NAMES.index(name)
            users = range(n % 8, len(ORDER), 8)
            for back in range(len(ORDER)):
                for k in reversed([k for k in users if back or k < n]):
                    _, lag, sem, per, upto = ORDER[k]
                    g = s - back - lag
                    if live(s - back, lag, NG):
                        apart_from(eng, g * per + upto)
                        wait(eng, EDGE[1][sem], g * per + upto)
                        return
                if isinstance(s, int) and back > s:
                    return

        def pbank(name, rows=128):
            return bank(NAMES.index(name) % 8, rows)

        def steps1(eng, body):
            steps(eng, NG, body, lead=8, lag=5)

        def attn_sync(eng):
            S = EDGE[1]
            stored(eng, 0)

            def step(s, par):
                if live(s, 0, NG):
                    held(eng, s - 1)
                    apart(eng)
                    wait(eng, S["z"], s - 1)
                    wait(eng, S["hv"], s - 1)
                    sem = S["rows1"] if par else S["rows0"]
                    cols = bass.ds(s * GE, GE)
                    eng.dma_start(z_in[:, par, :, :], t["rbf_sh"][:, cols].rearrange("(k p) e -> p k e", k=2)).then_inc(sem, 16)
                    eng.dma_start(y_big[:, par, :, :], t["sh_big"][:, cols].rearrange("(k p) e -> p k e", k=4)).then_inc(sem, 16)
            steps(eng, NG, step, lead=8, lag=0)

        def attn_gpsimd(eng):
            S = EDGE[1]
            stored(eng, 0)

            def step(s, par):
                held(eng, N - 1)
                if live(s, 0, NG):
                    g = s
                    read, now, before = held(eng, (g - par) * 64), held(eng, g + 1), held(eng, g - 1)
                    apart(eng)
                    wait(eng, S["gather1"] if par else S["gather0"], read)
                    eng.tensor_copy(idx_dst[:, par, :], dst_i[:, bass.ds(g * T, T)])
                    eng.tensor_copy(idx_src[:, par, :], src_i[:, bass.ds(g * T, T)]).then_inc(S["index"], 1)
                    apart(eng)
                    wait(eng, S["applied"], before)
                    wait(eng, S["index"], now)
                    for b in range(T):
                        for rows, idx in ((gathered, idx_src), (gathered_d, idx_dst)):
                            eng.indirect_dma_start(rows[:, par, b, 0:D], None, x_table[1][:, :],
                                                   bass.IndirectOffsetOnAxis(idx[:, par, b:b + 1], 0))\
                               .then_inc(S["gather1"] if par else S["gather0"], 16)
                if live(s, 1, NG):
                    g, q = s - 1, 1 - par
                    wait(eng, S["eps"], 2 * g + 2)
                    eng.tensor_tensor(ln_r[:, q].rearrange("p a b c -> p (a b c)"),
                                      ln_var[:, q].rearrange("p a b c -> p (a b c)"), minus_half[:, :], ALU.pow)\
                       .then_inc(S["rstd"], 1)
                if live(s, 5, NG):
                    g, q = s - 5, 1 - par
                    sem = S["scatter1"] if q else S["scatter0"]
                    read, now = held(eng, (g - q) * 32, sem), held(eng, g + 1, S["agg"])
                    apart(eng)
                    wait(eng, sem, read)
                    eng.tensor_copy(idx_last[:, q, :], last_i[:, bass.ds(g * T, T)]).then_inc(S["index_used"], 1)
                    apart(eng)
                    wait(eng, S["index_used"], now)
                    wait(eng, S["agg"], now)
                    for b in range(T):
                        eng.indirect_dma_start(agg_table[:, :], bass.IndirectOffsetOnAxis(idx_last[:, q, b:b + 1], 0),
                                               agg_out[:, q, b, :], None, bounds_check=N - 1, oob_is_err=False)\
                           .then_inc(sem, 16)
            steps1(eng, step)

        def attn_scalar(eng):
            S = EDGE[1]
            eng.wait_ge(P["bias"], 1)

            def step(s, par):
                if live(s, 2, NG):
                    g = s - 2
                    wait(eng, S["mv_mm"], g)
                    for k, rows in enumerate((128, 96, 96)):
                        wait(eng, S["nt"], 3 * g + k + 1)
                        eng.activation(nt[0:rows, k, :], pbank(f"NT{k}", rows), ACT.Copy).then_inc(S["nt_copied"], 1)
                    wait(eng, S["ms_mm"], g + 1)
                    wait(eng, S["prods"], 6 * g)
                    eng.activation(m_s[:, :], pbank("MS"), ACT.Identity, bias=bias[:, 0:1]).then_inc(S["m_copied"], 1)
                    wait(eng, S["mv_mm"], g + 1)
                    eng.activation(m_v[:, :], pbank("MV", 96), ACT.Copy).then_inc(S["m_copied"], 1)
                if live(s, 3, NG):
                    g = s - 3
                    wait(eng, S["av_mm"], g + 1)
                    wait(eng, S["uv_mm"], g)
                    wait(eng, S["at_mm"], g)
                    eng.activation(th[64:128, :], pbank("AV")[64:128, :], ACT.Tanh, scale=0.5)
                    eng.activation(lk, pbank("AV", 64), ACT.Copy, scale=0.2).then_inc(S["av_read"], 1)
                    wait(eng, S["gt_mm"], g + 1)
                    wait(eng, S["gated"], g)
                    eng.activation(gt[:, :], pbank("GT", 96), ACT.Tanh, scale=0.5).then_inc(S["gate_t"], 1)
                if live(s, 4, NG):
                    g = s - 4
                    wait(eng, S["p_mm"], 2 * g + 1)
                    wait(eng, S["back"], g)
                    eng.activation(us[:, :], pbank("PS", 64), ACT.Copy).then_inc(S["p_copied"], 1)
                    wait(eng, S["p_mm"], 2 * g + 2)
                    eng.activation(uv[:, :], pbank("PV", 96), ACT.Copy).then_inc(S["p_copied"], 1)
                    wait(eng, S["back"], g + 1)
                    wait(eng, S["scatter1"] if par else S["scatter0"], (g - par) * 32)
                    rows = agg_out[:, par]
                    eng.activation(rows[:, :, 0:64], pbank("R0")[:, 0:256].rearrange("p (t c) -> p t c", c=64), ACT.Copy)
                    eng.activation(rows[:, :, 64:D].rearrange("p t (v m) -> p t v m", m=3),
                                   pbank("R1")[:, 0:384].rearrange("p (t m v) -> p t v m", t=T, m=3), ACT.Copy)\
                       .then_inc(S["agg"], 1)
                if live(s, 3, NG):
                    g = s - 3
                    wait(eng, S["step"], g + 1)
                    wait(eng, S["den"], g)
                    wait(eng, S["gv_mm"], g)
                    eng.activation(dec[:, :], carried[:, :], ACT.Exp).then_inc(S["decay"], 1)
                    wait(eng, S["a_less_max"], g + 1)
                    eng.activation(ex[:, :], am[:, :], ACT.Exp).then_inc(S["ex"], 1)
            steps1(eng, step)

        def attn_tensor(eng):
            S = EDGE[1]
            eng.wait_ge(P["bias"], 1)

            def mm(name, rows, *pairs):
                for n, (w, x) in enumerate(pairs):
                    op = eng.matmul(pbank(name, rows), w, x, start=n == 0, stop=n == len(pairs) - 1)
                return op

            def step(s, par):
                A, B, C = live(s, 2, NG), live(s, 3, NG), live(s, 4, NG)
                a, b_, c = s - 2, s - 3, s - 4
                if A:
                    apart(eng)
                    wait(eng, S["applied"], a + 1)
                    for k, (lo, n) in enumerate(((0, 128), (128, 96), (224, 96))):
                        bank_free(eng, s, f"NT{k}")
                        for b in range(T):
                            op = eng.transpose(pbank(f"NT{k}", n)[:, b * 128:b * 128 + 128], normed[:, par, b, lo:lo + n],
                                               ident[:, :])
                        op.then_inc(S["nt"], 1)
                if C:
                    wait(eng, S["ex"], c + 1)
                    bank_free(eng, s, "XS")
                    mm("XS", 64, (V("S64")[0:4, 0:64], ex[:, :])).then_inc(S["xs_mm"], 1)
                    bank_free(eng, s, "XV")
                    mm("XV", 96, (V("S96")[0:4, 0:96], ex[:, :])).then_inc(S["xv_mm"], 1)
                    wait(eng, S["decay"], c + 1)
                    bank_free(eng, s, "GS")
                    mm("GS", 64, (V("S64")[0:4, 0:64], dec[:, :])).then_inc(S["gs_mm"], 1)
                    bank_free(eng, s, "GV")
                    mm("GV", 96, (V("S96")[0:4, 0:96], dec[:, :])).then_inc(S["gv_mm"], 1)
                if A:
                    wait(eng, S["nt_copied"], 3 * a + 1)
                    bank_free(eng, s, "MS")
                    mm("MS", 128, (V("MS"), nt[:, 0, :])).then_inc(S["ms_mm"], 1)
                    wait(eng, S["nt_copied"], 3 * a + 3)
                    bank_free(eng, s, "MV")
                    mm("MV", 96, (V("M1")[0:96, 0:96], nt[0:96, 1, :]), (V("M2")[0:96, 0:96], nt[0:96, 2, :]))\
                        .then_inc(S["mv_mm"], 1)
                if B:
                    wait(eng, S["prods"], 6 * b_ + 6)
                    bank_free(eng, s, "AV")
                    mm("AV", 128, (V("A1")[0:64, :], pr[0:64, 0, :]), (V("A2")[0:96, :], pr[0:96, 3, :]))\
                        .then_inc(S["av_mm"], 1)
                    bank_free(eng, s, "GT")
                    mm("GT", 96, (V("G1")[0:64, 0:96], pr[0:64, 0, :]), (V("G2")[0:96, 0:96], pr[0:96, 3, :]))\
                        .then_inc(S["gt_mm"], 1)
                    bank_free(eng, s, "VV")
                    mm("VV", 96, (V("V0")[:, 0:96], pr[:, 0, :]), (V("V1")[:, 0:96], pr[:, 1, :]),
                       (V("VC")[0:96, 0:96], pr[0:96, 2, :]), (V("VF")[0:96, 0:96], pr[0:96, 4, :]),
                       (V("VG")[0:96, 0:96], pr[0:96, 5, :])).then_inc(S["vv_mm"], 1)
                if A:
                    wait(eng, S["z"], a + 1)
                    for name, n in (("B1", 128), ("B2", 128), ("C", 96), ("D", 96), ("F", 96), ("G", 96)):
                        bank_free(eng, s, name)
                        mm(name, n, (V(name)[0:64, 0:n], z_rows[:, :])).then_inc(S["w_mm"], 1)
                if C:
                    wait(eng, S["rden"], c + 1)
                    bank_free(eng, s, "RS")
                    mm("RS", 64, (V("S64")[0:4, 0:64], rden[:, :])).then_inc(S["rs_mm"], 1)
                    bank_free(eng, s, "RV")
                    mm("RV", 96, (V("S96")[0:4, 0:96], rden[:, :])).then_inc(S["rv_mm"], 1)
                if B:
                    wait(eng, S["leaky"], b_ + 1)
                    bank_free(eng, s, "AT")
                    mm("AT", 4, (V("AD")[0:64, 0:4], lk)).then_inc(S["at_mm"], 1)
                    wait(eng, S["av_read"], b_ + 1)
                    bank_free(eng, s, "US")
                    mm("US", 64, (V("US")[64:128, 0:64], th[64:128, :])).then_inc(S["us_mm"], 1)
                    bank_free(eng, s, "UV")
                    mm("UV", 96, (V("UV")[64:128, 0:96], th[64:128, :])).then_inc(S["uv_mm"], 1)
                    wait(eng, S["vy"], 4 * b_ + 4)
                    bank_free(eng, s, "HS")
                    mm("HS", 64, (V("HD")[0:96, 0:64], vy[:, 1, :])).then_inc(S["hs_mm"], 1)
                    bank_free(eng, s, "HV")
                    mm("HV", 96, (V("H0")[0:96, 0:96], vy[:, 0, :]), (V("HF")[0:96, 0:96], vy[:, 2, :]),
                       (V("HG")[0:96, 0:96], vy[:, 3, :])).then_inc(S["hv_mm"], 1)
                if C:
                    wait(eng, S["norm"], 2 * c + 1)
                    bank_free(eng, s, "PS")
                    mm("PS", 64, (V("PS")[0:64, 0:64], xt1[0:64, :])).then_inc(S["p_mm"], 1)
                    wait(eng, S["norm"], 2 * c + 2)
                    bank_free(eng, s, "PV")
                    mm("PV", 96, (V("PV")[0:96, 0:96], xt2[0:96, :])).then_inc(S["p_mm"], 1)
                    apart_from(eng, 2 * c + 2)
                    wait(eng, S["p_copied"], 2 * c + 2)
                    bank_free(eng, s, "R0")
                    bank_free(eng, s, "R1")
                    apart(eng)
                    for b in range(T):
                        eng.transpose(pbank("R0")[:, b * 64:b * 64 + 64], us[:, b * 128:b * 128 + 128], ident[0:64, 0:64])
                    for b in range(T):
                        op = eng.transpose(pbank("R1")[:, b * 96:b * 96 + 96], uv[:, b * 128:b * 128 + 128],
                                           ident[0:96, 0:96])
                    op.then_inc(S["back"], 1)
            steps1(eng, step)

        def attn_vector(eng):
            S = EDGE[1]
            stored(eng, 0)
            eng.memset(a_max[:, :, :], 0.0).then_inc(S["carry"], 1)

            def step(s, par):
                if live(s, 1, NG):
                    g, q = s - 1, 1 - par
                    wait(eng, S["gather1"] if q else S["gather0"], (g - q) * 64 + 128)
                    for side, rows in enumerate((gathered, gathered_d)):
                        for b in range(T):
                            eng.bn_stats(ln_st[:, side, b, 0, :], rows[:, q, b, 0:64])
                            op = eng.bn_stats(ln_st[:, side, b, 1, :], rows[:, q, b, 64:D])
                    op.then_inc(S["stats"], 1)
                    apart_from(eng, g + 1)
                    wait(eng, S["stats"], g + 1)
                    for side in range(2):
                        for b in range(T):
                            for k in range(2):
                                op = eng.bn_aggr(ln_mv[:, q, side, b, k, :], ln_st[:, side, b, k, :])
                    op.then_inc(S["aggr"], 1)
                    wait(eng, S["aggr"], g + 1)
                    wait(eng, S["rstd"], g - 1)
                    eng.tensor_scalar(ln_var[:, q, :, :, 0], ln_mv[:, q, :, :, 0, 1], EPS, None, ALU.add)\
                       .then_inc(S["eps"], 1)
                    eng.tensor_tensor(ln_sq[:, :, :], ln_mv[:, q, :, :, 1, 0], ln_mv[:, q, :, :, 1, 0], ALU.mult)\
                       .then_inc(S["square"], 1)
                    wait(eng, S["square"], g + 1)
                    eng.tensor_tensor(ln_sq[:, :, :], ln_sq[:, :, :], ln_mv[:, q, :, :, 1, 1], ALU.add).then_inc(S["ms"], 1)
                    wait(eng, S["ms"], g + 1)
                    eng.tensor_scalar(ln_var[:, q, :, :, 1], ln_sq[:, :, :], 3.0, EPS, ALU.mult, ALU.add)\
                       .then_inc(S["eps"], 1)
                if live(s, 4, NG):
                    g = s - 4
                    wait(eng, S["xs_mm"], g + 1)
                    wait(eng, S["hs"], g + 1)
                    eng.tensor_tensor(vec_y[0:64, :], h_s[:, :], pbank("XS", 64), ALU.mult).then_inc(S["hx_s"], 1)
                    wait(eng, S["xv_mm"], g + 1)
                    wait(eng, S["hv"], g + 1)
                    eng.tensor_tensor(vec_m[:, :], h_v[:, :], pbank("XV", 96), ALU.mult).then_inc(S["hx_v"], 1)
                    first = isinstance(g, int) and g == 0
                    wait(eng, S["gs_mm"], g + 1)
                    wait(eng, S["hx_s"], g + 1)
                    wait(eng, S["scan_s"], g)
                    eng.tensor_tensor_scan(sum_s[0:64, par, :], pbank("GS", 64), vec_y[0:64, :],
                                           0.0 if first else sum_s[0:64, 1 - par, GE - 1:GE], ALU.mult, ALU.add)\
                       .then_inc(S["scan_s"], 1)
                    wait(eng, S["gv_mm"], g + 1)
                    wait(eng, S["hx_v"], g + 1)
                    wait(eng, S["scan_v"], g)
                    eng.tensor_tensor_scan(sum_v[:, par, :], pbank("GV", 96), vec_m[:, :],
                                           0.0 if first else sum_v[:, 1 - par, GE - 1:GE], ALU.mult, ALU.add)\
                       .then_inc(S["scan_v"], 1)
                    wait(eng, S["ex"], g + 1)
                    wait(eng, S["decay"], g + 1)
                    wait(eng, S["den"], g)
                    eng.tensor_tensor_scan(den[:, par, :], dec[:, :], ex[:, :],
                                           0.0 if first else den[:, 1 - par, GE - 1:GE], ALU.mult, ALU.add)\
                       .then_inc(S["den"], 1)
                    wait(eng, S["den"], g + 1)
                    wait(eng, S["rv_mm"], g)
                    eng.tensor_scalar(rden[:, :], den[:, par, :], 1e-16, None, ALU.add).then_inc(S["den_e"], 1)
                    wait(eng, S["den_e"], g + 1)
                    eng.reciprocal(rden[:, :], rden[:, :]).then_inc(S["rden"], 1)
                if live(s, 1, NG):
                    g, q = s - 1, 1 - par
                    wait(eng, S["rstd"], g + 1)
                    wait(eng, S["nt"], 3 * (g - 1))
                    for side, rows in enumerate((gathered, gathered_d)):
                        for b in range(T):
                            eng.tensor_scalar(normed[:, q, b, 64 * side:64 * side + 64], rows[:, q, b, 0:64],
                                              ln_mv[:, q, side, b, 0, 0:1], ln_r[:, q, side, b, 0:1],
                                              ALU.subtract, ALU.mult)
                            op = eng.tensor_scalar(normed[:, q, b, 128 + 96 * side:224 + 96 * side],
                                                   rows[:, q, b, 64:D], ln_r[:, q, side, b, 1:2], None, ALU.mult)
                    op.then_inc(S["applied"], 1)
                if live(s, 2, NG):
                    g = s - 2
                    wait(eng, S["rows1"] if par else S["rows0"], (g - par) * 16 + 32)
                    wait(eng, S["w_mm"], 6 * g)
                    eng.tensor_tensor(z_rows[:, :], z_in[:, par, 0, :], z_in[:, par, 1, :], ALU.mult).then_inc(S["z"], 1)
                if live(s, 3, NG):
                    g, q = s - 3, 1 - par
                    wait(eng, S["av_read"], g + 1)
                    eng.tensor_tensor(lk, lk, pbank("AV", 64), ALU.max).then_inc(S["leaky"], 1)
                    wait(eng, S["vv_mm"], g + 1)
                    wait(eng, S["gate_t"], g + 1)
                    wait(eng, S["vy"], 4 * g)
                    eng.scalar_tensor_tensor(out=vg[:, :], in0=gt[:, :], scalar=1.0, in1=pbank("VV", 96),
                                             op0=ALU.add, op1=ALU.mult).then_inc(S["gated"], 1)
                    wait(eng, S["gated"], g + 1)
                    wait(eng, S["hv_mm"], g)
                    for k in range(4):
                        eng.tensor_tensor(vy[:, k, :], vg[:, :], y_big[:, q, k, :], ALU.mult).then_inc(S["vy"], 1)
                if live(s, 2, NG):
                    g = s - 2
                    wait(eng, S["m_copied"], 2 * g + 2)
                    wait(eng, S["vv_mm"], g)
                    for k, (name, n, m) in enumerate((("B1", 128, m_s), ("B2", 128, m_s), ("C", 96, m_v),
                                                      ("D", 96, m_v), ("F", 96, m_v), ("G", 96, m_v))):
                        wait(eng, S["w_mm"], 6 * g + k + 1)
                        eng.tensor_tensor(pr[0:n, k, :], m[0:n, :], pbank(name, n), ALU.mult).then_inc(S["prods"], 1)
                if live(s, 4, NG):
                    g = s - 4
                    wait(eng, S["rs_mm"], g + 1)
                    wait(eng, S["scan_s"], g + 1)
                    wait(eng, S["p_mm"], 2 * g)
                    eng.tensor_tensor(xt1[0:64, :], sum_s[0:64, par, :], pbank("RS", 64), ALU.mult).then_inc(S["norm"], 1)
                    wait(eng, S["rv_mm"], g + 1)
                    wait(eng, S["scan_v"], g + 1)
                    eng.tensor_tensor(xt2[0:96, :], sum_v[:, par, :], pbank("RV", 96), ALU.mult).then_inc(S["norm"], 1)
                if live(s, 3, NG):
                    g, q = s - 3, 1 - par
                    eng.tensor_scalar(neg[:, :], goes_on[0:4, bass.ds(g * GE, GE)], -1.0, 1e30, ALU.add, ALU.mult)\
                       .then_inc(S["neg"], 1)
                    wait(eng, S["maxed"], g)
                    eng.tensor_copy(a_max[:, q, 0:1], a_max[:, 1 - q, GE:GE + 1]).then_inc(S["carry"], 1)
                    wait(eng, S["carry"], g + 2)
                    wait(eng, S["neg"], g + 1)
                    wait(eng, S["at_mm"], g + 1)
                    eng.tensor_tensor_scan(a_max[:, q, 1:GE + 1], neg[:, :], pbank("AT", 4), a_max[:, q, 0:1],
                                           ALU.add, ALU.max).then_inc(S["maxed"], 1)
                    wait(eng, S["maxed"], g + 1)
                    wait(eng, S["decay"], g)
                    eng.tensor_tensor(carried[:, :], a_max[:, q, 0:GE], neg[:, :], ALU.add).then_inc(S["carried"], 1)
                    wait(eng, S["ex"], g)
                    eng.tensor_tensor(am[:, :], pbank("AT", 4), a_max[:, q, 1:GE + 1], ALU.subtract)\
                       .then_inc(S["a_less_max"], 1)
                    wait(eng, S["carried"], g + 1)
                    eng.tensor_tensor(carried[:, :], carried[:, :], a_max[:, q, 1:GE + 1], ALU.subtract).then_inc(S["step"], 1)
                if live(s, 3, NG):
                    g, q = s - 3, 1 - par
                    wait(eng, S["us_mm"], g + 1)
                    eng.scalar_tensor_tensor(out=xs_y[:, :], in0=pbank("US", 64), scalar=bias[0:64, 1:2],
                                             in1=y_big[0:64, q, 0, :], op0=ALU.add, op1=ALU.mult).then_inc(S["us_y"], 1)
                    wait(eng, S["uv_mm"], g + 1)
                    eng.scalar_tensor_tensor(out=xv_y[:, :], in0=pbank("UV", 96), scalar=bias[0:96, 2:3],
                                             in1=y_big[:, q, 1, :], op0=ALU.add, op1=ALU.mult).then_inc(S["uv_y"], 1)
                    wait(eng, S["hs_mm"], g + 1)
                    wait(eng, S["us_y"], g + 1)
                    eng.tensor_tensor(h_s[:, :], xs_y[:, :], pbank("HS", 64), ALU.add).then_inc(S["hs"], 1)
                    wait(eng, S["hv_mm"], g + 1)
                    wait(eng, S["uv_y"], g + 1)
                    eng.tensor_tensor(h_v[:, :], xv_y[:, :], pbank("HV", 96), ALU.add).then_inc(S["hv"], 1)
            steps1(eng, step)

        def scattered(eng, l):
            S = EDGE[l]
            eng.wait_ge(S["scatter0"], 32 * NG + base.get(S["scatter0"].name, 0))
            eng.wait_ge(S["scatter1"], 32 * NG + base.get(S["scatter1"].name, 0))

        def stored(eng, l):
            eng.wait_ge(NODE[l]["store0"], 8 * NC * (l + 1))
            eng.wait_ge(NODE[l]["store1"], 8 * NC * (l + 1))

        def chunk(c):
            return c * GE if not isinstance(c, int) else min(c * GE, N - GE)

        def node_steps(eng, body):
            for s in range(4):
                body(s, s % 2)
            with eng.Fori(4, NC - 3, 2) as s:
                body(s, 0)
                body(s + 1, 1)
            for s in range(NC - 2, NC + 3):
                body(s, s % 2)

        agg_cols = {0: D, 1: D, 2: AW, 3: D + 1}

        def node_sync(eng, l):
            S = NODE[l]
            width = D + 1 if l == 0 else D

            def step(s, par):
                if live(s, 0, NC):
                    c = s
                    sem = S["load1"] if par else S["load0"]
                    held(eng, c - 1, S["res"])
                    held(eng, c - 1, S["transposed"])
                    apart(eng)
                    wait(eng, S["res"], c - 1)
                    if l != 1:
                        wait(eng, S["transposed"], c - 1)
                    rows = bass.ds(chunk(c), GE)
                    if l == 0:
                        eng.dma_start(x_in[:, par, :, :].rearrange("p j c -> p (j c)"),
                                      x_table[0][rows, :].rearrange("(p j) c -> p (j c)", j=T)).then_inc(sem, 16)
                    else:
                        eng.dma_start(x_in[:, par, :, 0:D], x_table[l][rows, :].rearrange("(p j) c -> p j c", j=T))\
                           .then_inc(sem, 16)
                    eng.dma_start(agg_in[:, par, :, 0:agg_cols[l]],
                                  agg_table[rows, 0:agg_cols[l]].rearrange("(p j) c -> p j c", j=T)).then_inc(sem, 16)
                    if l in (0, 3):
                        eng.dma_start(attr_in[:, par, :], t["node_attr"][rows, :].rearrange("(p j) c -> p (j c)", j=T))\
                           .then_inc(sem, 16)
                if live(s, 2, NC):
                    c = s - 2
                    held(eng, c + 1, S["applied"])
                    apart(eng)
                    wait(eng, S["applied"], c + 1)
                    if isinstance(c, int) and c == NC - 1:
                        wait(eng, S["store0"], 8 * NC)
                    eng.dma_start(x_table[l + 1][bass.ds(chunk(c), GE), :].rearrange("(p j) c -> p (j c)", j=T),
                                  y_out[:, par, :, :].rearrange("p j c -> p (j c)"))\
                       .then_inc(S["store1"] if par else S["store0"], 16)
            scattered(eng, l)
            node_steps(eng, step)

        def node_tensor(eng, l):
            if l == 1:
                return
            S = NODE[l]
            ns = {0: 64, 2: 96, 3: 64}[l]

            def step(s, par):
                if live(s, 0, NC):
                    c = s
                    loaded = held(eng, (c - par) * 8 * loads[l] + 16 * loads[l], S["load0"])
                    before = held(eng, c - 1, S["xt_copied"])
                    apart(eng)
                    wait(eng, S["load1"] if par else S["load0"], loaded)
                    wait(eng, S["xt_copied"], before)
                    for b in range(T):
                        eng.transpose(psum[0:64, par, b * 128:b * 128 + 128], x_in[:, par, b, 0:64], ident[:, :])
                        op = eng.transpose(psum[0:96, 2 + par, b * 128:b * 128 + 128], x_in[:, par, b, 64:D], ident[:, :])
                    op.then_inc(S["transposed"], 1)
                if live(s, 1, NC):
                    c, q = s - 1, 1 - par
                    wait(eng, S["xt_copied"], c + 1)
                    wait(eng, S["mid"], c - 1)
                    for b in range(T):
                        o = psum[:, 4 + 2 * q + b // 2, (b % 2) * 256:(b % 2) * 256 + 256]
                        cols = slice(b * 128, b * 128 + 128)
                        eng.matmul(o[:, 0:ns], nt_s[:, q, cols], W(l, "SS")[0:64, 0:ns], start=True, stop=True)
                        op = eng.matmul(o[:, ns:ns + 96], nt_v[:, q, cols], W(l, "SV")[0:96, 0:96], start=True, stop=True)
                    op.then_inc(S["u_mm"], 1)
            node_steps(eng, step)

        def node_scalar(eng, l):
            S = NODE[l]
            if l == 1:
                return

            def step(s, par):
                if live(s, 0, NC):
                    c = s
                    wait(eng, S["transposed"], c + 1)
                    wait(eng, S["u_mm"], c - 1)
                    eng.activation(nt_s[:, par, :], psum[0:64, par, :], ACT.Copy)
                    eng.activation(nt_v[:, par, :], psum[0:96, 2 + par, :], ACT.Copy).then_inc(S["xt_copied"], 1)
                if live(s, 1, NC) and l == 2:
                    c, q = s - 1, 1 - par
                    wait(eng, S["mid"], c + 1)
                    wait(eng, S["feat"], c - 1)
                    wait(eng, S["res"], c - 1)
                    eng.activation(feat[:, q, :, 0:64], mid[:, q, :, 0:64], ACT.Silu)
                    eng.activation(gate[:, q, :, :], mid[:, q, :, 64:96], ACT.Silu).then_inc(S["act"], 1)
                if live(s, 1, NC) and l == 3:
                    c, q = s - 1, 1 - par
                    wait(eng, S["turn"], 5 * c + 5)
                    wait(eng, S["res"], c - 1)
                    eng.activation(trig[:, q], turn[:, q], ACT.Sin, scale=6.283185).then_inc(S["trig"], 1)
            node_steps(eng, step)

        def node_gpsimd(eng, l):
            S = NODE[l]

            def step(s, par):
                if live(s, 0, NC) and l == 3:
                    c = s
                    wait(eng, S["load1"] if par else S["load0"], (c - par) * 8 * 3 + 48)
                    wait(eng, S["trig"], c - 1)
                    eng.tensor_tensor(turn[:, par, 1, :].unsqueeze(2), agg_in[:, par, :, D:D + 1],
                                      attr_in[:, par, :].unsqueeze(2), ALU.mult).then_inc(S["turn"], 1)
                    held(eng, 5 * c + 1, S["turn"])
                    apart(eng)
                    wait(eng, S["turn"], 5 * c + 1)
                    eng.tensor_scalar(turn[:, par, 1, :], turn[:, par, 1, :], 0.1 / (2 * math.pi), None, ALU.mult)\
                       .then_inc(S["turn"], 1)
                    held(eng, 5 * c + 2, S["turn"])
                    apart(eng)
                    wait(eng, S["turn"], 5 * c + 2)
                    eng.tensor_scalar(turn[:, par, 0, :], turn[:, par, 1, :], 0.25, None, ALU.add).then_inc(S["turn"], 1)
                    held(eng, 5 * c + 3, S["turn"])
                    apart(eng)
                    wait(eng, S["turn"], 5 * c + 3)
                    eng.tensor_scalar(turn_k[:, par], turn[:, par], MAGIC, MAGIC, ALU.add, ALU.subtract)\
                       .then_inc(S["turn"], 1)
                    wait(eng, S["turn"], 5 * c + 4)
                    eng.tensor_tensor(turn[:, par], turn[:, par], turn_k[:, par], ALU.subtract).then_inc(S["turn"], 1)
                if live(s, 2, NC):
                    c = s - 2
                    wait(eng, S["eps"], c + 1)
                    eng.tensor_tensor(rstd[:, par, :], var_eps[:, par, :], minus_half[:, 0:T], ALU.pow)\
                       .then_inc(S["rstd"], 1)
            if l == 0:
                eng.wait_ge(P["consts"], 3)
            node_steps(eng, step)

        def node_vector(eng, l):
            S = NODE[l]

            def step(s, par):
                if live(s, 1, NC):
                    c, q = s - 1, 1 - par
                    loaded = (c - q) * 8 * loads[l] + 16 * loads[l]
                    u = psum[:, 4 + 2 * q:6 + 2 * q, :].rearrange("p a (b c) -> p (a b) c", c=256)
                    wait(eng, S["load1"] if q else S["load0"], loaded)
                    wait(eng, S["applied"], c - 1)
                    if l != 1:
                        wait(eng, S["u_mm"], c + 1)
                    if l == 0:
                        for b in range(T):
                            op = eng.scalar_tensor_tensor(out=mid[:, q, b, 0:D], in0=agg_in[:, q, b, 0:D],
                                                          scalar=attr_in[:, q, b:b + 1], in1=u[:, b, 0:D],
                                                          op0=ALU.mult, op1=ALU.add)
                        op.then_inc(S["mid"], 1)
                        wait(eng, S["mid"], c + 1)
                        for b in range(T):
                            op = eng.scalar_tensor_tensor(out=res[:, q, b, :], in0=mid[:, q, b, 0:D],
                                                          scalar=attr_in[:, q, b:b + 1], in1=x_in[:, q, b, 0:D],
                                                          op0=ALU.mult, op1=ALU.add)
                        op.then_inc(S["res"], 1)
                    if l == 1:
                        eng.scalar_tensor_tensor(out=res[:, q], in0=x_in[:, q, :, 0:D], scalar=2.0,
                                                 in1=agg_in[:, q, :, 0:D], op0=ALU.mult, op1=ALU.add).then_inc(S["res"], 1)
                    if l == 2:
                        eng.tensor_tensor(mid[:, q], agg_in[:, q], u[:, :, 0:AW], ALU.add).then_inc(S["mid"], 1)
                        wait(eng, S["mid"], c + 1)
                        wait(eng, S["act"], c + 1)
                        for b in range(T):
                            op = eng.tensor_tensor(feat[:, q, b, 64:D].rearrange("p (v m) -> p v m", m=3),
                                                   mid[:, q, b, 96:AW].rearrange("p (v m) -> p v m", m=3),
                                                   gate[:, q, b, :].unsqueeze(2).to_broadcast([128, CV, 3]), ALU.mult)
                        op.then_inc(S["feat"], 1)
                        wait(eng, S["feat"], c + 1)
                        eng.scalar_tensor_tensor(out=res[:, q], in0=x_in[:, q, :, 0:D], scalar=2.0, in1=feat[:, q],
                                                 op0=ALU.mult, op1=ALU.add).then_inc(S["res"], 1)
                    if l == 3:
                        wait(eng, S["trig"], c + 1)
                        f = fact[:, q]
                        eng.tensor_tensor(f[:, 0:2, :], trig[:, q], attr_in[:, q, :].unsqueeze(1).to_broadcast([128, 2, T]),
                                          ALU.mult).then_inc(S["half"], 1)
                        wait(eng, S["half"], c + 1)
                        for b in range(T):
                            op = eng.scalar_tensor_tensor(out=mid[:, q, b, 0:D], in0=u[:, b, 0:D],
                                                          scalar=f[:, 0, b:b + 1], in1=x_in[:, q, b, 0:D],
                                                          op0=ALU.mult, op1=ALU.add)
                        op.then_inc(S["mid"], 1)
                        wait(eng, S["mid"], c + 1)
                        for b in range(T):
                            op = eng.scalar_tensor_tensor(out=res[:, q, b, :], in0=agg_in[:, q, b, 0:D],
                                                          scalar=f[:, 1, b:b + 1], in1=mid[:, q, b, 0:D],
                                                          op0=ALU.mult, op1=ALU.add)
                        op.then_inc(S["res"], 1)
                    wait(eng, S["res"], c + 1)
                    for b in range(T):
                        op = eng.bn_stats(stats[:, q, b, :], res[:, q, b, :])
                    op.then_inc(S["stats"], 1)
                    held(eng, c + 1, S["stats"])
                    apart(eng)
                    wait(eng, S["stats"], c + 1)
                    for b in range(T):
                        op = eng.bn_aggr(mv[:, q, b, :], stats[:, q, b, :])
                    op.then_inc(S["aggr"], 1)
                    wait(eng, S["aggr"], c + 1)
                    wait(eng, S["rstd"], c - 1)
                    eng.tensor_scalar(var_eps[:, q, :].unsqueeze(2), mv[:, q, :, 1:2], EPS, None, ALU.add)\
                       .then_inc(S["eps"], 1)
                if live(s, 2, NC):
                    c = s - 2
                    wait(eng, S["rstd"], c + 1)
                    wait(eng, S["store1"] if par else S["store0"], (c - par) * 8)
                    for b in range(T):
                        op = eng.tensor_scalar(y_out[:, par, b, :], res[:, par, b, :], mv[:, par, b, 0:1],
                                               rstd[:, par, b:b + 1], ALU.subtract, ALU.mult)
                    op.then_inc(S["applied"], 1)
            node_steps(eng, step)

        @block.sync
        def _(eng):
            setup_sync(eng)
            for l in range(layers):
                begin(l)
                if l == 1:
                    attn_sync(eng)
                else:
                    edge_sync(eng, l)
                node_sync(eng, l)
            stored(eng, layers - 1)

        @block.gpsimd
        def _(eng):
            setup_gpsimd(eng)
            for l in range(layers):
                begin(l)
                if l == 1:
                    attn_gpsimd(eng)
                else:
                    edge_gpsimd(eng, l)
                node_gpsimd(eng, l)

        @block.scalar
        def _(eng):
            setup_scalar(eng)
            for l in range(layers):
                begin(l)
                if l == 1:
                    attn_scalar(eng)
                else:
                    edge_scalar(eng, l)
                node_scalar(eng, l)

        @block.tensor
        def _(eng):
            setup_tensor(eng)
            for l in range(layers):
                begin(l)
                if l == 1:
                    attn_tensor(eng)
                else:
                    edge_tensor(eng, l)
                node_tensor(eng, l)

        @block.vector
        def _(eng):
            setup_vector(eng)
            for l in range(layers):
                begin(l)
                if l == 1:
                    attn_vector(eng)
                else:
                    edge_vector(eng, l)
                node_vector(eng, l)


LAYERS = 4


def packed_weights(w):
    import numpy as np
    names = {
        0: dict(fc1="L0_gnn_Wfc1", fc2="L0_gnn_Wfc2", l0="L0_gnn_Wl1_0", l1="L0_gnn_Wl1_1", s="L0_gnn_Wl2_s",
                v="L0_gnn_Wl2_v", x="L0_gnn_Wa", sc0="L0_gnn_Wsc0", sc1="L0_gnn_Wsc1"),
        2: dict(fc1="L2_gnn_fc_w1", fc2="L2_gnn_fc_w2", l0="L2_gnn_W1_s", l1="L2_gnn_W1_v", s="L2_gnn_W2_s",
                v="L2_gnn_W2_v", x=None, sc0="L2_gnn_Wsc_s", sc1="L2_gnn_Wsc_v"),
        3: dict(fc1="L3_gnn_fc_w1", fc2="L3_gnn_fc_w2", l0="L3_gnn_lin1_w0", l1="L3_gnn_lin1_w1", s="L3_gnn_lin2_w0",
                v="L3_gnn_lin2_w1", x="L3_gnn_lin3_w", sc0="L3_gnn_sc_w0", sc1="L3_gnn_sc_w1"),
    }
    out = np.zeros((128, len(BLOCKS), 128), np.float32)
    for layer, n in names.items():
        g = {k: (w[v] if v else None) for k, v in n.items()}

        def put(name):
            return out[:, BLOCKS.index((layer, name)), :]
        fc2, ws, wv = g["fc2"], g["s"], g["v"]
        so = ws.shape[1]
        b = put("E1")
        b[0:64, 0:64] = g["l0"]
        b[64:128, 64:128] = g["l0"]
        b = put("E2")
        for m in range(3):
            b[m:96:3, 32 * m:32 * m + 32] = g["l1"]
        b[96:128, 96:128] = g["l1"]
        put("F1")[0:g["fc1"].shape[0], 0:64] = g["fc1"]
        b = put("W1")
        b[0:64, 0:64] = fc2[:, 64:128]
        b[0:64, 64:128] = fc2[:, 0:64]
        b = put("W2")
        for m in range(3):
            b[0:64, 32 * m:32 * m + 32] = fc2[:, 128:160]
        b[0:64, 96:128] = fc2[:, 160:192]
        put("A1")[64:128, 0:so] = ws[0:64]
        put("A2")[96:128, 0:so] = ws[64:96]
        if g["x"] is not None:
            put("A1")[64:128, 64:65] = g["x"][0:64]
            put("A2")[96:128, 64:65] = g["x"][64:96]
        for m in range(3):
            put("B1")[0:64, 32 * m:32 * m + 32] = wv[0:64]
            put("B2")[32 * m:32 * m + 32, 32 * m:32 * m + 32] = wv[64:96]
        put("SS")[0:64, 0:so] = g["sc0"]
        for m in range(3):
            put("SV")[m:96:3, m:96:3] = g["sc1"]
        if layer == 0:
            put("CN")[0, 65] = 1.0
    return out.reshape(128, -1)


def packed_weights_1(w):
    import numpy as np
    out = np.zeros((128, NW1, 128), np.float32)
    g = {k[7:]: v for k, v in w.items() if k.startswith("L1_gnn_")}

    def put(name):
        return out[:, ATT_BLOCKS.index(name), :]

    def spread(name, a, rows, shift=0):
        for m in range(3):
            to = (m + shift) % 3
            n = a.shape[1]
            put(name)[32 * m:32 * m + 32, (n * to if rows == 3 else 0):(n * to if rows == 3 else 0) + n] = a
    for k in range(2):
        put("MS")[0:64, 64 * k:64 * k + 64] = g["Ws_src"]
        put("MS")[64:128, 64 * k:64 * k + 64] = g["Ws_dst"]
    rbf = g["W_rbf"]
    for m in range(3):
        put("M1")[m:96:3, 32 * m:32 * m + 32] = g["Wv_src"]
        put("M2")[m:96:3, 32 * m:32 * m + 32] = g["Wv_dst"]
        cols = slice(32 * m, 32 * m + 32)
        put("C")[0:16, cols] = rbf[:, 128:160]
        put("D")[16 * (1 + m):16 * (2 + m), cols] = rbf[:, 160:192]
        for name, shift in (("F", 1), ("G", 2)):
            c = 1 + (m + shift) % 3
            put(name)[16 * c:16 * c + 16, cols] = rbf[:, 192:224]
        put("V0")[64:128, 0:32] = g["Wv_val"][0:64]
        put("VT2")[0:64, cols] = g["Ws_val"][64:96].T
        put("WG")[0:64, cols] = g["Wg"]
        put("UV")[64:128, cols] = g["Wv_vlin"][0:64]
    put("B1")[0:16, 0:64] = rbf[:, 0:64]
    put("B1")[16:32, 64:128] = rbf[:, 64:128]
    put("B2")[32:48, 0:64] = rbf[:, 64:128]
    put("B2")[48:64, 64:128] = rbf[:, 64:128]
    put("A1")[0:64, 0:64] = g["W_alpha"][0:64]
    put("A1")[0:64, 64:128] = g["Ws_val"][0:64]
    spread("A2", np.concatenate([g["W_alpha"][64:96], g["Ws_val"][64:96]], axis=1), 1)
    put("VT1")[0:64, 0:64] = g["Ws_val"][0:64].T
    put("V1")[0:64, 32:64] = g["Wv_val"][0:64]
    put("V1")[64:128, 64:96] = g["Wv_val"][0:64]
    spread("VC", g["Wv_val"][64:96], 3)
    spread("VF", g["Wv_val"][96:128], 3, -1)
    spread("VG", g["Wv_val"][96:128], 3, 1)
    for h in range(4):
        put("AD")[16 * h:16 * h + 16, h] = g["alpha_dot"][0, h]
        put("S64")[h, 16 * h:16 * h + 16] = 1.0
        for m in range(3):
            put("S96")[h, 32 * m + 8 * h:32 * m + 8 * h + 8] = 1.0
    put("US")[64:128, 0:64] = g["Ws_vlin"][0:64]
    spread("HD", g["Ws_vlin"][64:96], 1)
    spread("H0", g["Wv_vlin"][64:96], 3)
    spread("HF", g["Wv_vlin"][96:128], 3, -1)
    spread("HG", g["Wv_vlin"][96:128], 3, 1)
    put("PS")[0:64, 0:64] = g["Wps"]
    spread("PV", g["Wpv"], 3)
    return out.reshape(128, -1)


def kernel(**inputs):
    import numpy as np
    import concourse.bacc as _bacc
    from concourse import mybir as _mybir
    from concourse.bass_utils import run_bass_kernel_spmd as _run

    w = {k: np.asarray(v) for k, v in inputs.items()}
    tiles = EP // TILE

    def by_tile(a, fill):
        full = np.full((EP,) + a.shape[1:], fill, a.dtype)
        full[:len(a)] = a
        return np.ascontiguousarray(full.reshape((tiles, TILE) + a.shape[1:]).swapaxes(0, 1)).reshape(TILE, -1)

    def by_row(a):
        full = np.zeros((a.shape[1], EP), a.dtype)
        full[:, :len(a)] = a.T
        return full
    dst_next = np.full(E, N, np.int32)
    dst_next[:-1] = w["dst"][1:]
    dst_row = np.full((1, EP + 1), N, np.int32)
    dst_row[0, 0] = -1
    dst_row[0, 1:E + 1] = w["dst"]
    small = np.zeros((128, NSMALL), np.float32)
    small[0:64, SM["b1"]] = w["L2_gnn_fc_b1"]
    b2 = w["L2_gnn_fc_b2"]
    small[0:64, SM["b2"]] = b2[64:128]
    small[64:128, SM["b2"]] = b2[0:64]
    for m in range(3):
        small[32 * m:32 * m + 32, SM["b2"] + 1] = b2[128:160]
    small[96:128, SM["b2"] + 1] = b2[160:192]
    for k in range(2):
        small[64 * k:64 * k + 64, SM["gamma_s"]] = w["L1_gnn_gamma_s"]
        small[64 * k:64 * k + 64, SM["beta"]] = w["L1_gnn_beta_s"]
    small[64:128, SM["ss"]] = w["L1_gnn_w2_ss"]
    small[64:128, SM["sv"]] = w["L1_gnn_w2_sv"]
    for m in range(3):
        small[m:96:3, SM["gamma_v"]] = w["L1_gnn_gamma_v"]
        small[32 * m:32 * m + 32, SM["vs"]] = w["L1_gnn_w2_vs"]
        small[32 * m:32 * m + 32, SM["vv0"]] = w["L1_gnn_w2_vv0"]
        small[32 * m:32 * m + 32, SM["vv1"]] = w["L1_gnn_w2_vv1"]
    sh = by_row(w["edge_attr_4"])
    sh_big = np.repeat(sh[[0, 0, 0, 1, 2, 3, 2, 3, 1, 3, 1, 2]], 32, axis=0)
    rbf = by_row(w["edge_attr_16"])
    rbf_sh = np.concatenate([rbf, rbf, rbf, rbf, np.repeat(sh, 16, axis=0)])
    arrays = {
        "x": np.concatenate([w["x"], w["node_vec1"]], axis=1),
        "node_attr": w["node_vec1"],
        "src": by_tile(w["src"], 0), "dst": by_tile(w["dst"], N), "dst_next": by_tile(dst_next, N),
        "dst_row": dst_row,
        "sh_cols": by_tile(w["edge_attr_4"], 0), 
        "attr16": by_row(w["edge_attr_16"]), "attr8": by_row(w["edge_attr_8"]),
        "weights": packed_weights(w), "small": small,
        "weights1": packed_weights_1(w), "sh_big": sh_big, "rbf_sh": rbf_sh,
    }
    nc = _bacc.Bacc("TRN2", target_bir_lowering=False, num_devices=1)
    t = {}
    for name in arrays:
        arrays[name] = np.ascontiguousarray(arrays[name])
        t[name] = nc.dram_tensor("in_" + name, arrays[name].shape, _mybir.dt.from_np(arrays[name].dtype),
                                 kind="ExternalInput").ap()
    out = nc.dram_tensor("out", (N, D), _mybir.dt.float32, kind="ExternalOutput").ap()
    gnn_kernel(nc, t, out, LAYERS)
    r = _run(nc, [{"in_" + name: a for name, a in arrays.items()}], core_ids=[0])
    return r.results[0]["out"]
```

```python
import concourse.bass as bass
from concourse import mybir
from contextlib import ExitStack
import math

N = 50000
E = 25000
D = 160
CS, CV = 64, 32
TILE = 128
T = 4
GE = TILE * T
NG = -(-E // GE)
NG += NG % 2
EP = NG * GE
NC = -(-N // GE)
AW = 192
NB = 4
EPS = 1e-5
BIG = float(1 << 22)

fp32 = mybir.dt.float32
i32 = mybir.dt.int32
u8 = mybir.dt.uint8
ALU = mybir.AluOpType
ACT = mybir.ActivationFunctionType
AX = mybir.AxisListType

R3, R8, R32, R96 = 3 ** -0.5, 1 / 8, 32 ** -0.5, 96 ** -0.5

CONV = {
    0: dict(S=66, K=16, silu=1 / 4, scale=dict(E1=R8, E2=R32, F1=1.0, W1=R8, W2=R8, A1=R96, A2=R96 * R3,
                                            B1=R96, B2=R96, CN=1.0, SS=R8, SV=R32)),
    2: dict(S=96, K=8, silu=1.0, scale=dict(E1=R8, E2=R32, F1=1.0, W1=1.0, W2=1.0, A1=2 * R96,
                                          A2=2 * R96 * R3, B1=2 * R96, B2=2 * R96, SS=R8, SV=R32)),
    3: dict(S=65, K=8, silu=8 ** -0.5, scale=dict(E1=R8, E2=R32, F1=1.0, W1=R8, W2=R8, A1=R96 / 4,
                                                 A2=R96 * R3 / 4, B1=R96 / 4, B2=R96 / 4, SS=R8, SV=R32)),
}
MAGIC = 1.5 * 2 ** 23
SM = dict(b1=0, b2=1, gamma_s=3, gamma_v=4, beta=5, ss=6, sv=7, vs=8, vv0=9, vv1=10)
NSMALL = 11
R2 = 2 ** -0.5
ATT = dict(MS=(1.0, "gamma_s"), M1=(1.0, "gamma_v"), M2=(1.0, "gamma_v"),
           B1=(1.0, None), B2=(1.0, None), C=(1.0, None), D=(1.0, None), F=(1.0, None), G=(1.0, None),
           A1=(1.0, None), A2=(R3, None),
           WG=(1.0, None), V0=(1.0, None), V1=(1.0, None), VC=(1.0, None), VF=(R2, None), VG=(-R2, None),
           US=(0.5, "ss"), UV=(0.5, "sv"), HD=(0.5 * R3, "vv0"), H0=(0.5, "vs"),
           HF=(0.5 * R2, "vv1"), HG=(-0.5 * R2, "vv1"), PS=(1.0, None), PV=(1.0, None), S64=(1.0, None), S96=(1.0, None))
ATT_BLOCKS = list(ATT)
NW1 = len(ATT_BLOCKS)
ORDER = [("NT0", 2, "nt_copied", 3, 1), ("NT1", 2, "nt_copied", 3, 2), ("NT2", 2, "nt_copied", 3, 3),
         ("MS", 2, "m_copied", 2, 1), ("MV", 2, "m_copied", 2, 2),
         ("AV", 3, "leaky", 1, 1), ("VV", 3, "gated", 1, 1), ("GT", 3, "gate_t", 1, 1),
         ("XS", 4, "hx_s", 1, 1), ("XV", 4, "hx_v", 1, 1), ("GS", 4, "scan_s", 1, 1), ("GV", 4, "scan_v", 1, 1),
         ("B1", 2, "prods", 6, 1), ("B2", 2, "prods", 6, 2), ("C", 2, "prods", 6, 3),
         ("D", 2, "prods", 6, 4), ("F", 2, "prods", 6, 5), ("G", 2, "prods", 6, 6),
         ("PS", 4, "p_copied", 2, 1), ("PV", 4, "p_copied", 2, 2),
         ("US", 3, "us_y", 1, 1), ("UV", 3, "uv_y", 1, 1), ("R0", 4, "agg", 1, 1), ("R1", 4, "agg", 1, 1)] + 2 * [
         ("-", 0, "", 0, 0)] + [("HS", 3, "hs", 1, 1), ("HV", 3, "hv", 1, 1)]
NAMES = [o[0] for o in ORDER]
BLOCKS = [(layer, name) for layer in CONV for name in CONV[layer]["scale"]]


def live(s, lag, count):
    return 0 <= s - lag < count if isinstance(s, int) else True


def steps(eng, count, body, lead=6, lag=3):
    for s in range(lead):
        body(s, s % 2)
    with eng.Fori(lead, count - 1, 2) as s:
        body(s, 0)
        body(s + 1, 1)
    for s in range(count, count + lag):
        body(s, s % 2)


def gnn_kernel(nc, t, out, layers=4):
    ctx = ExitStack()
    with ctx:
        def sb(name, shape, dt=fp32, scope=ctx):
            return scope.enter_context(nc.sbuf_tensor(name, shape, dt))

        def sems(prefix, names):
            return {n: ctx.enter_context(nc.semaphore(f"{prefix}_{n}")) for n in names.split()}

        x_table = [t["x"]] + [nc.dram_tensor(f"x_layer{l}", (N, D), fp32).ap() for l in (1, 2, 3)] + [out]
        if layers < 4:
            x_table[layers] = out
        agg_table = nc.dram_tensor("aggregates", (N, AW), fp32).ap()

        weights = sb("weights", [128, len(BLOCKS), 128])
        wl1 = sb("weights_layer1", [128, NW1, 128])
        small = sb("small_columns", [128, NSMALL])
        ident = sb("identity", [128, 128])
        bias = sb("layer1_biases", [128, 3])
        minus_half = sb("minus_half", [128, 4 * T])
        ones_col = sb("ones_column", [128, 1])
        ones_row = sb("ones_row", [1, GE])
        src_i = sb("src_index", [128, EP // TILE], i32)
        dst_i = sb("dst_index", [128, EP // TILE], i32)
        last_i = sb("last_index", [128, EP // TILE], i32)
        y_col = sb("sh_columns", [128, EP // TILE, 4])
        ya_col = sb("sh_times_attr", [128, EP // TILE, 4])
        a_src = sb("attr_of_src", [128, EP // TILE])
        goes_on = sb("segment_goes_on", [128, EP], u8)

        def V(name):
            return wl1[:, ATT_BLOCKS.index(name), :]

        def W(layer, name):
            return weights[:, BLOCKS.index((layer, name)), :]

        gathered = sb("gathered", [128, 2, T, D + 1])
        idx_src = sb("gather_index", [128, 2, T], i32)
        idx_last = sb("scatter_index", [128, 2, T], i32)
        xt1 = sb("scaled_x_T1", [128, GE])
        xt2 = sb("scaled_x_T2", [128, GE])
        vec_y = sb("vector_times_y", [96, GE])
        vec_m = sb("vector_message", [96, GE])
        fact = sb("mean_and_alpha", [128, 2, 3, T])
        sum_s = sb("running_scalars", [96, 2, GE])
        sum_v = sb("running_vectors", [96, 2, GE])
        agg_out = sb("agg_out", [128, 2, T, AW])
        with ExitStack() as part:
            gathered_d = sb("gathered_dst", [128, 2, T, D], scope=part)
            idx_dst = sb("gather_index_dst", [128, 2, T], i32, scope=part)
            ln_st = sb("edge_ln_stats", [128, 2, T, 2, 6], scope=part)
            ln_mv = sb("edge_ln_mean_var", [128, 2, 2, T, 2, 2], scope=part)
            ln_sq = sb("edge_ln_square", [128, 2, T], scope=part)
            ln_var = sb("edge_ln_var", [128, 2, 2, T, 2], scope=part)
            ln_r = sb("edge_ln_rstd", [128, 2, 2, T, 2], scope=part)
            normed = sb("normed", [128, 2, T, 320], scope=part)
            y_big = sb("sh_rows_4", [96, 2, 4, GE], scope=part)
            z_in = sb("rbf_and_sh_rows", [64, 2, 2, GE], scope=part)
            z_rows = sb("rbf_times_sh", [64, GE], scope=part)
            nt = sb("normed_T", [128, 3, GE], scope=part)
            m_s = sb("message_scalars", [128, GE], scope=part)
            m_v = sb("message_vectors", [96, GE], scope=part)
            pr = sb("message_products", [128, 6, GE], scope=part)
            def heads(name, free):
                return sb(name, [68] + free, scope=part)[64:68]
            th = sb("leaky_and_tanh", [128, GE], scope=part)
            lk = th[0:64, :]
            gt = sb("tanh_gates", [96, GE], scope=part)
            vg = sb("gated_vectors", [96, GE], scope=part)
            vy = sb("gated_times_y", [96, 4, GE], scope=part)
            us_val = sb("projected_and_value_scalars", [128, GE], scope=part)
            us, val = us_val[0:64, :], us_val[64:128, :]
            uv = sb("projected_vectors", [96, GE], scope=part)
            xs_y = sb("value_scalars_y0", [64, GE], scope=part)
            xv_y = sb("value_vectors_ym", [96, GE], scope=part)
            h_s = sb("head_scalars", [64, GE], scope=part)
            h_v = sb("head_vectors", [96, GE], scope=part)
            neg = heads("segment_start_minus", [GE])
            a_max = heads("running_max", [2, GE + 1])
            carried = heads("max_carried", [GE])
            am = heads("a_minus_max", [GE])
            dec = heads("decay", [GE])
            ex = heads("exp_a", [GE])
            den = heads("denominator", [2, GE])
            rden = heads("reciprocal_denominator", [GE])
        with ExitStack() as part:
            row_i = sb("dst_rows", [128, 2, GE + 1], i32, scope=part)
            attr_t = sb("edge_attr_rows", [16, 2, GE], scope=part)
            y_rows = sb("sh_rows", [96, 2, GE], scope=part)
            scaled = sb("scaled_x", [128, 2, T, 256], scope=part)
            xq_prod = sb("x1_times_y", [128, T, 96], scope=part)
            hid = sb("hidden", [64, GE], scope=part)
            w_sb = sb("edge_weights", [128, 2, GE], scope=part)
            prod = sb("products", [128, 2, GE], scope=part)
        with ExitStack() as part:
            x_in = sb("x_chunk", [128, NB, T, D + 1], scope=part)
            agg_in = sb("agg_chunk", [128, NB, T, AW], scope=part)
            attr_all = sb("node_attr", [128, NC * T], scope=part)
            y_out = sb("y_chunk", [128, NB, T, D], scope=part)
            nt_s = sb("x_scalars_T", [64, 2, GE], scope=part)
            nt_v = sb("x_vectors_T", [96, 2, GE], scope=part)
            mid = sb("node_mid", [128, 2, T, AW], scope=part)
            feat = sb("node_features", [128, 2, T, D], scope=part)
            gate = sb("node_gates", [128, 2, T, CV], scope=part)
            res = sb("residual", [128, NB, T, D], scope=part)
            stats = sb("ln_stats", [128, 2, T, 6], scope=part)
            mv = sb("ln_mean_var", [128, NB, T, 2], scope=part)
            var_eps = sb("ln_var_eps", [128, 2, T], scope=part)
            rstd = sb("ln_rstd", [128, NB, T], scope=part)
            neg_mean = sb("ln_minus_mean", [128, 2, T], scope=part)
            shift = sb("ln_minus_mean_rstd", [128, NB, T], scope=part)
            turn = sb("angle_turns", [128, 2, 2, T], scope=part)
            turn_k = sb("angle_whole_turns", [128, 2, 2, T], scope=part)
            trig = sb("cos_sin", [128, 2, 2, T], scope=part)
            turned = sb("cos_sin_times_attr", [128, 2, 2, T], scope=part)

        psum = ctx.enter_context(nc.psum_tensor("psum", [128, 8, GE], fp32))

        def bank(b, rows=128):
            return psum[0:rows, b, :]

        P = sems("setup", "attr_in beta bias clamp cols_in consts eq ident ident0 idx_in last rows_done rows_in0 "
                          "rows_in1 scaled scaled1 small_in table_zeroed weights_in zeroed")
        conv_sems = sems("edge", "agg aprod aprod_v attr0 attr1 back e_mm fact gather0 gather1 hidden hidden_mm "
                                 "index index_used products proj scan_s scan_v scatter0 scatter1 transposed vec_m "
                                 "vec_y w_copied w_mm xa xq xs_act xt_copied ya")
        EDGE = {0: conv_sems, 2: conv_sems, 3: conv_sems}
        EDGE[1] = sems("edge1", "a_less_max agg aggr applied applied_v av_mm beta av_read back carried carry decay den "
                                "den_e eps ex gate_t gated gather0 gather1 gs_mm gt_mm gv_mm hs hs_mm hv hv_mm "
                                "hx_s hx_v index index_used leaky m_copied maxed ms ms_mm mv_mm neg gamma nt "
                                "nt_copied p_copied p_mm prods rden rest rows0 rows1 rstd val scan_s scan_v "
                                "scatter0 scatter1 square stats step us_mm us_y uv_mm uv_y vv_mm vy w_mm xs_mm "
                                "xv_mm ys0 ys1 z")
        node_sems = sems("node", "act aggr applied eps feat half load0 load1 load2 load3 mid neg_mean res rstd shift stats "
                                 "store0 store1 store2 store3 transposed trig turn u_mm xt_copied")
        NODE = {l: node_sems for l in range(4)}

        def edge_counts(l):
            if l == 1:
                return {}
            n = {name: NG for name in conv_sems}
            n.update(gather0=32 * NG, gather1=32 * NG, scatter0=32 * NG, scatter1=32 * NG, attr0=16 * NG, attr1=16 * NG)
            if l:
                n.update(ya=0, aprod=0, fact=0)
            return n

        def chunks_of(b):
            return len(range(b, NC, NB))

        def node_counts(l):
            n = {name: NC for name in node_sems}
            for b in range(NB):
                n.update({f"load{b}": 16 * loads[l] * chunks_of(b), f"store{b}": 16 * chunks_of(b)})
            if l == 1:
                n.update(mid=0, transposed=0, xt_copied=0, u_mm=0)
            n.update(act=NC, feat=NC) if l == 2 else n.update(act=0, feat=0)
            n.update(turn=5 * NC, trig=NC, half=NC) if l == 3 else n.update(turn=0, trig=0, half=0)
            return n

        loads = {0: 2, 1: 2, 2: 2, 3: 2}
        base = {}

        def begin(l):
            base.clear()
            for group, counts in ((conv_sems, edge_counts), (node_sems, node_counts)):
                for name, sem in group.items():
                    base[sem.name] = sum(counts(k).get(name, 0) for k in range(l))

        def wait(eng, sem, value):
            if not isinstance(value, int) or value > 0:
                eng.wait_ge(sem, value + base.get(sem.name, 0))

        def at(sem, value):
            return value + base.get(sem.name, 0)

        def held(eng, value, sem=None):
            eng.lower_val(value + (base.get(sem.name, 0) if sem is not None else 0))
            return value

        block = ctx.enter_context(nc.Block())

        def apart(eng):
            eng.wait_ge(P["consts"], 3)

        def apart_from(eng, value):
            held(eng, value)
            apart(eng)

        def setup_sync(eng):
            eng.dma_start(weights[:, :, :].rearrange("p b c -> p (b c)"), t["weights"]).then_inc(P["weights_in"], 16)
            eng.dma_start(wl1[:, :, :].rearrange("p b c -> p (b c)"), t["weights1"]).then_inc(P["weights_in"], 16)
            eng.dma_start(small[:, :], t["small"]).then_inc(P["small_in"], 16)
            eng.dma_start(src_i[:, :], t["src"]).then_inc(P["idx_in"], 16)
            eng.dma_start(dst_i[:, :], t["dst"]).then_inc(P["idx_in"], 16)
            eng.dma_start(last_i[:, :], t["dst_next"]).then_inc(P["idx_in"], 16)
            eng.dma_start(y_col[:, :, :].rearrange("p t c -> p (t c)"), t["sh_cols"]).then_inc(P["cols_in"], 16)

            def row(s, par):
                if live(s, 0, NG):
                    if not isinstance(s, int) or s >= 2:
                        held(eng, s - 1)
                        apart(eng)
                        wait(eng, P["rows_done"], s - 1)
                    eng.dma_start(row_i[:, par, :],
                                  t["dst_row"][0:1, bass.ds(s * GE, GE + 1)].to_broadcast([128, GE + 1]))\
                       .then_inc(P["rows_in1"] if par else P["rows_in0"], 16)
            steps(eng, NG, row, lag=0)

        def setup_tensor(eng):
            eng.wait_ge(P["weights_in"], 32)
            eng.wait_ge(P["small_in"], 16)
            eng.matmul(bank(0)[:, 0:1], V("MS"), small[:, SM["beta"]:SM["beta"] + 1], start=True, stop=True)\
               .then_inc(P["beta"], 1)
            eng.wait_ge(P["scaled1"], n_scaled1)
            eng.wait_ge(P["consts"], 3)
            eng.matmul(bank(3)[:, 0:1], V("US"), ones_col[:, :], start=True, stop=True)
            eng.matmul(bank(4)[:, 0:1], V("UV"), ones_col[:, :], start=True, stop=True).then_inc(P["beta"], 1)

        def setup_gpsimd(eng):
            eng.memset(ones_col[:, :], 1.0).then_inc(P["consts"], 1)
            eng.memset(ident[:, :], 0.0).then_inc(P["ident0"], 1)
            eng.memset(ones_row[:, :], 1.0).then_inc(P["consts"], 1)
            eng.memset(minus_half[:, :], -0.5).then_inc(P["consts"], 1)
            eng.memset(agg_out[:, :, :, :], 0.0).then_inc(P["zeroed"], 1)
            eng.wait_ge(P["ident0"], 1)
            eng.affine_select(out=ident[:, :], in_=ident[:, :], compare_op=ALU.not_equal, fill=1.0,
                              base=0, pattern=[[-1, 128]], channel_multiplier=1).then_inc(P["ident"], 1)

        def setup_scalar(eng):
            eng.wait_ge(P["zeroed"], 1)
            zeros = agg_out[:, :, :, :].rearrange("p a t c -> p (a t c)")
            rows = 8 * TILE
            for c in range(N // rows):
                eng.dma_start(agg_table[c * rows:(c + 1) * rows, :].rearrange("(p j) c -> p (j c)", p=128),
                              zeros).then_inc(P["table_zeroed"], 16)
            left = N - N // rows * rows
            eng.dma_start(agg_table[N - left:N, :].rearrange("(p j) c -> p (j c)", j=8), zeros[0:left // 8, :])\
               .then_inc(P["table_zeroed"], 16)
        table_zeroed = 16 * (N // (8 * TILE) + 1)

        def setup_vector(eng):
            eng.wait_ge(P["weights_in"], 32)
            n = 0
            for layer, name in BLOCKS:
                scale = CONV[layer]["scale"][name]
                if scale != 1.0:
                    eng.tensor_scalar(W(layer, name), W(layer, name), scale, None, ALU.mult).then_inc(P["scaled"], 1)
                    n += 1
            eng.wait_ge(P["small_in"], 16)
            eng.wait_ge(P["beta"], 1)
            for name, (scale, col) in ATT.items():
                if col:
                    eng.tensor_scalar(V(name), V(name), scale, small[:, SM[col]:SM[col] + 1], ALU.mult, ALU.mult)\
                       .then_inc(P["scaled1"], 1)
                elif scale != 1.0:
                    eng.tensor_scalar(V(name), V(name), scale, None, ALU.mult).then_inc(P["scaled1"], 1)
            eng.tensor_copy(bias[:, 0:1], bank(0)[:, 0:1])
            eng.wait_ge(P["beta"], 2)
            eng.tensor_copy(bias[:, 1:2], bank(3)[:, 0:1])
            eng.tensor_copy(bias[:, 2:3], bank(4)[:, 0:1]).then_inc(P["bias"], 1)
            eng.wait_ge(P["idx_in"], 48)
            same = xq_prod[:, :, :].rearrange("p t c -> p (t c)")[:, 0:EP // TILE]
            eng.tensor_tensor(same, last_i[:, :], dst_i[:, :], ALU.is_equal).then_inc(P["eq"], 1)
            eng.wait_ge(P["eq"], 1)
            eng.scalar_tensor_tensor(out=last_i[:, :], in0=same, scalar=BIG, in1=dst_i[:, :],
                                     op0=ALU.mult, op1=ALU.add).then_inc(P["last"], 1)
            eng.wait_ge(P["last"], 1)
            eng.tensor_scalar(dst_i[:, :], dst_i[:, :], float(N - 1), None, ALU.min).then_inc(P["clamp"], 1)

            def row(s, par):
                if live(s, 0, NG):
                    sem = P["rows_in1"] if par else P["rows_in0"]
                    wait(eng, sem, (s - par) * 8 + 16)
                    eng.tensor_tensor(goes_on[:, bass.ds(s * GE, GE)], row_i[:, par, 1:GE + 1], row_i[:, par, 0:GE],
                                      ALU.is_equal).then_inc(P["rows_done"], 1)
            steps(eng, NG, row, lag=0)
        n_scaled1 = sum(v != (1.0, None) for v in ATT.values())
        n_scaled = sum(CONV[l]["scale"][b] != 1.0 for l, b in BLOCKS)

        TA, TB, H, OS, OV2, OV3, E1, E2 = range(8)
        W1, W2, R0 = TA, TB, OS

        def edge_sync(eng, l):
            S = EDGE[l]
            K = CONV[l]["K"]
            if l:
                stored(eng, l - 1)

            def step(s, par):
                if live(s, 0, NG):
                    held(eng, s - 1, S["hidden_mm"])
                    held(eng, s - 1, S["vec_y"])
                    apart(eng)
                    wait(eng, S["hidden_mm"], s - 1)
                    wait(eng, S["vec_y"], s - 1)
                    sem = S["attr1"] if par else S["attr0"]
                    eng.dma_start(attr_t[0:K, par, :], t[f"attr{K}"][:, bass.ds(s * GE, GE)]).then_inc(sem, 16)
                    eng.dma_start(y_rows[:, par, :], t["sh_big"][96:192, bass.ds(s * GE, GE)]).then_inc(sem, 16)
            steps(eng, NG, step, lag=0)

        def edge_gpsimd(eng, l):
            S = EDGE[l]
            width = D + 1 if l == 0 else D
            if l == 0:
                eng.wait_ge(P["idx_in"], 48)
            else:
                stored(eng, l - 1)
            if l == 0:
                eng.wait_ge(P["last"], 1)

            def step(s, par):
                held(eng, N - 1)
                if live(s, 0, NG):
                    g = s
                    read = held(eng, (g - par) * 32, S["gather0"])
                    now, before = held(eng, g + 1, S["index"]), held(eng, g - 1, S["xs_act"])
                    apart(eng)
                    wait(eng, S["gather1"] if par else S["gather0"], read)
                    eng.tensor_copy(idx_src[:, par, :], src_i[:, bass.ds(g * T, T)]).then_inc(S["index"], 1)
                    apart(eng)
                    wait(eng, S["xs_act"], before)
                    wait(eng, S["xq"], before)
                    wait(eng, S["xa"], before)
                    eng.wait_ge(S["index"], at(S["index"], now))
                    for b in range(T):
                        eng.indirect_dma_start(gathered[:, par, b, 0:width], None, x_table[l][:, :],
                                               bass.IndirectOffsetOnAxis(idx_src[:, par, b:b + 1], 0))\
                           .then_inc(S["gather1"] if par else S["gather0"], 16)
                if live(s, 3, NG):
                    g = s - 3
                    q = 1 - par
                    sem = S["scatter1"] if q else S["scatter0"]
                    if isinstance(g, int) and g == 0 and l == 0:
                        eng.wait_ge(P["table_zeroed"], table_zeroed)
                    read, now = held(eng, (g - q) * 32, sem), held(eng, g + 1, S["agg"])
                    apart(eng)
                    wait(eng, sem, read)
                    eng.tensor_copy(idx_last[:, q, :], last_i[:, bass.ds(g * T, T)]).then_inc(S["index_used"], 1)
                    apart(eng)
                    eng.wait_ge(S["index_used"], at(S["index_used"], now))
                    eng.wait_ge(S["agg"], at(S["agg"], now))
                    for b in range(T):
                        eng.indirect_dma_start(agg_table[:, :], bass.IndirectOffsetOnAxis(idx_last[:, q, b:b + 1], 0),
                                               agg_out[:, q, b, :], None, bounds_check=N - 1, oob_is_err=False)\
                           .then_inc(sem, 16)
            steps(eng, NG, step)

        def edge_scalar(eng, l):
            S = EDGE[l]
            C = CONV[l]
            rows_s = C["S"]
            ns = {0: 64, 2: 96, 3: 64}[l]
            y = y_col if l == 2 else ya_col
            if l == 2:
                eng.wait_ge(P["small_in"], 16)

            def step(s, par):
                if live(s, 0, NG):
                    g = s
                    wait(eng, S["gather1"] if par else S["gather0"], (g - par) * 32 + 64)
                    wait(eng, S["transposed"], g - 1)
                    if l == 0:
                        eng.wait_ge(S["ya"], at(S["ya"], g + 1))
                    for b in range(T):
                        op = eng.activation(scaled[:, par, b, 64:224], gathered[:, par, b, 0:D], ACT.Copy,
                                            scale=y[:, bass.ds(g * T + b, 1), 0:1].rearrange("p t c -> p (t c)"))
                    op.then_inc(S["xs_act"], 1)
                if live(s, 1, NG):
                    g = s - 1
                    eng.wait_ge(S["transposed"], at(S["transposed"], g + 1))
                    wait(eng, S["e_mm"], g)
                    eng.activation(xt1[:, :], bank(TA), ACT.Copy)
                    eng.activation(xt2[:, :], bank(TB), ACT.Copy).then_inc(S["xt_copied"], 1)
                    eng.wait_ge(S["hidden_mm"], at(S["hidden_mm"], g + 1))
                    wait(eng, S["w_mm"], g)
                    bias = small[0:64, SM["b1"]:SM["b1"] + 1] if l == 2 else 0.0
                    eng.activation(hid[:, :], bank(H, 64), ACT.Silu, bias=bias, scale=C["silu"]).then_inc(S["hidden"], 1)
                    eng.wait_ge(S["w_mm"], at(S["w_mm"], g + 1))
                    wait(eng, S["products"], g)
                    for k, b in enumerate((W1, W2)):
                        if l == 2:
                            op = eng.activation(w_sb[:, k, :], bank(b), ACT.Identity,
                                                bias=small[:, SM["b2"] + k:SM["b2"] + k + 1])
                        else:
                            op = eng.activation(w_sb[:, k, :], bank(b), ACT.Copy)
                    op.then_inc(S["w_copied"], 1)
                if live(s, 2, NG) and l:
                    g = s - 2
                    eng.wait_ge(S["back"], at(S["back"], g + 1))
                    sem = S["scatter1"] if par else S["scatter0"]
                    wait(eng, sem, (g - par) * 32)
                    r = psum[:, R0:R0 + 2, :].rearrange("p a (b c) -> p (a b) c", c=256)
                    rows = agg_out[:, par]
                    eng.activation(rows[:, :, 0:ns], r[:, :, 0:ns], ACT.Copy)
                    if l == 3:
                        eng.activation(rows[:, :, D:D + 1], r[:, :, 64:65], ACT.Copy)
                    op = eng.activation(rows[:, :, ns:ns + 96].rearrange("p t (v m) -> p t v m", m=3),
                                        r[:, :, 128:224].rearrange("p t (m v) -> p t v m", m=3), ACT.Copy)
                    op.then_inc(S["agg"], 1)
            steps(eng, NG, step)

        def edge_tensor(eng, l):
            S = EDGE[l]
            C = CONV[l]
            rows_s = C["S"]
            if l == 0:
                eng.wait_ge(P["scaled"], n_scaled)
                eng.wait_ge(P["ident"], 1)
                eng.wait_ge(P["consts"], 3)

            def step(s, par):
                if live(s, 1, NG):
                    g, q = s - 1, 1 - par
                    eng.wait_ge(S["xs_act"], at(S["xs_act"], g + 1))
                    eng.wait_ge(S["xq"], at(S["xq"], g + 1))
                    eng.wait_ge(S["xa"], at(S["xa"], g + 1))
                    wait(eng, S["w_copied"], g)
                    for b in range(T):
                        eng.transpose(psum[:, TA, b * 128:b * 128 + 128], scaled[:, q, b, 0:128], ident[:, :])
                        op = eng.transpose(psum[:, TB, b * 128:b * 128 + 128], scaled[:, q, b, 128:256], ident[:, :])
                    op.then_inc(S["transposed"], 1)
                    wait(eng, S["attr1"] if q else S["attr0"], (g - q) * 16 + 32)
                    wait(eng, S["hidden"], g)
                    eng.matmul(bank(H, 64), W(l, "F1")[0:C["K"], 0:64], attr_t[0:C["K"], q, :], start=True, stop=True)\
                       .then_inc(S["hidden_mm"], 1)
                if live(s, 2, NG):
                    g = s - 2
                    eng.wait_ge(S["products"], at(S["products"], g + 1))
                    wait(eng, S["vec_m"], g)
                    eng.matmul(bank(OV3, 96), W(l, "B2")[:, 0:96], prod[:, 1, :], start=True, stop=True)
                    wait(eng, S["agg"], g)
                    eng.matmul(bank(OS, rows_s), W(l, "A1")[:, 0:rows_s], prod[:, 0, :], start=True, stop=False)
                    if l == 0:
                        eng.matmul(bank(OS, rows_s), W(l, "CN")[0:1, 0:rows_s], ones_row[:, :], start=False, stop=False)
                    eng.matmul(bank(OS, rows_s), W(l, "A2")[:, 0:rows_s], prod[:, 1, :], start=False, stop=True)
                    eng.matmul(bank(OV2, 96), W(l, "B1")[:, 0:96], prod[:, 0, :], start=True, stop=True)\
                       .then_inc(S["proj"], 1)
                if live(s, 1, NG):
                    g = s - 1
                    eng.wait_ge(S["hidden"], at(S["hidden"], g + 1))
                    eng.wait_ge(S["xt_copied"], at(S["xt_copied"], g + 1))
                    eng.matmul(bank(W1), W(l, "W1")[0:64, :], hid[:, :], start=True, stop=True)
                    eng.matmul(bank(W2), W(l, "W2")[0:64, :], hid[:, :], start=True, stop=True).then_inc(S["w_mm"], 1)
                    wait(eng, S["products"], g)
                    eng.matmul(bank(E1), W(l, "E1"), xt1[:, :], start=True, stop=True)
                    eng.matmul(bank(E2), W(l, "E2"), xt2[:, :], start=True, stop=True).then_inc(S["e_mm"], 1)
                if live(s, 2, NG):
                    g = s - 2
                    eng.wait_ge(S["scan_s"], at(S["scan_s"], g + 1))
                    eng.wait_ge(S["scan_v"], at(S["scan_v"], g + 1))
                    for b in range(T):
                        o = psum[:, R0 + b // 2, (b % 2) * 256:(b % 2) * 256 + 256]
                        eng.transpose(o[:, 0:rows_s], sum_s[0:rows_s, par, b * 128:b * 128 + 128],
                                      ident[0:rows_s, 0:rows_s])
                        op = eng.transpose(o[:, 128:224], sum_v[:, par, b * 128:b * 128 + 128], ident[0:96, 0:96])
                    op.then_inc(S["back"], 1)
            steps(eng, NG, step)

        def edge_vector(eng, l):
            S = EDGE[l]
            rows_s = CONV[l]["S"]
            if l == 0:
                eng.wait_ge(P["cols_in"], 16)
                eng.wait_ge(P["rows_done"], NG)
                eng.wait_ge(P["consts"], 3)
            y = y_col if l == 2 else ya_col

            def step(s, par):
                if live(s, 0, NG):
                    g = s
                    tiles = bass.ds(g * T, T)
                    wait(eng, S["gather1"] if par else S["gather0"], (g - par) * 32 + 64)
                    if l == 0:
                        a = gathered[:, par, :, D:D + 1]
                        eng.tensor_copy(a_src[:, tiles].unsqueeze(2), a).then_inc(S["aprod"], 1)
                        eng.tensor_tensor(ya_col[:, tiles, :], y_col[:, tiles, :], a.to_broadcast([128, T, 4]), ALU.mult)\
                           .then_inc(S["ya"], 1)
                        eng.wait_ge(S["aprod"], at(S["aprod"], g + 1))
                        eng.wait_ge(S["ya"], at(S["ya"], g + 1))
                    wait(eng, S["transposed"], g - 1)
                    if l == 2:
                        eng.tensor_copy(scaled[:, par, :, 0:64], gathered[:, par, :, 0:64]).then_inc(S["xa"], 1)
                    else:
                        eng.tensor_tensor(scaled[:, par, :, 0:64], gathered[:, par, :, 0:64],
                                          a_src[:, tiles].unsqueeze(2).to_broadcast([128, T, 64]), ALU.mult)\
                           .then_inc(S["xa"], 1)
                    prod4 = xq_prod[:, :, :].rearrange("p t (u m) -> p t u m", m=3)
                    wait(eng, S["xq"], g)
                    eng.tensor_tensor(prod4, gathered[:, par, :, 64:D].rearrange("p t (u m) -> p t u m", m=3),
                                      y[:, tiles, 1:4].unsqueeze(2).to_broadcast([128, T, CV, 3]), ALU.mult)\
                       .then_inc(S["aprod_v"], 1)
                    eng.wait_ge(S["aprod_v"], at(S["aprod_v"], g + 1))
                    eng.tensor_reduce(scaled[:, par, :, 224:256], prod4, AX.X, ALU.add).then_inc(S["xq"], 1)
                if live(s, 2, NG):
                    g = s - 2
                    cols = bass.ds(g * GE, GE)
                    eng.wait_ge(S["proj"], at(S["proj"], g + 1))
                    wait(eng, S["attr1"] if par else S["attr0"], (g - par) * 16 + 32)
                    eng.tensor_tensor(vec_y[:, :], bank(OV2, 96), y_rows[:, par, :], ALU.mult).then_inc(S["vec_y"], 1)
                    wait(eng, S["back"], g - 1)
                    first = isinstance(g, int) and g == 0
                    wait(eng, S["scan_s"], g)
                    eng.tensor_tensor_scan(sum_s[0:rows_s, par, :], goes_on[0:rows_s, cols], bank(OS, rows_s),
                                           0.0 if first else sum_s[0:rows_s, 1 - par, GE - 1:GE],
                                           ALU.mult, ALU.add).then_inc(S["scan_s"], 1)
                    eng.wait_ge(S["vec_y"], at(S["vec_y"], g + 1))
                    wait(eng, S["scan_v"], g)
                    eng.tensor_tensor(vec_m[:, :], vec_y[:, :], bank(OV3, 96), ALU.add).then_inc(S["vec_m"], 1)
                    eng.wait_ge(S["vec_m"], at(S["vec_m"], g + 1))
                    eng.tensor_tensor_scan(sum_v[:, par, :], goes_on[0:96, cols], vec_m[:, :],
                                           0.0 if first else sum_v[:, 1 - par, GE - 1:GE],
                                           ALU.mult, ALU.add).then_inc(S["scan_v"], 1)
                if live(s, 1, NG):
                    g = s - 1
                    eng.wait_ge(S["w_copied"], at(S["w_copied"], g + 1))
                    eng.wait_ge(S["e_mm"], at(S["e_mm"], g + 1))
                    wait(eng, S["proj"], g)
                    eng.tensor_tensor(prod[:, 0, :], w_sb[:, 0, :], bank(E1), ALU.mult)
                    eng.tensor_tensor(prod[:, 1, :], w_sb[:, 1, :], bank(E2), ALU.mult).then_inc(S["products"], 1)
                if live(s, 2, NG) and l == 0:
                    g = s - 2
                    eng.wait_ge(S["back"], at(S["back"], g + 1))
                    sem = S["scatter1"] if par else S["scatter0"]
                    wait(eng, sem, (g - par) * 32)
                    if isinstance(g, int) and g == 0:
                        eng.wait_ge(P["table_zeroed"], table_zeroed)
                    r = psum[:, R0:R0 + 2, :].rearrange("p a (b c) -> p (a b) c", c=256)
                    f = fact[:, par]
                    eng.reciprocal(f[:, 0, :].unsqueeze(2), r[:, :, 65:66]).then_inc(S["fact"], 1)
                    eng.wait_ge(S["fact"], at(S["fact"], 3 * g + 1))
                    eng.tensor_tensor(f[:, 1, :].unsqueeze(2), r[:, :, 64:65], f[:, 0, :].unsqueeze(2), ALU.mult)\
                       .then_inc(S["fact"], 1)
                    eng.wait_ge(S["fact"], at(S["fact"], 3 * g + 2))
                    eng.tensor_tensor(f[:, 2, :], f[:, 1, :], f[:, 0, :], ALU.mult).then_inc(S["fact"], 1)
                    eng.wait_ge(S["fact"], at(S["fact"], 3 * g + 3))
                    rows = agg_out[:, par]
                    eng.tensor_tensor(rows[:, :, 0:64], r[:, :, 0:64],
                                      f[:, 2, :].unsqueeze(2).to_broadcast([128, T, 64]), ALU.mult)
                    eng.tensor_tensor(rows[:, :, 64:D].rearrange("p t (v m) -> p t v m", m=3),
                                      r[:, :, 128:224].rearrange("p t (m v) -> p t v m", m=3),
                                      f[:, 2, :].unsqueeze(2).unsqueeze(3).to_broadcast([128, T, CV, 3]), ALU.mult)\
                       .then_inc(S["agg"], 1)
            steps(eng, NG, step)

        def bank_free(eng, s, name):
            n = NAMES.index(name)
            users = [k for k in range(n % 8, len(ORDER), 8) if NAMES[k] != "-"]
            for back in range(len(ORDER)):
                for k in reversed([k for k in users if back or k < n]):
                    _, lag, sem, per, upto = ORDER[k]
                    g = s - back - lag
                    if live(s - back, lag, NG):
                        apart_from(eng, g * per + upto)
                        wait(eng, EDGE[1][sem], g * per + upto)
                        return
                if isinstance(s, int) and back > s:
                    return

        def pbank(name, rows=128):
            return bank(NAMES.index(name) % 8, rows)

        def steps1(eng, body):
            steps(eng, NG, body, lead=8, lag=5)

        def attn_sync(eng):
            S = EDGE[1]
            stored(eng, 0)

            def step(s, par):
                if live(s, 0, NG):
                    cols = bass.ds(s * GE, GE)
                    held(eng, s - 1)
                    held(eng, 4 * (s - 1))
                    apart(eng)
                    wait(eng, S["z"], s - 1)
                    eng.dma_start(z_in[:, par, :, :], t["rbf_sh"][:, cols].rearrange("(k p) e -> p k e", k=2))\
                       .then_inc(S["rows1"] if par else S["rows0"], 16)
                    apart(eng)
                    wait(eng, S["vy"], 4 * (s - 1))
                    wait(eng, S["uv_y"], s - 1)
                    wait(eng, S["us_y"], s - 1)
                    eng.dma_start(y_big[:, par, :, :], t["sh_big"][:, cols].rearrange("(k p) e -> p k e", k=4))\
                       .then_inc(S["ys1"] if par else S["ys0"], 16)
            steps(eng, NG, step, lead=8, lag=0)

        def attn_gpsimd(eng):
            S = EDGE[1]
            stored(eng, 0)

            def step(s, par):
                held(eng, N - 1)
                if live(s, 1, NG):
                    g, q = s - 1, 1 - par
                    eng.wait_ge(S["eps"], at(S["eps"], 2 * g + 2))
                    eng.tensor_tensor(ln_r[:, q].rearrange("p a b c -> p (a b c)"),
                                      ln_var[:, q].rearrange("p a b c -> p (a b c)"), minus_half[:, :], ALU.pow)\
                       .then_inc(S["rstd"], 1)
                if live(s, 0, NG):
                    g = s
                    read, now, before = held(eng, (g - par) * 64), held(eng, g + 1), held(eng, g - 1)
                    apart(eng)
                    wait(eng, S["gather1"] if par else S["gather0"], read)
                    eng.tensor_copy(idx_dst[:, par, :], dst_i[:, bass.ds(g * T, T)])
                    eng.tensor_copy(idx_src[:, par, :], src_i[:, bass.ds(g * T, T)]).then_inc(S["index"], 1)
                    apart(eng)
                    wait(eng, S["applied_v"], before)
                    wait(eng, S["applied"], before)
                    eng.wait_ge(S["index"], at(S["index"], now))
                    for b in range(T):
                        for rows, idx in ((gathered, idx_src), (gathered_d, idx_dst)):
                            eng.indirect_dma_start(rows[:, par, b, 0:D], None, x_table[1][:, :],
                                                   bass.IndirectOffsetOnAxis(idx[:, par, b:b + 1], 0))\
                               .then_inc(S["gather1"] if par else S["gather0"], 16)
                if live(s, 5, NG):
                    g, q = s - 5, 1 - par
                    sem = S["scatter1"] if q else S["scatter0"]
                    read, now = held(eng, (g - q) * 32, sem), held(eng, g + 1, S["agg"])
                    apart(eng)
                    wait(eng, sem, read)
                    eng.tensor_copy(idx_last[:, q, :], last_i[:, bass.ds(g * T, T)]).then_inc(S["index_used"], 1)
                    apart(eng)
                    eng.wait_ge(S["index_used"], at(S["index_used"], now))
                    eng.wait_ge(S["agg"], at(S["agg"], now))
                    for b in range(T):
                        eng.indirect_dma_start(agg_table[:, :], bass.IndirectOffsetOnAxis(idx_last[:, q, b:b + 1], 0),
                                               agg_out[:, q, b, :], None, bounds_check=N - 1, oob_is_err=False)\
                           .then_inc(sem, 16)
            steps1(eng, step)

        def attn_scalar(eng):
            S = EDGE[1]
            eng.wait_ge(P["bias"], 1)

            def step(s, par):
                if live(s, 2, NG):
                    g = s - 2
                    wait(eng, S["mv_mm"], g)
                    for k, rows in enumerate((128, 96, 96)):
                        eng.wait_ge(S["nt"], at(S["nt"], 3 * g + k + 1))
                        eng.activation(nt[0:rows, k, :], pbank(f"NT{k}", rows), ACT.Copy).then_inc(S["nt_copied"], 1)
                    eng.wait_ge(S["ms_mm"], at(S["ms_mm"], g + 1))
                    wait(eng, S["prods"], 6 * g)
                    eng.activation(m_s[:, :], pbank("MS"), ACT.Identity, bias=bias[:, 0:1]).then_inc(S["m_copied"], 1)
                    eng.wait_ge(S["mv_mm"], at(S["mv_mm"], g + 1))
                    eng.activation(m_v[:, :], pbank("MV", 96), ACT.Copy).then_inc(S["m_copied"], 1)
                if live(s, 3, NG):
                    g = s - 3
                    eng.wait_ge(S["av_mm"], at(S["av_mm"], g + 1))
                    wait(eng, S["gt_mm"], g)
                    eng.activation(val, pbank("AV")[64:128, :], ACT.Copy).then_inc(S["val"], 1)
                    wait(eng, S["uv_mm"], g)
                    eng.activation(th[64:128, :], pbank("AV")[64:128, :], ACT.Tanh, scale=0.5)
                    eng.activation(lk, pbank("AV", 64), ACT.Copy, scale=0.2).then_inc(S["av_read"], 1)
                    eng.wait_ge(S["gt_mm"], at(S["gt_mm"], g + 1))
                    wait(eng, S["gated"], g)
                    eng.activation(gt[:, :], pbank("GT", 96), ACT.Tanh, scale=0.5).then_inc(S["gate_t"], 1)
                if live(s, 1, NG):
                    g, q = s - 1, 1 - par
                    eng.wait_ge(S["rstd"], at(S["rstd"], g + 1))
                    wait(eng, S["nt"], 3 * (g - 1))
                    for side, rows in enumerate((gathered, gathered_d)):
                        for b in range(T):
                            op = eng.activation(normed[:, q, b, 128 + 96 * side:224 + 96 * side], rows[:, q, b, 64:D],
                                                ACT.Copy, scale=ln_r[:, q, side, b, 1:2])
                    op.then_inc(S["applied_v"], 1)
                if live(s, 4, NG):
                    g = s - 4
                    eng.wait_ge(S["p_mm"], at(S["p_mm"], 2 * g + 1))
                    wait(eng, S["back"], g)
                    eng.activation(us[:, :], pbank("PS", 64), ACT.Copy).then_inc(S["p_copied"], 1)
                    eng.wait_ge(S["p_mm"], at(S["p_mm"], 2 * g + 2))
                    eng.activation(uv[:, :], pbank("PV", 96), ACT.Copy).then_inc(S["p_copied"], 1)
                if live(s, 3, NG):
                    g = s - 3
                    eng.wait_ge(S["step"], at(S["step"], g + 1))
                    wait(eng, S["den"], g)
                    wait(eng, S["gv_mm"], g)
                    eng.activation(dec[:, :], carried[:, :], ACT.Exp).then_inc(S["decay"], 1)
                    eng.wait_ge(S["a_less_max"], at(S["a_less_max"], g + 1))
                    eng.activation(ex[:, :], am[:, :], ACT.Exp).then_inc(S["ex"], 1)
                if live(s, 4, NG):
                    g = s - 4
                    eng.wait_ge(S["back"], at(S["back"], g + 1))
                    wait(eng, S["scatter1"] if par else S["scatter0"], (g - par) * 32)
                    rows = agg_out[:, par]
                    eng.activation(rows[:, :, 0:64], pbank("R0")[:, 0:256].rearrange("p (t c) -> p t c", c=64), ACT.Copy)
                    eng.activation(rows[:, :, 64:D].rearrange("p t (v m) -> p t v m", m=3),
                                   pbank("R1")[:, 0:384].rearrange("p (t m v) -> p t v m", t=T, m=3), ACT.Copy)\
                       .then_inc(S["agg"], 1)
            steps1(eng, step)

        def attn_tensor(eng):
            S = EDGE[1]
            eng.wait_ge(P["bias"], 1)

            def mm(name, rows, *pairs):
                for n, (w, x) in enumerate(pairs):
                    op = eng.matmul(pbank(name, rows), w, x, start=n == 0, stop=n == len(pairs) - 1)
                return op

            def step(s, par):
                A, B, C = live(s, 2, NG), live(s, 3, NG), live(s, 4, NG)
                a, b_, c = s - 2, s - 3, s - 4
                if A:
                    apart(eng)
                    eng.wait_ge(S["applied"], at(S["applied"], a + 1))
                    eng.wait_ge(S["applied_v"], at(S["applied_v"], a + 1))
                    for k, (lo, n) in enumerate(((0, 128), (128, 96), (224, 96))):
                        bank_free(eng, s, f"NT{k}")
                        for b in range(T):
                            op = eng.transpose(pbank(f"NT{k}", n)[:, b * 128:b * 128 + 128], normed[:, par, b, lo:lo + n],
                                               ident[:, :])
                        op.then_inc(S["nt"], 1)
                if A:
                    eng.wait_ge(S["nt_copied"], at(S["nt_copied"], 3 * a + 1))
                    bank_free(eng, s, "MS")
                    mm("MS", 128, (V("MS"), nt[:, 0, :])).then_inc(S["ms_mm"], 1)
                    eng.wait_ge(S["nt_copied"], at(S["nt_copied"], 3 * a + 3))
                    bank_free(eng, s, "MV")
                    mm("MV", 96, (V("M1")[0:96, 0:96], nt[0:96, 1, :]), (V("M2")[0:96, 0:96], nt[0:96, 2, :]))\
                        .then_inc(S["mv_mm"], 1)
                if B:
                    eng.wait_ge(S["prods"], at(S["prods"], 6 * b_ + 6))
                    bank_free(eng, s, "AV")
                    mm("AV", 128, (V("A1")[0:64, :], pr[0:64, 0, :]), (V("A2")[0:96, :], pr[0:96, 3, :]))\
                        .then_inc(S["av_mm"], 1)
                    bank_free(eng, s, "VV")
                    mm("VV", 96, (V("V0")[:, 0:96], pr[:, 0, :]), (V("V1")[:, 0:96], pr[:, 1, :]),
                       (V("VC")[0:96, 0:96], pr[0:96, 2, :]), (V("VF")[0:96, 0:96], pr[0:96, 4, :]),
                       (V("VG")[0:96, 0:96], pr[0:96, 5, :])).then_inc(S["vv_mm"], 1)
                    eng.wait_ge(S["val"], at(S["val"], b_ + 1))
                    bank_free(eng, s, "GT")
                    mm("GT", 96, (V("WG")[64:128, 0:96], val)).then_inc(S["gt_mm"], 1)
                if C:
                    eng.wait_ge(S["beta"], at(S["beta"], c + 1))
                    bank_free(eng, s, "XS")
                    mm("XS", 64, (V("S64")[64:68, 0:64], ex)).then_inc(S["xs_mm"], 1)
                    bank_free(eng, s, "XV")
                    mm("XV", 96, (V("S96")[64:68, 0:96], ex)).then_inc(S["xv_mm"], 1)
                    eng.wait_ge(S["gamma"], at(S["gamma"], c + 1))
                    bank_free(eng, s, "GS")
                    mm("GS", 64, (V("S64")[64:68, 0:64], dec)).then_inc(S["gs_mm"], 1)
                    bank_free(eng, s, "GV")
                    mm("GV", 96, (V("S96")[64:68, 0:96], dec)).then_inc(S["gv_mm"], 1)
                if A:
                    eng.wait_ge(S["z"], at(S["z"], a + 1))
                    for name, n in (("B1", 128), ("B2", 128), ("C", 96), ("D", 96), ("F", 96), ("G", 96)):
                        bank_free(eng, s, name)
                        mm(name, n, (V(name)[0:64, 0:n], z_rows[:, :])).then_inc(S["w_mm"], 1)
                if C:
                    apart_from(eng, c + 1)
                    eng.wait_ge(S["scan_s"], at(S["scan_s"], c + 1))
                    bank_free(eng, s, "PS")
                    mm("PS", 64, (V("PS")[0:64, 0:64], sum_s[0:64, par, :])).then_inc(S["p_mm"], 1)
                    eng.wait_ge(S["scan_v"], at(S["scan_v"], c + 1))
                    bank_free(eng, s, "PV")
                    mm("PV", 96, (V("PV")[0:96, 0:96], sum_v[:, par, :])).then_inc(S["p_mm"], 1)
                if B:
                    eng.wait_ge(S["leaky"], at(S["leaky"], b_ + 1))
                    eng.wait_ge(S["av_read"], at(S["av_read"], b_ + 1))
                    bank_free(eng, s, "US")
                    mm("US", 68, (V("US")[:, 0:68], th[:, :])).then_inc(S["us_mm"], 1)
                    bank_free(eng, s, "UV")
                    mm("UV", 96, (V("UV")[64:128, 0:96], th[64:128, :])).then_inc(S["uv_mm"], 1)
                if C:
                    apart_from(eng, 2 * c + 2)
                    eng.wait_ge(S["p_copied"], at(S["p_copied"], 2 * c + 2))
                    bank_free(eng, s, "R0")
                    bank_free(eng, s, "R1")
                    apart(eng)
                    for b in range(T):
                        eng.transpose(pbank("R0")[:, b * 64:b * 64 + 64], us[:, b * 128:b * 128 + 128], ident[0:64, 0:64])
                    for b in range(T):
                        op = eng.transpose(pbank("R1")[:, b * 96:b * 96 + 96], uv[:, b * 128:b * 128 + 128],
                                           ident[0:96, 0:96])
                    op.then_inc(S["back"], 1)
                if B:
                    eng.wait_ge(S["vy"], at(S["vy"], 4 * b_ + 4))
                    bank_free(eng, s, "HS")
                    mm("HS", 64, (V("HD")[0:96, 0:64], vy[:, 1, :])).then_inc(S["hs_mm"], 1)
                    bank_free(eng, s, "HV")
                    mm("HV", 96, (V("H0")[0:96, 0:96], vy[:, 0, :]), (V("HF")[0:96, 0:96], vy[:, 2, :]),
                       (V("HG")[0:96, 0:96], vy[:, 3, :])).then_inc(S["hv_mm"], 1)
            steps1(eng, step)

        def attn_vector(eng):
            S = EDGE[1]
            stored(eng, 0)
            eng.memset(a_max[:, :, :], 0.0).then_inc(S["carry"], 1)

            def step(s, par):
                if live(s, 4, NG):
                    g = s - 4
                    eng.wait_ge(S["hs_mm"], at(S["hs_mm"], g + 1))
                    eng.wait_ge(S["us_y"], at(S["us_y"], g + 1))
                    eng.tensor_tensor(h_s[:, :], xs_y[:, :], pbank("HS", 64), ALU.add).then_inc(S["hs"], 1)
                    eng.wait_ge(S["hv_mm"], at(S["hv_mm"], g + 1))
                    eng.wait_ge(S["uv_y"], at(S["uv_y"], g + 1))
                    eng.tensor_tensor(h_v[:, :], xv_y[:, :], pbank("HV", 96), ALU.add).then_inc(S["hv"], 1)
                if live(s, 2, NG):
                    g = s - 2
                    wait(eng, S["rows1"] if par else S["rows0"], (g - par) * 8 + 16)
                    wait(eng, S["w_mm"], 6 * g)
                    eng.tensor_tensor(z_rows[:, :], z_in[:, par, 0, :], z_in[:, par, 1, :], ALU.mult).then_inc(S["z"], 1)
                if live(s, 4, NG):
                    g = s - 4
                    first = isinstance(g, int) and g == 0
                    eng.wait_ge(S["ex"], at(S["ex"], g + 1))
                    eng.wait_ge(S["decay"], at(S["decay"], g + 1))
                    wait(eng, S["den"], g)
                    eng.tensor_tensor_scan(den[:, par, :], dec, ex, 0.0 if first else den[:, 1 - par, GE - 1:GE],
                                           ALU.mult, ALU.add).then_inc(S["den"], 1)
                    eng.wait_ge(S["den"], at(S["den"], g + 1))
                    eng.tensor_scalar(rden, den[:, par, :], 1e-16, None, ALU.add).then_inc(S["den_e"], 1)
                    eng.tensor_tensor(dec, den[:, par, :], ex, ALU.subtract).then_inc(S["rest"], 1)
                    eng.wait_ge(S["den_e"], at(S["den_e"], g + 1))
                    eng.reciprocal(rden, rden).then_inc(S["rden"], 1)
                    eng.wait_ge(S["rden"], at(S["rden"], g + 1))
                    eng.wait_ge(S["rest"], at(S["rest"], g + 1))
                    eng.tensor_tensor(ex, ex, rden, ALU.mult).then_inc(S["beta"], 1)
                    eng.tensor_tensor(dec, dec, rden, ALU.mult).then_inc(S["gamma"], 1)
                if live(s, 1, NG):
                    g, q = s - 1, 1 - par
                    wait(eng, S["gather1"] if q else S["gather0"], (g - q) * 64 + 128)
                    for side, rows in enumerate((gathered, gathered_d)):
                        for b in range(T):
                            eng.bn_stats(ln_st[:, side, b, 0, :], rows[:, q, b, 0:64])
                            op = eng.bn_stats(ln_st[:, side, b, 1, :], rows[:, q, b, 64:D])
                    op.then_inc(S["stats"], 1)
                    apart_from(eng, g + 1)
                    eng.wait_ge(S["stats"], at(S["stats"], g + 1))
                    for side in range(2):
                        for b in range(T):
                            for k in range(2):
                                op = eng.bn_aggr(ln_mv[:, q, side, b, k, :], ln_st[:, side, b, k, :])
                    op.then_inc(S["aggr"], 1)
                    eng.wait_ge(S["aggr"], at(S["aggr"], g + 1))
                    wait(eng, S["rstd"], g - 1)
                    eng.tensor_scalar(ln_var[:, q, :, :, 0], ln_mv[:, q, :, :, 0, 1], EPS, None, ALU.add)\
                       .then_inc(S["eps"], 1)
                    eng.tensor_tensor(ln_sq[:, :, :], ln_mv[:, q, :, :, 1, 0], ln_mv[:, q, :, :, 1, 0], ALU.mult)\
                       .then_inc(S["square"], 1)
                    eng.wait_ge(S["square"], at(S["square"], g + 1))
                    eng.tensor_tensor(ln_sq[:, :, :], ln_sq[:, :, :], ln_mv[:, q, :, :, 1, 1], ALU.add).then_inc(S["ms"], 1)
                    eng.wait_ge(S["ms"], at(S["ms"], g + 1))
                    eng.tensor_scalar(ln_var[:, q, :, :, 1], ln_sq[:, :, :], 3.0, EPS, ALU.mult, ALU.add)\
                       .then_inc(S["eps"], 1)
                if live(s, 3, NG):
                    g, q = s - 3, 1 - par
                    eng.wait_ge(S["av_read"], at(S["av_read"], g + 1))
                    eng.tensor_tensor(lk, lk, pbank("AV", 64), ALU.max).then_inc(S["leaky"], 1)
                if live(s, 3, NG):
                    g, q = s - 3, 1 - par
                    eng.wait_ge(S["vv_mm"], at(S["vv_mm"], g + 1))
                    eng.wait_ge(S["gate_t"], at(S["gate_t"], g + 1))
                    wait(eng, S["vy"], 4 * g)
                    eng.scalar_tensor_tensor(out=vg[:, :], in0=gt[:, :], scalar=1.0, in1=pbank("VV", 96),
                                             op0=ALU.add, op1=ALU.mult).then_inc(S["gated"], 1)
                    eng.wait_ge(S["gated"], at(S["gated"], g + 1))
                    wait(eng, S["ys1"] if q else S["ys0"], (g - q) * 8 + 16)
                    wait(eng, S["hv_mm"], g)
                    for k in range(4):
                        eng.tensor_tensor(vy[:, k, :], vg[:, :], y_big[:, q, k, :], ALU.mult).then_inc(S["vy"], 1)
                if live(s, 4, NG):
                    g = s - 4
                    eng.wait_ge(S["xs_mm"], at(S["xs_mm"], g + 1))
                    eng.wait_ge(S["hs"], at(S["hs"], g + 1))
                    eng.tensor_tensor(vec_y[0:64, :], h_s[:, :], pbank("XS", 64), ALU.mult).then_inc(S["hx_s"], 1)
                    eng.wait_ge(S["xv_mm"], at(S["xv_mm"], g + 1))
                    eng.wait_ge(S["hv"], at(S["hv"], g + 1))
                    eng.tensor_tensor(vec_m[:, :], h_v[:, :], pbank("XV", 96), ALU.mult).then_inc(S["hx_v"], 1)
                    first = isinstance(g, int) and g == 0
                    eng.wait_ge(S["gs_mm"], at(S["gs_mm"], g + 1))
                    eng.wait_ge(S["hx_s"], at(S["hx_s"], g + 1))
                    wait(eng, S["scan_s"], g)
                    eng.tensor_tensor_scan(sum_s[0:64, par, :], pbank("GS", 64), vec_y[0:64, :],
                                           0.0 if first else sum_s[0:64, 1 - par, GE - 1:GE], ALU.mult, ALU.add)\
                       .then_inc(S["scan_s"], 1)
                    eng.wait_ge(S["gv_mm"], at(S["gv_mm"], g + 1))
                    eng.wait_ge(S["hx_v"], at(S["hx_v"], g + 1))
                    wait(eng, S["scan_v"], g)
                    eng.tensor_tensor_scan(sum_v[:, par, :], pbank("GV", 96), vec_m[:, :],
                                           0.0 if first else sum_v[:, 1 - par, GE - 1:GE], ALU.mult, ALU.add)\
                       .then_inc(S["scan_v"], 1)
                if live(s, 2, NG):
                    g = s - 2
                    eng.wait_ge(S["m_copied"], at(S["m_copied"], 2 * g + 2))
                    wait(eng, S["vv_mm"], g)
                    for k, (name, n, m) in enumerate((("B1", 128, m_s), ("B2", 128, m_s), ("C", 96, m_v),
                                                      ("D", 96, m_v), ("F", 96, m_v), ("G", 96, m_v))):
                        eng.wait_ge(S["w_mm"], at(S["w_mm"], 6 * g + k + 1))
                        eng.tensor_tensor(pr[0:n, k, :], m[0:n, :], pbank(name, n), ALU.mult).then_inc(S["prods"], 1)
                if live(s, 1, NG):
                    g, q = s - 1, 1 - par
                    eng.wait_ge(S["rstd"], at(S["rstd"], g + 1))
                    wait(eng, S["nt"], 3 * (g - 1))
                    for side, rows in enumerate((gathered, gathered_d)):
                        for b in range(T):
                            op = eng.tensor_scalar(normed[:, q, b, 64 * side:64 * side + 64], rows[:, q, b, 0:64],
                                                   ln_mv[:, q, side, b, 0, 0:1], ln_r[:, q, side, b, 0:1],
                                                   ALU.subtract, ALU.mult)
                    op.then_inc(S["applied"], 1)
                if live(s, 3, NG):
                    g, q = s - 3, 1 - par
                    eng.tensor_scalar(neg[:, :], goes_on[64:68, bass.ds(g * GE, GE)], -1.0, 1e30, ALU.add, ALU.mult)\
                       .then_inc(S["neg"], 1)
                    wait(eng, S["maxed"], g)
                    eng.tensor_copy(a_max[:, q, 0:1], a_max[:, 1 - q, GE:GE + 1]).then_inc(S["carry"], 1)
                    eng.wait_ge(S["carry"], at(S["carry"], g + 2))
                    eng.wait_ge(S["neg"], at(S["neg"], g + 1))
                    eng.wait_ge(S["us_mm"], at(S["us_mm"], g + 1))
                    eng.tensor_tensor_scan(a_max[:, q, 1:GE + 1], neg[:, :], pbank("US", 68)[64:68, :], a_max[:, q, 0:1],
                                           ALU.add, ALU.max).then_inc(S["maxed"], 1)
                    eng.wait_ge(S["maxed"], at(S["maxed"], g + 1))
                    wait(eng, S["decay"], g)
                    eng.tensor_tensor(carried[:, :], a_max[:, q, 0:GE], neg[:, :], ALU.add).then_inc(S["carried"], 1)
                    wait(eng, S["ex"], g)
                    eng.tensor_tensor(am[:, :], pbank("US", 68)[64:68, :], a_max[:, q, 1:GE + 1], ALU.subtract)\
                       .then_inc(S["a_less_max"], 1)
                    eng.wait_ge(S["carried"], at(S["carried"], g + 1))
                    eng.tensor_tensor(carried[:, :], carried[:, :], a_max[:, q, 1:GE + 1], ALU.subtract).then_inc(S["step"], 1)
                if live(s, 3, NG):
                    g, q = s - 3, 1 - par
                    eng.wait_ge(S["a_less_max"], at(S["a_less_max"], g + 1))
                    eng.scalar_tensor_tensor(out=xs_y[:, :], in0=pbank("US", 64), scalar=bias[0:64, 1:2],
                                             in1=y_big[0:64, q, 0, :], op0=ALU.add, op1=ALU.mult).then_inc(S["us_y"], 1)
                    eng.wait_ge(S["uv_mm"], at(S["uv_mm"], g + 1))
                    eng.scalar_tensor_tensor(out=xv_y[:, :], in0=pbank("UV", 96), scalar=bias[0:96, 2:3],
                                             in1=y_big[:, q, 1, :], op0=ALU.add, op1=ALU.mult).then_inc(S["uv_y"], 1)
            steps1(eng, step)

        def scattered(eng, l):
            S = EDGE[l]
            eng.wait_ge(S["scatter0"], 32 * NG + base.get(S["scatter0"].name, 0))
            eng.wait_ge(S["scatter1"], 32 * NG + base.get(S["scatter1"].name, 0))

        def stored(eng, l):
            for b in range(NB):
                eng.wait_ge(NODE[l][f"store{b}"], 16 * chunks_of(b) * (l + 1))

        def chunk(c):
            return c * GE if not isinstance(c, int) else min(c * GE, N - GE)

        TURN, USE = 2, 3

        def summed(l):
            return 4 if l == 2 else 3

        def node_steps(eng, body):
            lead = 2 * NB + (NC - 1) % NB
            for s in range(lead):
                body(s, s % NB)
            with eng.Fori(lead, NC - NB, NB) as s:
                for k in range(NB):
                    body(s + k, (lead + k) % NB)
            for s in range(NC - 1, NC + 7):
                body(s, s % NB)

        agg_cols = {0: D, 1: D, 2: AW, 3: D + 1}

        def loaded(l, c, b):
            return (c - b) * (16 // NB) * loads[l] + 16 * loads[l]

        def node_sync(eng, l):
            S = NODE[l]

            def step(s, par):
                if live(s, 0, NC):
                    c = s
                    sem = S[f"load{par}"]
                    held(eng, c - 3, S["res"])
                    held(eng, c - 3, S["transposed"])
                    apart(eng)
                    wait(eng, S["res"], c - 3)
                    if l != 1:
                        wait(eng, S["transposed"], c - 3)
                    rows = bass.ds(chunk(c), GE)
                    if l == 0:
                        eng.dma_start(x_in[:, par, :, :].rearrange("p j c -> p (j c)"),
                                      x_table[0][rows, :].rearrange("(p j) c -> p (j c)", j=T)).then_inc(sem, 16)
                    else:
                        eng.dma_start(x_in[:, par, :, 0:D], x_table[l][rows, :].rearrange("(p j) c -> p j c", j=T))\
                           .then_inc(sem, 16)
                    eng.dma_start(agg_in[:, par, :, 0:agg_cols[l]],
                                  agg_table[rows, 0:agg_cols[l]].rearrange("(p j) c -> p j c", j=T)).then_inc(sem, 16)
                lag = summed(l) + 3
                if live(s, lag, NC):
                    c, b = s - lag, (par - lag) % NB
                    held(eng, c + 1, S["applied"])
                    apart(eng)
                    eng.wait_ge(S["applied"], at(S["applied"], c + 1))
                    if isinstance(c, int) and c == NC - 1:
                        wait(eng, S[f"store{(NC - 2) % NB}"], 16 * chunks_of((NC - 2) % NB))
                    eng.dma_start(x_table[l + 1][bass.ds(chunk(c), GE), :].rearrange("(p j) c -> p (j c)", j=T),
                                  y_out[:, b, :, :].rearrange("p j c -> p (j c)")).then_inc(S[f"store{b}"], 16)
            scattered(eng, l)
            if l in (0, 3):
                eng.dma_start(attr_all[:, :], t["node_attr"]).then_inc(P["attr_in"], 16)
            node_steps(eng, step)

        def node_tensor(eng, l):
            if l == 1:
                return
            S = NODE[l]
            ns = {0: 64, 2: 96, 3: 64}[l]

            def step(s, par):
                if live(s, TURN, NC):
                    c, buf, q = s - TURN, (par - TURN) % NB, (par - TURN) % 2
                    value = held(eng, loaded(l, c, buf), S[f"load{buf}"])
                    before = held(eng, c - 1, S["xt_copied"])
                    apart(eng)
                    eng.wait_ge(S[f"load{buf}"], at(S[f"load{buf}"], value))
                    wait(eng, S["xt_copied"], before)
                    for b in range(T):
                        eng.transpose(psum[0:64, q, b * 128:b * 128 + 128], x_in[:, buf, b, 0:64], ident[:, :])
                        op = eng.transpose(psum[0:96, 2 + q, b * 128:b * 128 + 128], x_in[:, buf, b, 64:D], ident[:, :])
                    op.then_inc(S["transposed"], 1)
                if live(s, USE, NC):
                    c, q = s - USE, (par - USE) % 2
                    eng.wait_ge(S["xt_copied"], at(S["xt_copied"], c + 1))
                    wait(eng, S["mid"], c - 1)
                    for b in range(T):
                        o = psum[:, 4 + 2 * q + b // 2, (b % 2) * 256:(b % 2) * 256 + 256]
                        cols = slice(b * 128, b * 128 + 128)
                        eng.matmul(o[:, 0:ns], nt_s[:, q, cols], W(l, "SS")[0:64, 0:ns], start=True, stop=True)
                        op = eng.matmul(o[:, ns:ns + 96], nt_v[:, q, cols], W(l, "SV")[0:96, 0:96], start=True, stop=True)
                    op.then_inc(S["u_mm"], 1)
            node_steps(eng, step)

        def node_scalar(eng, l):
            S = NODE[l]

            def step(s, par):
                if l != 1 and live(s, TURN, NC):
                    c, q = s - TURN, (par - TURN) % 2
                    eng.wait_ge(S["transposed"], at(S["transposed"], c + 1))
                    wait(eng, S["u_mm"], c - 1)
                    eng.activation(nt_s[:, q, :], psum[0:64, q, :], ACT.Copy)
                    eng.activation(nt_v[:, q, :], psum[0:96, 2 + q, :], ACT.Copy).then_inc(S["xt_copied"], 1)
                if live(s, TURN, NC) and l == 3:
                    c, q = s - TURN, (par - TURN) % 2
                    eng.wait_ge(S["turn"], at(S["turn"], 5 * c + 5))
                    wait(eng, S["half"], c - 1)
                    eng.activation(trig[:, q], turn[:, q], ACT.Sin, scale=6.283185).then_inc(S["trig"], 1)
                if live(s, USE, NC) and l == 2:
                    c, q = s - USE, (par - USE) % 2
                    eng.wait_ge(S["mid"], at(S["mid"], c + 1))
                    wait(eng, S["feat"], c - 1)
                    wait(eng, S["res"], c - 1)
                    eng.activation(feat[:, q, :, 0:64], mid[:, q, :, 0:64], ACT.Silu)
                    eng.activation(gate[:, q, :, :], mid[:, q, :, 64:96], ACT.Silu).then_inc(S["act"], 1)
                lag = summed(l) + 2
                if live(s, lag, NC):
                    c, buf = s - lag, (par - lag) % NB
                    eng.wait_ge(S["shift"], at(S["shift"], c + 1))
                    wait(eng, S[f"store{buf}"], (c - buf) * (16 // NB))
                    for b in range(T):
                        op = eng.activation(y_out[:, buf, b, :], res[:, buf, b, :], ACT.Identity,
                                            bias=shift[:, buf, b:b + 1], scale=rstd[:, buf, b:b + 1])
                    op.then_inc(S["applied"], 1)
            node_steps(eng, step)

        def node_gpsimd(eng, l):
            S = NODE[l]

            def step(s, par):
                lag = summed(l) + 1
                if live(s, lag, NC):
                    c, buf, q = s - lag, (par - lag) % NB, (par - lag) % 2
                    eng.wait_ge(S["eps"], at(S["eps"], c + 1))
                    wait(eng, S["applied"], c - 3)
                    eng.tensor_tensor(rstd[:, buf, :], var_eps[:, q, :], minus_half[:, 0:T], ALU.pow)\
                       .then_inc(S["rstd"], 1)
                    eng.wait_ge(S["rstd"], at(S["rstd"], c + 1))
                    eng.wait_ge(S["neg_mean"], at(S["neg_mean"], c + 1))
                    eng.tensor_tensor(shift[:, buf, :], neg_mean[:, q, :], rstd[:, buf, :], ALU.mult)\
                       .then_inc(S["shift"], 1)
                if live(s, TURN - 1, NC) and l == 3:
                    c, buf, q = s - TURN + 1, (par - TURN + 1) % NB, (par - TURN + 1) % 2
                    wait(eng, S[f"load{buf}"], loaded(l, c, buf))
                    wait(eng, S["trig"], c - 1)
                    eng.tensor_tensor(turn[:, q, 1, :].unsqueeze(2), agg_in[:, buf, :, D:D + 1],
                                      attr_all[:, bass.ds(c * T, T)].unsqueeze(2), ALU.mult).then_inc(S["turn"], 1)
                    held(eng, 5 * c + 1, S["turn"])
                    apart(eng)
                    eng.wait_ge(S["turn"], at(S["turn"], 5 * c + 1))
                    eng.tensor_scalar(turn[:, q, 1, :], turn[:, q, 1, :], 0.1 / (2 * math.pi), None, ALU.mult)\
                       .then_inc(S["turn"], 1)
                    held(eng, 5 * c + 2, S["turn"])
                    apart(eng)
                    eng.wait_ge(S["turn"], at(S["turn"], 5 * c + 2))
                    eng.tensor_scalar(turn[:, q, 0, :], turn[:, q, 1, :], 0.25, None, ALU.add).then_inc(S["turn"], 1)
                    held(eng, 5 * c + 3, S["turn"])
                    apart(eng)
                    eng.wait_ge(S["turn"], at(S["turn"], 5 * c + 3))
                    eng.tensor_scalar(turn_k[:, q], turn[:, q], MAGIC, MAGIC, ALU.add, ALU.subtract)\
                       .then_inc(S["turn"], 1)
                    eng.wait_ge(S["turn"], at(S["turn"], 5 * c + 4))
                    eng.tensor_tensor(turn[:, q], turn[:, q], turn_k[:, q], ALU.subtract).then_inc(S["turn"], 1)
            if l == 0:
                eng.wait_ge(P["consts"], 3)
            if l == 3:
                eng.wait_ge(P["attr_in"], 32)
            node_steps(eng, step)

        def node_vector(eng, l):
            S = NODE[l]

            def first_half(c, buf, q):
                u = psum[:, 4 + 2 * q:6 + 2 * q, :].rearrange("p a (b c) -> p (a b) c", c=256)
                eng.wait_ge(S["u_mm"], at(S["u_mm"], c + 1))
                if l == 2:
                    wait(eng, S[f"load{buf}"], loaded(l, c, buf))
                    eng.tensor_tensor(mid[:, q], agg_in[:, buf], u[:, :, 0:AW], ALU.add).then_inc(S["mid"], 1)
                    return
                if l == 3:
                    eng.wait_ge(S["half"], at(S["half"], c + 1))
                for b in range(T):
                    if l == 0:
                        op = eng.scalar_tensor_tensor(out=mid[:, q, b, 0:D], in0=agg_in[:, buf, b, 0:D],
                                                      scalar=attr_all[:, bass.ds(c * T + b, 1)], in1=u[:, b, 0:D],
                                                      op0=ALU.mult, op1=ALU.add)
                    else:
                        op = eng.scalar_tensor_tensor(out=mid[:, q, b, 0:D], in0=u[:, b, 0:D],
                                                      scalar=turned[:, q, 0, b:b + 1], in1=x_in[:, buf, b, 0:D],
                                                      op0=ALU.mult, op1=ALU.add)
                op.then_inc(S["mid"], 1)

            def second_half(c, buf, q):
                wait(eng, S["applied"], c - 3)
                if l == 1:
                    wait(eng, S[f"load{buf}"], loaded(l, c, buf))
                    eng.scalar_tensor_tensor(out=res[:, buf], in0=x_in[:, buf, :, 0:D], scalar=2.0,
                                             in1=agg_in[:, buf, :, 0:D], op0=ALU.mult, op1=ALU.add)\
                       .then_inc(S["res"], 1)
                    return
                if l == 2:
                    eng.wait_ge(S["feat"], at(S["feat"], c + 1))
                    eng.scalar_tensor_tensor(out=res[:, buf], in0=x_in[:, buf, :, 0:D], scalar=2.0, in1=feat[:, q],
                                             op0=ALU.mult, op1=ALU.add).then_inc(S["res"], 1)
                    return
                eng.wait_ge(S["mid"], at(S["mid"], c + 1))
                for b in range(T):
                    if l == 0:
                        op = eng.scalar_tensor_tensor(out=res[:, buf, b, :], in0=mid[:, q, b, 0:D],
                                                      scalar=attr_all[:, bass.ds(c * T + b, 1)], in1=x_in[:, buf, b, 0:D],
                                                      op0=ALU.mult, op1=ALU.add)
                    else:
                        op = eng.scalar_tensor_tensor(out=res[:, buf, b, :], in0=agg_in[:, buf, b, 0:D],
                                                      scalar=turned[:, q, 1, b:b + 1], in1=mid[:, q, b, 0:D],
                                                      op0=ALU.mult, op1=ALU.add)
                op.then_inc(S["res"], 1)

            def step(s, par):
                if l == 3 and live(s, USE, NC):
                    c, buf, q = s - USE, (par - USE) % NB, (par - USE) % 2
                    eng.wait_ge(S["trig"], at(S["trig"], c + 1))
                    wait(eng, S[f"load{buf}"], loaded(l, c, buf))
                    eng.tensor_tensor(turned[:, q], trig[:, q], attr_all[:, bass.ds(c * T, T)].unsqueeze(1).to_broadcast([128, 2, T]),
                                      ALU.mult).then_inc(S["half"], 1)
                if l != 1 and live(s, USE, NC):
                    first_half(s - USE, (par - USE) % NB, (par - USE) % 2)
                lag = summed(l) + 1
                if live(s, lag, NC):
                    c, buf, q = s - lag, (par - lag) % NB, (par - lag) % 2
                    held(eng, c + 1, S["stats"])
                    apart(eng)
                    eng.wait_ge(S["stats"], at(S["stats"], c + 1))
                    for b in range(T):
                        op = eng.bn_aggr(mv[:, buf, b, :], stats[:, q, b, :])
                    op.then_inc(S["aggr"], 1)
                if l == 2 and live(s, summed(l), NC):
                    c, q = s - summed(l), (par - summed(l)) % 2
                    eng.wait_ge(S["act"], at(S["act"], c + 1))
                    for b in range(T):
                        op = eng.tensor_tensor(feat[:, q, b, 64:D].rearrange("p (v m) -> p v m", m=3),
                                               mid[:, q, b, 96:AW].rearrange("p (v m) -> p v m", m=3),
                                               gate[:, q, b, :].unsqueeze(2).to_broadcast([128, CV, 3]), ALU.mult)
                    op.then_inc(S["feat"], 1)
                if l != 2 and live(s, summed(l), NC):
                    second_half(s - summed(l), (par - summed(l)) % NB, (par - summed(l)) % 2)
                if live(s, lag, NC):
                    c, buf, q = s - lag, (par - lag) % NB, (par - lag) % 2
                    eng.wait_ge(S["aggr"], at(S["aggr"], c + 1))
                    wait(eng, S["rstd"], c - 1)
                    wait(eng, S["shift"], c - 1)
                    eng.tensor_scalar(var_eps[:, q, :].unsqueeze(2), mv[:, buf, :, 1:2], EPS, None, ALU.add)\
                       .then_inc(S["eps"], 1)
                    eng.tensor_scalar(neg_mean[:, q, :].unsqueeze(2), mv[:, buf, :, 0:1], -1.0, None, ALU.mult)\
                       .then_inc(S["neg_mean"], 1)
                if l == 2 and live(s, summed(l), NC):
                    second_half(s - summed(l), (par - summed(l)) % NB, (par - summed(l)) % 2)
                if live(s, summed(l), NC):
                    c, buf, q = s - summed(l), (par - summed(l)) % NB, (par - summed(l)) % 2
                    eng.wait_ge(S["res"], at(S["res"], c + 1))
                    for b in range(T):
                        op = eng.bn_stats(stats[:, q, b, :], res[:, buf, b, :])
                    op.then_inc(S["stats"], 1)
            if l in (0, 3):
                eng.wait_ge(P["attr_in"], 16 if l == 0 else 32)
            node_steps(eng, step)

        @block.sync
        def _(eng):
            setup_sync(eng)
            for l in range(layers):
                begin(l)
                if l == 1:
                    attn_sync(eng)
                else:
                    edge_sync(eng, l)
                node_sync(eng, l)
            stored(eng, layers - 1)

        @block.gpsimd
        def _(eng):
            setup_gpsimd(eng)
            for l in range(layers):
                begin(l)
                if l == 1:
                    attn_gpsimd(eng)
                else:
                    edge_gpsimd(eng, l)
                node_gpsimd(eng, l)

        @block.scalar
        def _(eng):
            setup_scalar(eng)
            for l in range(layers):
                begin(l)
                if l == 1:
                    attn_scalar(eng)
                else:
                    edge_scalar(eng, l)
                node_scalar(eng, l)

        @block.tensor
        def _(eng):
            setup_tensor(eng)
            for l in range(layers):
                begin(l)
                if l == 1:
                    attn_tensor(eng)
                else:
                    edge_tensor(eng, l)
                node_tensor(eng, l)

        @block.vector
        def _(eng):
            setup_vector(eng)
            for l in range(layers):
                begin(l)
                if l == 1:
                    attn_vector(eng)
                else:
                    edge_vector(eng, l)
                node_vector(eng, l)


LAYERS = 4


def packed_weights(w):
    import numpy as np
    names = {
        0: dict(fc1="L0_gnn_Wfc1", fc2="L0_gnn_Wfc2", l0="L0_gnn_Wl1_0", l1="L0_gnn_Wl1_1", s="L0_gnn_Wl2_s",
                v="L0_gnn_Wl2_v", x="L0_gnn_Wa", sc0="L0_gnn_Wsc0", sc1="L0_gnn_Wsc1"),
        2: dict(fc1="L2_gnn_fc_w1", fc2="L2_gnn_fc_w2", l0="L2_gnn_W1_s", l1="L2_gnn_W1_v", s="L2_gnn_W2_s",
                v="L2_gnn_W2_v", x=None, sc0="L2_gnn_Wsc_s", sc1="L2_gnn_Wsc_v"),
        3: dict(fc1="L3_gnn_fc_w1", fc2="L3_gnn_fc_w2", l0="L3_gnn_lin1_w0", l1="L3_gnn_lin1_w1", s="L3_gnn_lin2_w0",
                v="L3_gnn_lin2_w1", x="L3_gnn_lin3_w", sc0="L3_gnn_sc_w0", sc1="L3_gnn_sc_w1"),
    }
    out = np.zeros((128, len(BLOCKS), 128), np.float32)
    for layer, n in names.items():
        g = {k: (w[v] if v else None) for k, v in n.items()}

        def put(name):
            return out[:, BLOCKS.index((layer, name)), :]
        fc2, ws, wv = g["fc2"], g["s"], g["v"]
        so = ws.shape[1]
        b = put("E1")
        b[0:64, 0:64] = g["l0"]
        b[64:128, 64:128] = g["l0"]
        b = put("E2")
        for m in range(3):
            b[m:96:3, 32 * m:32 * m + 32] = g["l1"]
        b[96:128, 96:128] = g["l1"]
        put("F1")[0:g["fc1"].shape[0], 0:64] = g["fc1"]
        b = put("W1")
        b[0:64, 0:64] = fc2[:, 64:128]
        b[0:64, 64:128] = fc2[:, 0:64]
        b = put("W2")
        for m in range(3):
            b[0:64, 32 * m:32 * m + 32] = fc2[:, 128:160]
        b[0:64, 96:128] = fc2[:, 160:192]
        put("A1")[64:128, 0:so] = ws[0:64]
        put("A2")[96:128, 0:so] = ws[64:96]
        if g["x"] is not None:
            put("A1")[64:128, 64:65] = g["x"][0:64]
            put("A2")[96:128, 64:65] = g["x"][64:96]
        for m in range(3):
            put("B1")[0:64, 32 * m:32 * m + 32] = wv[0:64]
            put("B2")[32 * m:32 * m + 32, 32 * m:32 * m + 32] = wv[64:96]
        put("SS")[0:64, 0:so] = g["sc0"]
        for m in range(3):
            put("SV")[m:96:3, m:96:3] = g["sc1"]
        if layer == 0:
            put("CN")[0, 65] = 1.0
    return out.reshape(128, -1)


def packed_weights_1(w):
    import numpy as np
    out = np.zeros((128, NW1, 128), np.float32)
    g = {k[7:]: v for k, v in w.items() if k.startswith("L1_gnn_")}

    def put(name):
        return out[:, ATT_BLOCKS.index(name), :]

    def spread(name, a, rows, shift=0):
        for m in range(3):
            to = (m + shift) % 3
            n = a.shape[1]
            put(name)[32 * m:32 * m + 32, (n * to if rows == 3 else 0):(n * to if rows == 3 else 0) + n] = a
    for k in range(2):
        put("MS")[0:64, 64 * k:64 * k + 64] = g["Ws_src"]
        put("MS")[64:128, 64 * k:64 * k + 64] = g["Ws_dst"]
    rbf = g["W_rbf"]
    for m in range(3):
        put("M1")[m:96:3, 32 * m:32 * m + 32] = g["Wv_src"]
        put("M2")[m:96:3, 32 * m:32 * m + 32] = g["Wv_dst"]
        cols = slice(32 * m, 32 * m + 32)
        put("C")[0:16, cols] = rbf[:, 128:160]
        put("D")[16 * (1 + m):16 * (2 + m), cols] = rbf[:, 160:192]
        for name, shift in (("F", 1), ("G", 2)):
            c = 1 + (m + shift) % 3
            put(name)[16 * c:16 * c + 16, cols] = rbf[:, 192:224]
        put("V0")[64:128, 0:32] = g["Wv_val"][0:64]
        put("WG")[64:128, cols] = g["Wg"]
        put("UV")[64:128, cols] = g["Wv_vlin"][0:64]
    put("B1")[0:16, 0:64] = rbf[:, 0:64]
    put("B1")[16:32, 64:128] = rbf[:, 64:128]
    put("B2")[32:48, 0:64] = rbf[:, 64:128]
    put("B2")[48:64, 64:128] = rbf[:, 64:128]
    put("A1")[0:64, 0:64] = g["W_alpha"][0:64]
    put("A1")[0:64, 64:128] = g["Ws_val"][0:64]
    spread("A2", np.concatenate([g["W_alpha"][64:96], g["Ws_val"][64:96]], axis=1), 1)
    put("V1")[0:64, 32:64] = g["Wv_val"][0:64]
    put("V1")[64:128, 64:96] = g["Wv_val"][0:64]
    spread("VC", g["Wv_val"][64:96], 3)
    spread("VF", g["Wv_val"][96:128], 3, -1)
    spread("VG", g["Wv_val"][96:128], 3, 1)
    for h in range(4):
        put("US")[16 * h:16 * h + 16, 64 + h] = g["alpha_dot"][0, h]
        put("S64")[64 + h, 16 * h:16 * h + 16] = 1.0
        for m in range(3):
            put("S96")[64 + h, 32 * m + 8 * h:32 * m + 8 * h + 8] = 1.0
    put("US")[64:128, 0:64] = g["Ws_vlin"][0:64]
    spread("HD", g["Ws_vlin"][64:96], 1)
    spread("H0", g["Wv_vlin"][64:96], 3)
    spread("HF", g["Wv_vlin"][96:128], 3, -1)
    spread("HG", g["Wv_vlin"][96:128], 3, 1)
    put("PS")[0:64, 0:64] = g["Wps"]
    spread("PV", g["Wpv"], 3)
    return out.reshape(128, -1)


def kernel(**inputs):
    import numpy as np
    import concourse.bacc as _bacc
    from concourse import mybir as _mybir
    from concourse.bass_utils import run_bass_kernel_spmd as _run

    w = {k: np.asarray(v) for k, v in inputs.items()}
    tiles = EP // TILE

    def by_tile(a, fill):
        full = np.full((EP,) + a.shape[1:], fill, a.dtype)
        full[:len(a)] = a
        return np.ascontiguousarray(full.reshape((tiles, TILE) + a.shape[1:]).swapaxes(0, 1)).reshape(TILE, -1)

    def by_row(a):
        full = np.zeros((a.shape[1], EP), a.dtype)
        full[:, :len(a)] = a.T
        return full
    dst_next = np.full(E, N, np.int32)
    dst_next[:-1] = w["dst"][1:]
    dst_row = np.full((1, EP + 1), N, np.int32)
    dst_row[0, 0] = -1
    dst_row[0, 1:E + 1] = w["dst"]
    small = np.zeros((128, NSMALL), np.float32)
    small[0:64, SM["b1"]] = w["L2_gnn_fc_b1"]
    b2 = w["L2_gnn_fc_b2"]
    small[0:64, SM["b2"]] = b2[64:128]
    small[64:128, SM["b2"]] = b2[0:64]
    for m in range(3):
        small[32 * m:32 * m + 32, SM["b2"] + 1] = b2[128:160]
    small[96:128, SM["b2"] + 1] = b2[160:192]
    for k in range(2):
        small[64 * k:64 * k + 64, SM["gamma_s"]] = w["L1_gnn_gamma_s"]
        small[64 * k:64 * k + 64, SM["beta"]] = w["L1_gnn_beta_s"]
    small[0:64, SM["ss"]] = 2.0
    small[64:128, SM["ss"]] = w["L1_gnn_w2_ss"]
    small[64:128, SM["sv"]] = w["L1_gnn_w2_sv"]
    for m in range(3):
        small[m:96:3, SM["gamma_v"]] = w["L1_gnn_gamma_v"]
        small[32 * m:32 * m + 32, SM["vs"]] = w["L1_gnn_w2_vs"]
        small[32 * m:32 * m + 32, SM["vv0"]] = w["L1_gnn_w2_vv0"]
        small[32 * m:32 * m + 32, SM["vv1"]] = w["L1_gnn_w2_vv1"]
    sh = by_row(w["edge_attr_4"])
    sh_big = np.repeat(sh[[0, 0, 0, 1, 2, 3, 2, 3, 1, 3, 1, 2]], 32, axis=0)
    rbf = by_row(w["edge_attr_16"])
    rbf_sh = np.concatenate([rbf, rbf, rbf, rbf, np.repeat(sh, 16, axis=0)])
    arrays = {
        "x": np.concatenate([w["x"], w["node_vec1"]], axis=1),
        "node_attr": np.stack([w["node_vec1"][min(c * GE, N - GE):][:GE].reshape(TILE, T) for c in range(NC)], axis=1)
                       .reshape(TILE, -1),
        "src": by_tile(w["src"], 0), "dst": by_tile(w["dst"], N), "dst_next": by_tile(dst_next, N),
        "dst_row": dst_row,
        "sh_cols": by_tile(w["edge_attr_4"], 0),
        "attr16": by_row(w["edge_attr_16"]), "attr8": by_row(w["edge_attr_8"]),
        "weights": packed_weights(w), "small": small,
        "weights1": packed_weights_1(w), "sh_big": sh_big, "rbf_sh": rbf_sh,
    }
    nc = _bacc.Bacc("TRN2", target_bir_lowering=False, num_devices=1)
    t = {}
    for name in arrays:
        arrays[name] = np.ascontiguousarray(arrays[name])
        t[name] = nc.dram_tensor("in_" + name, arrays[name].shape, _mybir.dt.from_np(arrays[name].dtype),
                                 kind="ExternalInput").ap()
    out = nc.dram_tensor("out", (N, D), _mybir.dt.float32, kind="ExternalOutput").ap()
    gnn_kernel(nc, t, out, LAYERS)
    r = _run(nc, [{"in_" + name: a for name, a in arrays.items()}], core_ids=[0])
    return r.results[0]["out"]
```
